# Optimizing a Trainium2 kernel written in Bass

```python
import numpy as np
import jax
import jax.numpy as jnp

def _softmax(x, axis=-1):
    return jax.nn.softmax(x, axis=axis)

def _gelu(x):
    return jax.nn.gelu(x, approximate=True)

def _silu(x):
    return jax.nn.silu(x)

def _sigmoid(x):
    return jax.nn.sigmoid(x)

def _layernorm(x, axis=-1, eps=1e-05):
    m = jnp.mean(x, axis=axis, keepdims=True)
    v = jnp.var(x, axis=axis, keepdims=True)
    return (x - m) / jnp.sqrt(v + eps)

def _scatter_add(tgt, idx, src, axis=0):
    return tgt.at[idx].add(src)

def _segment_sum(src, seg, n):
    return jax.ops.segment_sum(src, seg, n)
kernel_name = 'mk_seq_postln_d1_jaxref_r4_85837c'

def setup_inputs(seed: int=0):
    np.random.seed(seed)
    _w = jnp.asarray

    def _L0_attn_setup():
        import jax, jax.numpy as jnp
        import numpy as np
        H = 256
        NH = 16
        L = 4
        B = 4
        N = 512
        EPS_LN = 1e-12

        def gelu(x):
            return jax.nn.gelu(x, approximate=False)

        def layernorm(x, g, b):
            m = jnp.mean(x, axis=-1, keepdims=True)
            v = jnp.mean((x - m) ** 2, axis=-1, keepdims=True)
            return (x - m) / jnp.sqrt(v + EPS_LN) * g + b

        def conv1d_grouped(x, w, b, groups):
            y = jax.lax.conv_general_dilated(x, w, window_strides=(1,), padding=[(2, 2)], dimension_numbers=('NCH', 'OIH', 'NCH'), feature_group_count=groups)
            return y + b[None, :, None]

        def rope(x):
            b, n, c = x.shape
            half = c // 2
            inv = 1.0 / 10000.0 ** (jnp.arange(0, c, 2, dtype=jnp.float32) / c)
            freqs = jnp.arange(n, dtype=jnp.float32)[:, None] * inv[None, :]
            freqs = jnp.repeat(freqs, 2, axis=-1)
            cos, sin = (jnp.cos(freqs), jnp.sin(freqs))
            xp = x.reshape(b, n, half, 2)
            xr = jnp.stack([-xp[..., 1], xp[..., 0]], axis=-1).reshape(b, n, c)
            return x * cos + xr * sin

        def linear_attention(x, Wq, bq, Wk, bk, Wv, bv, g, bb):
            b, n, c = x.shape
            hd = c // NH
            q = gelu(x @ Wq + bq) + 0.21
            k = gelu(x @ Wk + bk) + 0.21
            v = x @ Wv + bv
            q_r = rope(q)
            k_r = rope(k)
            to_h = lambda t: t.reshape(b, n, NH, hd).transpose(0, 2, 1, 3)
            q, k, v, q_r, k_r = map(to_h, (q, k, v, q_r, k_r))
            kmean = jnp.mean(k, axis=2, keepdims=True)
            z = 1.0 / (jnp.einsum('bhnd,bhmd->bhnm', q, kmean) + 1e-06)
            kv = jnp.einsum('bhnd,bhne->bhde', k_r, v) / n
            out = jnp.einsum('bhnd,bhde->bhne', q_r, kv) * z
            out = out.transpose(0, 2, 1, 3).reshape(b, n, c)
            return layernorm(out + x, g, bb)
        key = jax.random.key(seed)
        ks = jax.random.split(key, 10)
        s = 0.02
        r = lambda k, sh: jax.random.normal(k, sh, dtype=jnp.float32) * s
        d = {}
        d['x'] = jax.random.normal(ks[0], (B, N, H), dtype=jnp.float32)
        d['conv1_w'] = r(ks[1], (4 * H, 1, 5))
        d['conv1_b'] = jnp.zeros((4 * H,), jnp.float32)
        d['conv2_w'] = r(ks[2], (H, 4, 5))
        d['conv2_b'] = jnp.zeros((H,), jnp.float32)
        d['ln0_g'] = jnp.ones((H,), jnp.float32)
        d['ln0_b'] = jnp.zeros((H,), jnp.float32)
        d['Wq'] = r(ks[3], (L, H, H))
        d['bq'] = jnp.zeros((L, H), jnp.float32)
        d['Wk'] = r(ks[4], (L, H, H))
        d['bk'] = jnp.zeros((L, H), jnp.float32)
        d['Wv'] = r(ks[5], (L, H, H))
        d['bv'] = jnp.zeros((L, H), jnp.float32)
        d['lnA_g'] = jnp.ones((L, H), jnp.float32)
        d['lnA_b'] = jnp.zeros((L, H), jnp.float32)
        d['W1'] = r(ks[6], (H, 4 * H))
        d['b1'] = jnp.zeros((4 * H,), jnp.float32)
        d['W2'] = r(ks[7], (4 * H, H))
        d['b2'] = jnp.zeros((H,), jnp.float32)
        d['ln2_g'] = jnp.ones((H,), jnp.float32)
        d['ln2_b'] = jnp.zeros((H,), jnp.float32)
        return d
    _L0_attn_in = _L0_attn_setup()

    def _L0_ffn_setup():
        import jax, jax.numpy as jnp
        import numpy as np
        TOP_K = 32
        TEMPERATURE = 1.0
        PARAM_SCALE = 0.02

        def _compose_weight(logits, A, B):
            vals, idx = jax.lax.top_k(logits, TOP_K)
            w = jax.nn.softmax(vals / TEMPERATURE)
            A_sel = A[idx]
            B_sel = B[idx]
            return jnp.einsum('k,kir,kro->io', w, A_sel, B_sel)
        key = jax.random.key(seed)
        ks = jax.random.split(key, 7)
        B, S, D, F, P, R = (2, 256, 256, 1024, 64, 64)
        x = jax.random.normal(ks[0], (B, S, D), dtype=jnp.float32)
        fc1_A = jax.random.normal(ks[1], (P, D, R), dtype=jnp.float32) * PARAM_SCALE
        fc1_B = jax.random.normal(ks[2], (P, R, F), dtype=jnp.float32) * PARAM_SCALE
        fc2_A = jax.random.normal(ks[3], (P, F, R), dtype=jnp.float32) * PARAM_SCALE
        fc2_B = jax.random.normal(ks[4], (P, R, D), dtype=jnp.float32) * PARAM_SCALE
        fc1_logits = jax.random.normal(ks[5], (P,), dtype=jnp.float32)
        fc2_logits = jax.random.normal(ks[6], (P,), dtype=jnp.float32)
        return {'x': x, 'fc1_A': fc1_A, 'fc1_B': fc1_B, 'fc2_A': fc2_A, 'fc2_B': fc2_B, 'fc1_logits': fc1_logits, 'fc2_logits': fc2_logits}
    _L0_ffn_in = _L0_ffn_setup()
    _d = {'L0_attn_x': _L0_attn_in['x'], 'L0_attn_conv1_w': _L0_attn_in['conv1_w'], 'L0_attn_conv1_b': _L0_attn_in['conv1_b'], 'L0_attn_conv2_w': _L0_attn_in['conv2_w'], 'L0_attn_conv2_b': _L0_attn_in['conv2_b'], 'L0_attn_ln0_g': _L0_attn_in['ln0_g'], 'L0_attn_ln0_b': _L0_attn_in['ln0_b'], 'L0_attn_Wq': _L0_attn_in['Wq'], 'L0_attn_bq': _L0_attn_in['bq'], 'L0_attn_Wk': _L0_attn_in['Wk'], 'L0_attn_bk': _L0_attn_in['bk'], 'L0_attn_Wv': _L0_attn_in['Wv'], 'L0_attn_bv': _L0_attn_in['bv'], 'L0_attn_lnA_g': _L0_attn_in['lnA_g'], 'L0_attn_lnA_b': _L0_attn_in['lnA_b'], 'L0_attn_W1': _L0_attn_in['W1'], 'L0_attn_b1': _L0_attn_in['b1'], 'L0_attn_W2': _L0_attn_in['W2'], 'L0_attn_b2': _L0_attn_in['b2'], 'L0_attn_ln2_g': _L0_attn_in['ln2_g'], 'L0_attn_ln2_b': _L0_attn_in['ln2_b'], 'L0_ffn_fc1_A': _L0_ffn_in['fc1_A'], 'L0_ffn_fc1_B': _L0_ffn_in['fc1_B'], 'L0_ffn_fc2_A': _L0_ffn_in['fc2_A'], 'L0_ffn_fc2_B': _L0_ffn_in['fc2_B'], 'L0_ffn_fc1_logits': _L0_ffn_in['fc1_logits'], 'L0_ffn_fc2_logits': _L0_ffn_in['fc2_logits']}
    _x0 = _d['L0_attn_x']
    _d['L0_attn_x'] = jax.random.normal(jax.random.fold_in(jax.random.key(seed), 1), (8, 1024, 256), dtype=_x0.dtype)
    del _x0
    return _d

def reference(L0_attn_x, L0_attn_conv1_w, L0_attn_conv1_b, L0_attn_conv2_w, L0_attn_conv2_b, L0_attn_ln0_g, L0_attn_ln0_b, L0_attn_Wq, L0_attn_bq, L0_attn_Wk, L0_attn_bk, L0_attn_Wv, L0_attn_bv, L0_attn_lnA_g, L0_attn_lnA_b, L0_attn_W1, L0_attn_b1, L0_attn_W2, L0_attn_b2, L0_attn_ln2_g, L0_attn_ln2_b, L0_ffn_fc1_A, L0_ffn_fc1_B, L0_ffn_fc2_A, L0_ffn_fc2_B, L0_ffn_fc1_logits, L0_ffn_fc2_logits):

    def _L0_attn_ref(x, conv1_w, conv1_b, conv2_w, conv2_b, ln0_g, ln0_b, Wq, bq, Wk, bk, Wv, bv, lnA_g, lnA_b, W1, b1, W2, b2, ln2_g, ln2_b):
        import jax, jax.numpy as jnp
        import numpy as np
        H = 256
        NH = 16
        L = 4
        B = 4
        N = 512
        EPS_LN = 1e-12

        def gelu(x):
            return jax.nn.gelu(x, approximate=False)

        def layernorm(x, g, b):
            m = jnp.mean(x, axis=-1, keepdims=True)
            v = jnp.mean((x - m) ** 2, axis=-1, keepdims=True)
            return (x - m) / jnp.sqrt(v + EPS_LN) * g + b

        def conv1d_grouped(x, w, b, groups):
            y = jax.lax.conv_general_dilated(x, w, window_strides=(1,), padding=[(2, 2)], dimension_numbers=('NCH', 'OIH', 'NCH'), feature_group_count=groups)
            return y + b[None, :, None]

        def rope(x):
            b, n, c = x.shape
            half = c // 2
            inv = 1.0 / 10000.0 ** (jnp.arange(0, c, 2, dtype=jnp.float32) / c)
            freqs = jnp.arange(n, dtype=jnp.float32)[:, None] * inv[None, :]
            freqs = jnp.repeat(freqs, 2, axis=-1)
            cos, sin = (jnp.cos(freqs), jnp.sin(freqs))
            xp = x.reshape(b, n, half, 2)
            xr = jnp.stack([-xp[..., 1], xp[..., 0]], axis=-1).reshape(b, n, c)
            return x * cos + xr * sin

        def linear_attention(x, Wq, bq, Wk, bk, Wv, bv, g, bb):
            b, n, c = x.shape
            hd = c // NH
            q = gelu(x @ Wq + bq) + 0.21
            k = gelu(x @ Wk + bk) + 0.21
            v = x @ Wv + bv
            q_r = rope(q)
            k_r = rope(k)
            to_h = lambda t: t.reshape(b, n, NH, hd).transpose(0, 2, 1, 3)
            q, k, v, q_r, k_r = map(to_h, (q, k, v, q_r, k_r))
            kmean = jnp.mean(k, axis=2, keepdims=True)
            z = 1.0 / (jnp.einsum('bhnd,bhmd->bhnm', q, kmean) + 1e-06)
            kv = jnp.einsum('bhnd,bhne->bhde', k_r, v) / n
            out = jnp.einsum('bhnd,bhde->bhne', q_r, kv) * z
            out = out.transpose(0, 2, 1, 3).reshape(b, n, c)
            return layernorm(out + x, g, bb)
        b, n, c = x.shape
        h = x.transpose(0, 2, 1)
        h = conv1d_grouped(h, conv1_w, conv1_b, c)
        h = gelu(h)
        h = conv1d_grouped(h, conv2_w, conv2_b, c)
        h = h.transpose(0, 2, 1)
        h = layernorm(h + x, ln0_g, ln0_b)
        for i in range(Wq.shape[0]):
            h = linear_attention(h, Wq[i], bq[i], Wk[i], bk[i], Wv[i], bv[i], lnA_g[i], lnA_b[i])
        f = gelu(h @ W1 + b1) @ W2 + b2
        return layernorm(f + h, ln2_g, ln2_b)

    def _L0_ffn_ref(x, fc1_A, fc1_B, fc2_A, fc2_B, fc1_logits, fc2_logits):
        import jax, jax.numpy as jnp
        import numpy as np
        TOP_K = 32
        TEMPERATURE = 1.0
        PARAM_SCALE = 0.02

        def _compose_weight(logits, A, B):
            vals, idx = jax.lax.top_k(logits, TOP_K)
            w = jax.nn.softmax(vals / TEMPERATURE)
            A_sel = A[idx]
            B_sel = B[idx]
            return jnp.einsum('k,kir,kro->io', w, A_sel, B_sel)
        W1 = _compose_weight(fc1_logits, fc1_A, fc1_B)
        W2 = _compose_weight(fc2_logits, fc2_A, fc2_B)
        h = jax.nn.gelu(jnp.einsum('bsd,df->bsf', x, W1))
        return jnp.einsum('bsf,fd->bsd', h, W2)
    x = L0_attn_x
    x = _layernorm(x + _L0_attn_ref(x, L0_attn_conv1_w, L0_attn_conv1_b, L0_attn_conv2_w, L0_attn_conv2_b, L0_attn_ln0_g, L0_attn_ln0_b, L0_attn_Wq, L0_attn_bq, L0_attn_Wk, L0_attn_bk, L0_attn_Wv, L0_attn_bv, L0_attn_lnA_g, L0_attn_lnA_b, L0_attn_W1, L0_attn_b1, L0_attn_W2, L0_attn_b2, L0_attn_ln2_g, L0_attn_ln2_b), axis=-1)
    x = _layernorm(x + _L0_ffn_ref(x, L0_ffn_fc1_A, L0_ffn_fc1_B, L0_ffn_fc2_A, L0_ffn_fc2_B, L0_ffn_fc1_logits, L0_ffn_fc2_logits), axis=-1)
    return x

_drawn_inputs = setup_inputs


def setup_inputs(seed=0):
    import zlib

    import numpy as np

    out = dict(_drawn_inputs(seed))
    spreads = {'L0_attn_conv1_b': (0.0, 0.8),
     'L0_attn_conv2_b': (0.0, 0.1),
     'L0_attn_ln0_g': (1.0, 0.2),
     'L0_attn_ln0_b': (0.0, 0.1),
     'L0_attn_bq': (0.0, 0.8),
     'L0_attn_bk': (0.0, 0.8),
     'L0_attn_bv': (0.0, 0.1),
     'L0_attn_lnA_g': (1.0, 0.2),
     'L0_attn_lnA_b': (0.0, 0.1),
     'L0_attn_b1': (0.0, 0.454),
     'L0_attn_b2': (0.0, 0.1),
     'L0_attn_ln2_g': (1.0, 0.2),
     'L0_attn_ln2_b': (0.0, 0.1)}
    factors = {'L0_attn_conv1_w': 8.0,
     'L0_attn_conv2_w': 8.0,
     'L0_attn_Wq': 8.0,
     'L0_attn_Wk': 8.0,
     'L0_ffn_fc1_A': 8.0,
     'L0_ffn_fc1_B': 8.0,
     'L0_ffn_fc2_A': 8.0,
     'L0_ffn_fc2_B': 8.0,
     'L0_ffn_fc1_logits': 8.0,
     'L0_ffn_fc2_logits': 8.0}
    for name, (base, spread) in spreads.items():
        noise = np.random.default_rng([zlib.crc32(name.encode()), seed]).standard_normal(out[name].shape)
        drawn = base * np.exp(spread * noise) if base else spread * noise
        out[name] = jnp.asarray(drawn.astype(out[name].dtype))
    for name, factor in factors.items():
        out[name] = (out[name] * factor).astype(out[name].dtype)
    return out
```

```python
import concourse.bass as bass
from concourse import mybir
from contextlib import ExitStack

F32 = mybir.dt.float32
F32R = mybir.dt.float32r
U32 = mybir.dt.uint32
I32 = mybir.dt.int32
ALU = mybir.AluOpType
ACT = mybir.ActivationFunctionType

P = 128
ENGINES = ("tensor", "vector", "scalar", "gpsimd", "sync")


class Stage:

    def __init__(self, nc, ctx, label):
        self.nc, self.ctx, self.label = nc, ctx, label
        self.queue = {e: [] for e in ENGINES}
        self.sem, self.count, self.event = {}, {}, {}
        self.dma_sem, self.dma_count, self.dma_engine = {}, {}, {}
        self.relay = {}

    def do(self, engine, make, done=None, after=(), dma=None, apart=False):
        if done is not None:
            if engine not in self.sem:
                self.sem[engine] = self.ctx.enter_context(self.nc.semaphore(f"{self.label}_{engine}"))
                self.count[engine] = 0
            self.count[engine] += 1
            assert done not in self.event, done
            self.event[done] = (engine, self.count[engine])
        if dma is not None:
            if dma not in self.dma_sem:
                tag = "_".join(str(x) for x in dma) if isinstance(dma, tuple) else dma
                self.dma_sem[dma] = self.ctx.enter_context(self.nc.semaphore(f"{self.label}_dma_{tag}"))
                self.dma_count[dma] = 0
                self.dma_engine[dma] = engine
            self.dma_count[dma] += 1
        apart = apart or engine in ("gpsimd", "sync")
        if apart and engine not in self.relay:
            self.relay[engine] = self.ctx.enter_context(self.nc.semaphore(f"{self.label}_relay_{engine}"))
        self.queue[engine].append((make, done, after, dma, apart))

    def value(self, name, iteration, back=0):
        if name in self.dma_sem:
            n = 16 * self.dma_count[name]
            return self.dma_sem[name], n, n * (2 - back)
        engine, k = self.event[name]
        n = self.count[engine]
        return self.sem[engine], n, n * (1 - back) + k

    def credit(self, engine, eng):
        if engine in self.sem:
            eng.sem_inc(self.sem[engine], self.count[engine])
        for name, count in self.dma_count.items():
            if self.dma_engine[name] == engine:
                eng.sem_inc(self.dma_sem[name], 16 * count)

    def emit(self, engine, eng, iteration, where_is=None, ops=None):
        seen = {}
        for make, done, after, dma, apart in (self.queue[engine] if ops is None else ops):
            waited = False
            for item in after:
                if isinstance(item, At):
                    stage, name, where, back = item.stage, item.name, item.iteration, 0
                    if isinstance(where, str):
                        where = where_is[where]
                elif isinstance(item, BankFree):
                    stage, name, where, back = self, item.banks.last[item.bank], iteration, 1
                elif isinstance(item, Prev):
                    stage, name, where, back = self, item.name, iteration, 1
                else:
                    stage, name, where, back = self, item, iteration, 0
                sem, per, const = stage.value(name, where, back)
                spot = (stage.label, id(sem), id(where))
                if seen.get(spot, -1) >= const:
                    continue
                seen[spot] = const
                eng.wait_ge(sem, where * per + const)
                waited = True
                if engine == "sync" and not isinstance(iteration, int):
                    eng.sem_inc(self.relay[engine], 1)
                    waited = False
            if waited and apart and not isinstance(iteration, int):
                eng.sem_inc(self.relay[engine], 1)
            inst = make(eng)
            if done is not None:
                inst.then_inc(self.sem[engine], 1)
            if dma is not None:
                inst.then_inc(self.dma_sem[dma], 16)


class Prev:
    def __init__(self, name):
        self.name = name


class At:
    def __init__(self, stage, name, iteration):
        self.stage, self.name, self.iteration = stage, name, iteration


class Banks:

    def __init__(self, tensors):
        self.tensors, self.turn, self.last = tensors, 0, {}

    def take(self, reader):
        b = self.turn % len(self.tensors)
        self.turn += 1
        free = self.last.get(b, None)
        self.last[b] = reader
        return self.tensors[b], (free if free is not None else BankFree(self, b))


class BankFree:

    def __init__(self, banks, bank):
        self.banks, self.bank = banks, bank


def mm(out, lhsT, rhs, start=True, stop=True):
    return lambda e: e.matmul(out, lhsT, rhs, start=start, stop=stop)


def mm3(parts):
    def make(e):
        for out, (wh, wl), (xh, xl), start, stop in parts:
            e.matmul(out, wh, xh, start=start, stop=False)
            e.matmul(out, wh, xl, start=False, stop=False)
            last = e.matmul(out, wl, xh, start=False, stop=stop)
        return last
    return make


def conv_phase(nc, x, bands1, bands2, conv1_b, conv2_b, ln0, eye, h0):
    B, N, H = x.shape
    S, W, TAPS_AHEAD = 4, 8, 2
    G = N // S
    MT = G // P
    CP = H // 32
    TILES = MT * S
    LANES = 2
    HB = 4

    xg = x.rearrange("b (g s) c -> b g s c", s=S)

    ctx = ExitStack()
    with ctx:
        sb = lambda n, s, d=F32: ctx.enter_context(nc.sbuf_tensor(n, s, d))
        pb = lambda n, s: ctx.enter_context(nc.psum_tensor(n, s, F32))

        band1 = sb("band1", [P, CP * HB * P])
        band1_hi = sb("band1_hi", [P, CP * HB, P], F32R)
        band1_lo = sb("band1_lo", [P, CP * HB, P], F32R)
        band2 = sb("band2", [P, CP * HB, 3, 32])
        bias1 = sb("bias1", [P, CP * HB])
        bias2 = sb("bias2", [P, CP])
        gain = sb("gain0", [P, H])
        shift = sb("shift0", [P, H])
        identity = sb("identityA", [P, P])
        minus_half = sb("minus_halfA", [P, TILES])
        xw = [sb(f"xw{l}", [P, MT, W, H]) for l in range(LANES)]
        xr = sb("xr", [P, 2, 2, MT, P])
        xt_hi = sb("xt_hi", [P, 2, 2, G], F32R)
        xt_lo = sb("xt_lo", [P, 2, 2, G], F32R)
        hidden = sb("hidden", [P, 2, HB, G + 2])
        convT = sb("convT", [P, 2, G])
        y = [sb(f"yA{l}", [P, TILES, H]) for l in range(LANES)]
        h = [sb(f"hA{l}", [P, TILES, H]) for l in range(LANES)]
        stats = sb("statsA", [P, LANES, TILES, 6])
        moments = sb("momentsA", [P, LANES, TILES, 2])
        var_eps = sb("var_epsA", [P, LANES, TILES])
        rstd = sb("rstdA", [P, LANES, TILES])

        xt_ps = [pb(f"xt_ps{i}", [P, 2, G]) for i in range(2)]
        hid_ps = [pb(f"hid_ps{i}", [P, 2, G]) for i in range(3)]
        conv_ps = pb("conv_ps", [P, 512])
        back_ps = [pb(f"back_ps{i}", [P, MT, P]) for i in range(2)]

        setup = Stage(nc, ctx, "convset")
        work = Stage(nc, ctx, "conv")

        setup.do("sync", lambda e: e.dma_start(band1[:, :], bands1), dma="band1")
        setup.do("sync", lambda e: e.dma_start(identity[:, :], eye), dma="small")
        setup.do("sync", lambda e: e.dma_start(bias1[:, :], conv1_b), dma="small")
        setup.do("scalar", lambda e: e.dma_start(band2[:, :, :, :].rearrange("p b d n -> p (b d n)"), bands2), dma="small")
        setup.do("scalar", lambda e: e.dma_start(bias2[:, :], conv2_b), dma="small")
        setup.do("scalar", lambda e: e.dma_start(gain[:, :], ln0[0:1, :].partition_broadcast(P)), dma="small")
        setup.do("scalar", lambda e: e.dma_start(shift[:, :], ln0[1:2, :].partition_broadcast(P)), dma="small")
        b1f = lambda t: t[:, :, :].rearrange("p b n -> p (b n)")
        setup.do("vector", lambda e: e.tensor_copy(b1f(band1_hi), band1[:, :]), done="hi", after=["band1"])
        setup.do("vector", lambda e: e.tensor_tensor(b1f(band1_lo), band1[:, :], b1f(band1_hi).bitcast(F32),
                                                     ALU.subtract), done="lo", after=["hi"])
        setup.do("gpsimd", lambda e: e.memset(minus_half[:, :], -0.5), done="half")
        for l in range(LANES):
            setup.do("gpsimd", lambda e, l=l: e.memset(xw[l][:, 0, 0:2, :], 0.0), done=("pad0", l))
            setup.do("gpsimd", lambda e, l=l: e.memset(xw[l][:, MT - 1, W - 2:W, :], 0.0), done=("pad1", l))
        setup.do("gpsimd", lambda e: e.memset(hidden[:, :, :, 0:1], 0.0), done="pad2")
        setup.do("gpsimd", lambda e: e.memset(hidden[:, :, :, G + 1:G + 2], 0.0), done="pad3")

        def load(l, reg):
            tile = xw[l]
            b = lambda e: reg[e] * LANES + l
            q = "sync"

            def copy(p0, p1, mt, w0, w1, s0, g0):
                def make(e):
                    src = xg[bass.ds(b(e), 1), g0:g0 + p1 - p0, s0:s0 + w1 - w0, :]
                    return e.dma_start(tile[p0:p1, mt, w0:w1, :], src.rearrange("a g s c -> (a g) s c"))
                free = [Prev(("x_read", l)), Prev(("x_sent", l))]
                work.do(q, make, dma=("x", l), after=free + [At(setup, ("pad0", l), 0), At(setup, ("pad1", l), 0)])

            cut = 112
            for mt in range(MT):
                g = mt * P
                copy(0, P, mt, 2, 6, 0, g)
                if mt == 0:
                    copy(1, 1 + cut, mt, 0, 2, 2, 0)
                    copy(1 + cut, P, mt, 0, 2, 2, cut)
                else:
                    copy(0, P, mt, 0, 2, 2, g - 1)
                if mt == MT - 1:
                    copy(0, cut, mt, 6, 8, 0, g + 1)
                    copy(cut, P - 1, mt, 6, 8, 0, g + 1 + cut)
                else:
                    copy(0, P, mt, 6, 8, 0, g + 1)

        steps = [(l, cp) for l in range(LANES) for cp in range(CP)]
        n_steps = len(steps)

        def earlier(kind, n, ring):
            return [(kind, n - ring)] if n >= ring else [Prev((kind, n - ring + n_steps))]

        def to_channels(n):
            l, cp = steps[n]
            bank = xt_ps[n % 2]
            for mt in range(MT):
                work.do("gpsimd", lambda e, mt=mt: e.tensor_copy(
                    xr[:, n % 2, :, mt, :].rearrange("p a (w c) -> p w a c", w=W),
                    xw[l][:, mt, :, 32 * cp:32 * cp + 32].rearrange("p w (a c) -> p w a c", a=2)),
                    done=("xr", n) if mt == MT - 1 else None,
                    after=[("x", l)] + earlier("xt", n, 2))
            for cg in range(2):
                for mt in range(MT):
                    last = cg == 1 and mt == MT - 1
                    work.do("tensor", lambda e, cg=cg, mt=mt: e.transpose(
                        bank[:, cg, mt * P:(mt + 1) * P], xr[:, n % 2, cg, mt, :], identity[:, :]),
                        done=("xt", n) if last else None,
                        after=[("xr", n), At(setup, "small", 0)] + earlier("xt_lo", n, 2))
            r = n % 2
            flat = lambda t: t[:, :, :].rearrange("p a g -> p (a g)")
            hi = xt_hi[:, r, :, :].rearrange("p a g -> p (a g)")
            lo = xt_lo[:, r, :, :].rearrange("p a g -> p (a g)")
            work.do("scalar", lambda e: e.activation(hi, flat(bank), ACT.Copy), done=("xt_hi", n),
                    after=[("xt", n)] + earlier("conv1", n, 2))
            work.do("vector", lambda e: e.tensor_tensor(lo, flat(bank), hi.bitcast(F32), ALU.subtract),
                    done=("xt_lo", n), after=[("xt_hi", n)])

        def conv1(n):
            l, cp = steps[n]
            r = n % 2
            for cg in range(2):
                k = 2 * n + cg
                bank = hid_ps[k % 3]
                parts = [(bank[:, j, :], (band1_hi[:, 4 * cp + 2 * cg + j, :], band1_lo[:, 4 * cp + 2 * cg + j, :]),
                          (xt_hi[:, r, cg, :], xt_lo[:, r, cg, :]), True, True) for j in range(2)]
                free = [("hidden", k - 3)] if k >= 3 else [Prev(("hidden", k - 3 + 2 * n_steps))]
                work.do("tensor", mm3(parts), done=("hid", k),
                        after=[("xt_lo", n), At(setup, "lo", 0)] + free)
                if cg == 1:
                    work.event[("conv1", n)] = work.event[("hid", k)]
                for j in range(2):
                    blk = 2 * cg + j
                    work.do("scalar", lambda e, j=j, blk=blk, bank=bank: e.activation(
                        hidden[:, r, blk, 1:1 + G], bank[:, j, :], ACT.Gelu,
                        bias=bias1[:, 4 * cp + blk:4 * cp + blk + 1]),
                        done=("hidden", k) if j else None,
                        after=[("hid", k)] + earlier("conv", n, 2))

        def conv2(n):
            l, cp = steps[n]
            r = n % 2
            for d in range(3):
                for blk in range(HB):
                    work.do("tensor", mm(conv_ps[32 * blk:32 * blk + 32, 0:G], band2[:, 4 * cp + blk, d, :],
                                         hidden[:, r, blk, d:d + G], d == 0, d == 2),
                            done=("conv", n) if d == 2 and blk == HB - 1 else None,
                            after=[("hidden", 2 * n + 1), At(setup, "pad2", 0), At(setup, "pad3", 0)] + earlier("convT", n, 1))
            work.do("vector", lambda e: e.tensor_scalar(convT[:, r, :], conv_ps[:, 0:G], bias2[:, cp:cp + 1], None,
                                                        ALU.add),
                    done=("convT", n), after=[("conv", n), At(setup, "small", 0)] + earlier("back", n, 2))

        def to_tokens(n):
            l, cp = steps[n]
            r = n % 2
            bank = back_ps[r]
            for mt in range(MT):
                work.do("tensor", lambda e, mt=mt: e.transpose(bank[:, mt, :], convT[:, r, mt * P:(mt + 1) * P],
                                                               identity[:, :]),
                        done=("back", n) if mt == MT - 1 else None,
                        after=[("convT", n)] + earlier("y", n, 2))
            for mt in range(MT):
                ins = bank[:, mt, :].rearrange("p (j s c) -> p j s c", j=4, s=S)
                res = xw[l][:, mt, 2:2 + S, 32 * cp:32 * cp + 32].rearrange("p s (j c) -> p j s c", j=4)
                out = y[l][:, mt * S:(mt + 1) * S, 32 * cp:32 * cp + 32].rearrange("p s (j c) -> p j s c", j=4)
                work.do("vector", lambda e, i=ins, q=res, o=out: e.tensor_tensor(o, i, q, ALU.add),
                        done=("y", n) if mt == MT - 1 else None,
                        after=[("back", n), Prev(("ln", l))])
            if cp == CP - 1:
                work.event[("x_read", l)] = work.event[("y", n)]
                work.event[("x_sent", l)] = work.event[("xr", n)]

        def finish(l):
            layernorm(work, l, [y[l][:, t, :] for t in range(TILES)], [h[l][:, t, :] for t in range(TILES)],
                      stats[:, l], moments[:, l], var_eps[:, l], rstd[:, l], minus_half, 1e-12,
                      gain[:, :], shift[:, :], ready=[("y", (l + 1) * CP - 1)], free=[Prev(("h0", l))],
                      done=("ln", l), first=[At(setup, "small", 0), At(setup, "half", 0)])

            def store(e):
                b = reg[e] * LANES + l
                return e.dma_start(h0[bass.ds(b, 1), :, :].rearrange("a p f -> (a p) f"),
                                   h[l][:, :, :].rearrange("p t c -> p (t c)"))
            work.do("sync", store, dma=("h0", l), after=[("ln", l)])

        reg = {}
        for n in range(n_steps + 3):
            if n < n_steps:
                if n % CP == 0 and n > 0:
                    pass
                to_channels(n)
            if 0 <= n - 1 < n_steps:
                conv1(n - 1)
            if 0 <= n - 2 < n_steps:
                conv2(n - 2)
            if 0 <= n - 3 < n_steps:
                to_tokens(n - 3)
                if (n - 3) % CP == CP - 1:
                    finish((n - 3) // CP)
        stores = [op for op in work.queue["sync"]]
        work.queue["sync"] = []
        for l in range(LANES):
            load(l, reg)
        work.queue["sync"] += stores

        run_loop(nc, setup, work, B // LANES, reg, waits=[("h0", l) for l in range(LANES)])


def attention_phase(nc, h_in, h_out, T, H, wqkv, rows, bq, rope, tables):
    B = h_in.shape[0]
    L = wqkv.shape[0] - 1
    TILES = T // P
    DUOS = TILES // 2
    CB = H // P
    NH = 16
    HD = H // NH
    HB = P // HD
    LANES = 2
    TQ = 512
    QH = T // TQ
    BK, BV, GAIN, SHIFT = range(4)

    ctx = ExitStack()
    with ctx:
        sb = lambda n, s, d=F32: ctx.enter_context(nc.sbuf_tensor(n, s, d))
        pb = lambda n, s: ctx.enter_context(nc.psum_tensor(n, s, F32))

        w_raw = sb("w_raw", [P, CB, 3 * H])
        w_hi = sb("w_hi", [P, CB, 2 * H], F32R)
        w_lo = sb("w_lo", [P, CB, 2 * H], F32R)
        vec = sb("vec", [P, L * 4 * H])
        bqs = sb("bqs", [P, L * CB])
        cos_k = sb("cos_k", [P, TILES, H])
        sin_k = sb("sin_k", [P, TILES, H])
        cos_q = sb("cos_q", [P, CB, T])
        sin_q = sb("sin_q", [P, CB, T])
        identity = sb("identityB", [P, P])
        rot = sb("rot", [P, P])
        kv_mask = sb("kv_mask", [P, P])
        head_mask = sb("head_mask", [P, HB])
        ones = sb("onesB", [P, P])
        minus_half = sb("minus_halfB", [P, TILES])

        h = [sb(f"hB{s}", [P, TILES, H + 1]) for s in range(LANES)]
        y = sb("yB", [P, TILES, H])
        hT_hi = sb("hT_hi", [P, CB, T], F32R)
        hT_lo = sb("hT_lo", [P, CB, T], F32R)
        kb = sb("kb", [P, 2, 2 * H])
        gk = sb("gk", [P, 2, 2 * H])
        kc = sb("kc", [P, 2, 2 * H])
        ks = sb("ks", [P, 2, 2 * H])
        kr = sb("kr", [P, 2, 2 * H])
        gsum = sb("gsum", [P, 2 * H])
        gT = sb("gT", [P, CB, T])
        qc = sb("qc", [P, CB, T])
        qs = sb("qs", [P, CB, T])
        G = sb("G", [P, CB, H + 1])
        GT = sb("GT", [P, CB, H])
        kv_raw = sb("kv_raw", [P, CB, P])
        kv = sb("kv", [P, LANES, CB, P])
        kv_rot = sb("kv_rot", [P, LANES, CB, P])
        km = sb("km", [P, CB])
        kmb = sb("kmb", [P, LANES, CB, HB])
        c21 = sb("c21", [P, CB, HB])
        cst = sb("cst", [P, LANES, NH])
        den = sb("den", [P, TILES, NH])
        z = sb("z", [P, TILES, NH])
        stats = sb("statsB", [P, TILES, 6])
        moments = sb("momentsB", [P, TILES, 2])
        var_eps = sb("var_epsB", [P, TILES])
        rstd = sb("rstdB", [P, TILES])

        banks = Banks([pb(f"bank{i}", [P, 512]) for i in range(5)])
        g_ps = [pb(f"g_ps{i}", [P, 512]) for i in range(CB)]
        m_ps = pb("m_ps", [P, 512])

        setup = Stage(nc, ctx, "attset")
        pair = Stage(nc, ctx, "attpair")
        lay = Stage(nc, ctx, "att")
        reg = {}

        two = lambda a: a.unsqueeze(1).broadcast_to([P, 2, a.shape[-1]])

        for name, dst, src in (("cos_k", cos_k, rope["cos_k"]), ("sin_k", sin_k, rope["sin_k"]),
                               ("cos_q", cos_q, rope["cos_q"]), ("sin_q", sin_q, rope["sin_q"])):
            setup.do("scalar", lambda e, d=dst, s=src: e.dma_start(d[:, :, :].rearrange("p a b -> p (a b)"), s), dma="consts")
        for dst, src in ((identity, tables["eye"]), (rot, tables["rot"]), (kv_mask, tables["kv_mask"]),
                         (head_mask, tables["head_mask"]), (bqs, bq)):
            setup.do("scalar", lambda e, d=dst, s=src: e.dma_start(d[:, :], s), dma="consts")
        setup.do("scalar", lambda e: e.dma_start(vec[:, :], rows.partition_broadcast(P)), dma="consts")
        setup.do("sync", lambda e: e.dma_start(w_raw[:, :, :].rearrange("p c n -> p (c n)"), wqkv[0]), dma="w0")
        setup.do("gpsimd", lambda e: e.memset(minus_half[:, :], -0.5), done="half")
        setup.do("gpsimd", lambda e: e.memset(ones[:, :], 1.0), done="ones")
        for s in range(LANES):
            setup.do("gpsimd", lambda e, s=s: e.memset(h[s][:, :, H:H + 1], 1.0), done=("ones", s))
        setup.do("scalar", lambda e: e.activation(w_hi[:, :, :], w_raw[:, :, 0:2 * H], ACT.Copy), done="w_hi", after=["w0"])
        setup.do("vector", lambda e: e.tensor_tensor(w_lo[:, :, :], w_raw[:, :, 0:2 * H], w_hi[:, :, :].bitcast(F32),
                                                     ALU.subtract), done="w_lo", after=["w_hi"])
        consts = [At(setup, "consts", 0)]
        w_now = [Prev("w_next"), At(setup, "w_lo", 0)]
        the_ones = [At(setup, "ones", 0)]

        def row(which):
            return lambda e: vec[:, bass.ds(reg[e][1] * (4 * H) + which * H, H)]

        batch = lambda e, h, s: h[bass.ds(reg[e][0] * LANES + s, 1)].rearrange("a p (t c) -> (a p) t c", c=H)
        for s in range(LANES):
            def load(e, s=s):
                return e.dma_start(h[s][:, :, 0:H], batch(e, h_in, s))
            pair.do("sync", load, dma=("h", s), after=[Prev(("sent", s))])

        def h_cols(s, u):
            bank, free = banks.take(("hT_lo", s, u))
            view = bank[:, :].rearrange("p (c t) -> p c t", c=CB)
            for cb in range(CB):
                for t in range(2):
                    lay.do("tensor", lambda e, cb=cb, t=t: e.transpose(
                        view[:, cb, t * P:(t + 1) * P], h[s][:, 2 * u + t, cb * P:(cb + 1) * P], identity[:, :]),
                        done=("hT", s, u) if cb == CB - 1 and t == 1 else None,
                        after=[free, At(pair, ("h", s), "pair"), Prev(("ln", s, u // 2))] + consts)
            cols = slice(u * 2 * P, (u + 1) * 2 * P)
            last_q = [("q", 0, CB * QH - 1)] if s == 1 else [Prev(("q", 1, CB * QH - 1))]
            lay.do("scalar", lambda e: e.activation(hT_hi[:, :, cols], view, ACT.Copy),
                   done=("hT_hi", s, u), after=[("hT", s, u)] + last_q)
            lay.do("vector", lambda e: e.tensor_tensor(hT_lo[:, :, cols], view, hT_hi[:, :, cols].bitcast(F32),
                                                       ALU.subtract),
                   done=("hT_lo", s, u), after=[("hT_hi", s, u)])

        def keys(s, u):
            bank, free = banks.take(("kb", s, u))
            parts = []
            for t in range(2):
                tok = slice((2 * u + t) * P, (2 * u + t + 1) * P)
                for cb in range(CB):
                    parts.append((bank[:, t * H:(t + 1) * H], (hT_hi[:, cb, tok], hT_lo[:, cb, tok]),
                                  (w_hi[:, cb, H:2 * H], w_lo[:, cb, H:2 * H]), cb == 0, cb == CB - 1))
            lay.do("tensor", mm3(parts), done=("k", s, u), after=[("hT_lo", s, u), free, *w_now])
            r = u % 2
            ring = lambda kind: [(kind, s, u - 2)] if u >= 2 else ([(kind, 0, DUOS - 2 + u)] if s else [Prev((kind, 1, DUOS - 2 + u))])
            d3 = lambda a: a.rearrange("p (t n) -> p t n", t=2)
            lay.do("vector", lambda e: e.tensor_tensor(d3(kb[:, r, :]), d3(bank[:, :]), two(row(BK)(e)), ALU.add),
                   done=("kb", s, u), after=[("k", s, u)] + ring("gk") + consts)
            lay.do("scalar", lambda e: e.activation(gk[:, r, :], kb[:, r, :], ACT.Gelu), done=("gk", s, u),
                   after=[("kb", s, u)] + ring("ks") + ring("gsum"))
            lay.do("vector", lambda e: e.scalar_tensor_tensor(
                kc[:, r, :], gk[:, r, :], 0.21, cos_k[:, 2 * u:2 * u + 2, :].rearrange("p t n -> p (t n)"),
                ALU.add, ALU.mult), done=("kc", s, u), after=[("gk", s, u)] + ring("kr"))
            pairs = lambda a: a.rearrange("p (i two) -> p i two", two=2)
            sin_d = sin_k[:, 2 * u:2 * u + 2, :].rearrange("p t n -> p (t n)")
            for k in range(2):
                lay.do("vector", lambda e, k=k: e.scalar_tensor_tensor(
                    pairs(ks[:, r, :])[:, :, k], pairs(gk[:, r, :])[:, :, 1 - k], 0.21, pairs(sin_d)[:, :, k],
                    ALU.add, ALU.mult), done=("ks", s, u) if k else None, after=[])
            lay.do("gpsimd", lambda e: e.tensor_tensor(kr[:, r, :], kc[:, r, :], ks[:, r, :], ALU.add),
                   done=("kr", s, u), after=[("ks", s, u)] + ring("G"))
            if u == 0:
                lay.do("gpsimd", lambda e: e.tensor_copy(gsum[:, :], gk[:, r, :]), done=("gsum", s, u),
                       after=[("S", 0) if s else Prev(("S", 1))])
            else:
                lay.do("gpsimd", lambda e: e.tensor_tensor(gsum[:, :], gsum[:, :], gk[:, r, :], ALU.add),
                       done=("gsum", s, u), after=[("gsum", s, u - 1)])

        def gram(s, u):
            r = u % 2
            evac = [("G_out", 0)] if s else [Prev(("G_out", 1))]
            for t in range(2):
                for db in range(CB):
                    lay.do("tensor", mm(g_ps[db][:, 0:H + 1], kr[:, r, t * H + db * P:t * H + (db + 1) * P],
                                        h[s][:, 2 * u + t, :], u == 0 and t == 0, u == DUOS - 1 and t == 1),
                           done=("G", s, u) if t == 1 and db == CB - 1 else None,
                           after=[("kr", s, u), At(setup, ("ones", s), 0)] + evac)

        def chain_1(s):
            prev_chain = [("kv_rot", 0)] if s else [Prev(("kv_rot", 1))]
            for db in range(CB):
                lay.do("scalar", lambda e, db=db: e.activation(G[:, db, :], g_ps[db][:, 0:H + 1], ACT.Copy),
                       done=("G_out", s) if db == CB - 1 else None,
                       after=[("G", s, DUOS - 1)] + ([("kv_raw", 0)] if s else [Prev(("kv_raw", 1))]))
            for db in range(CB):
                for cb in range(CB):
                    lay.do("tensor", lambda e, db=db, cb=cb: e.transpose(
                        m_ps[:, cb * H + db * P:cb * H + (db + 1) * P], G[:, db, cb * P:(cb + 1) * P], identity[:, :]),
                        done=("GT_ps", s) if db == CB - 1 and cb == CB - 1 else None,
                        after=[("G_out", s)] + prev_chain)
            lay.do("scalar", lambda e: e.activation(GT[:, :, :].rearrange("p c n -> p (c n)"), m_ps[:, :], ACT.Copy),
                   done=("GT", s), after=[("GT_ps", s)] + ([("kv_ps", 0)] if s else [Prev(("kv_ps", 1))]))
            bank, free = banks.take(("km", s))
            for db in range(CB):
                for t in range(2):
                    lay.do("tensor", mm(bank[:, db:db + 1], gsum[:, t * H + db * P:t * H + (db + 1) * P], ones[:, 0:1],
                                        t == 0, t == 1), done=("S", s) if db == CB - 1 and t == 1 else None,
                           after=[("gsum", s, DUOS - 1), free] + the_ones)
            den_read = [Prev(("D", s))]
            lay.do("vector", lambda e: e.tensor_scalar(km[:, :], bank[:, 0:CB], 1.0 / T, 0.21, ALU.mult, ALU.add),
                   done=("km", s), after=[("S", s)])
            for db in range(CB):
                lay.do("vector", lambda e, db=db: e.tensor_scalar(kmb[:, s, db, :], head_mask[:, :], km[:, db:db + 1], None,
                                                                  ALU.mult), done=("kmb", s) if db == CB - 1 else None,
                       after=[("km", s)] + den_read)
            lay.do("vector", lambda e: e.tensor_scalar(c21[:, :, :], kmb[:, s, :, :], 0.21, 1e-6 / P, ALU.mult, ALU.add),
                   done=("c21", s), after=[("kmb", s)] + ([("cst_ps", 0)] if s else [Prev(("cst_ps", 1))]))

        def chain_2(s):
            for db in range(CB):
                for cb in range(CB):
                    lay.do("tensor", mm(m_ps[:, db * P:(db + 1) * P], GT[:, cb, db * P:(db + 1) * P],
                                        w_raw[:, cb, 2 * H + db * P:2 * H + (db + 1) * P], cb == 0, cb == CB - 1),
                           done=("kv_ps", s) if db == CB - 1 and cb == CB - 1 else None, after=[("GT", s), *w_now])
            for db in range(CB):
                lay.do("vector", lambda e, db=db: e.scalar_tensor_tensor(
                    kv_raw[:, db, :], vec[:, bass.ds(reg[e][1] * (4 * H) + BV * H + db * P, P)],
                    G[:, db, H:H + 1], m_ps[:, db * P:(db + 1) * P], ALU.mult, ALU.add),
                    done=("kv_raw", s) if db == CB - 1 else None, after=[("kv_ps", s)] + consts)
            mask = kv_mask[:, :].unsqueeze(1).broadcast_to([P, CB, P])
            out_read = [Prev(("out", s, DUOS - 1))]
            lay.do("vector", lambda e: e.tensor_tensor(kv[:, s, :, :], kv_raw[:, :, :], mask, ALU.mult),
                   done=("kv", s), after=[("kv_raw", s)] + out_read)
            bank, free = banks.take(("cst", s))
            for db in range(CB):
                lay.do("tensor", mm(bank[:, db * HB:(db + 1) * HB], ones[:, :], c21[:, db, :]),
                       done=("cst_ps", s) if db == CB - 1 else None, after=[("c21", s), free])
            lay.do("vector", lambda e: e.tensor_copy(cst[:, s, :], bank[:, 0:NH]), done=("cst", s),
                   after=[("cst_ps", s)] + [Prev(("den", s))])

        def chain_3(s):
            lay.do("tensor", mm(m_ps[:, 0:CB * P], rot[:, :], kv[:, s, :, :].rearrange("p c n -> p (c n)")),
                   done=("rot_ps", s), after=[("kv", s)])
            out_read = [Prev(("out", s, DUOS - 1))]
            lay.do("scalar", lambda e: e.activation(kv_rot[:, s, :, :].rearrange("p c n -> p (c n)"), m_ps[:, 0:CB * P], ACT.Copy),
                   done=("kv_rot", s), after=[("rot_ps", s)] + out_read)

        def queries(s):
            for qh in range(QH):
                tok = slice(qh * TQ, (qh + 1) * TQ)
                for db in range(CB):
                    k = qh * CB + db
                    bank, free = banks.take(("gT", s, k))
                    parts = [(bank[:, :], (w_hi[:, cb, db * P:(db + 1) * P], w_lo[:, cb, db * P:(db + 1) * P]),
                              (hT_hi[:, cb, tok], hT_lo[:, cb, tok]), cb == 0, cb == CB - 1) for cb in range(CB)]
                    lay.do("tensor", mm3(parts), done=("q", s, k), after=[("hT_lo", s, DUOS - 1), free, *w_now])
                    used = [("out", 0, DUOS - 1)] if s else [Prev(("out", 1, DUOS - 1))]
                    lay.do("scalar", lambda e, db=db, tok=tok, bank=bank: e.activation(
                        gT[:, db, tok], bank[:, :], ACT.Gelu, bias=bqs[:, bass.ds(reg[e][1] * CB + db, 1)]),
                        done=("gT", s, k), after=[("q", s, k)] + used + consts, apart=True)
                    for nm, dst, tab in (("qc", qc, cos_q), ("qs", qs, sin_q)):
                        lay.do("vector", lambda e, dst=dst, tab=tab, db=db, tok=tok: e.scalar_tensor_tensor(
                            dst[:, db, tok], gT[:, db, tok], 0.21, tab[:, db, tok], ALU.add, ALU.mult),
                            done=(nm, s, k), after=[("gT", s, k)] + used)

        def denominators(s):
            bank, free = banks.take(("den", s))
            for t in range(TILES):
                for db in range(CB):
                    lay.do("tensor", mm(bank[:, t * NH + db * HB:t * NH + (db + 1) * HB],
                                        gT[:, db, t * P:(t + 1) * P], kmb[:, s, db, :]),
                           done=("D", s) if t == TILES - 1 and db == CB - 1 else None,
                           after=[("gT", s, CB * QH - 1), ("kmb", s), free])
            add = cst[:, s, :].unsqueeze(1).broadcast_to([P, TILES, NH])
            lay.do("vector", lambda e: e.tensor_tensor(
                den[:, :, :], bank[:, 0:TILES * NH].rearrange("p (t n) -> p t n", t=TILES), add, ALU.add),
                done=("den", s), after=[("D", s), ("cst", s)])
            lay.do("vector", lambda e: e.reciprocal(z[:, :, :], den[:, :, :]), done=("z", s), after=[("den", s)])

        def outputs(s, u):
            bank, free = banks.take(("att", s, u))
            for t in range(2):
                tok = slice((2 * u + t) * P, (2 * u + t + 1) * P)
                for db in range(CB):
                    o = bank[:, t * H + db * P:t * H + (db + 1) * P]
                    lay.do("tensor", mm(o, qc[:, db, tok], kv[:, s, db, :], True, False), after=[
                        ("qs", s, CB * QH - 1), ("kv_rot", s), free])
                    lay.do("tensor", mm(o, qs[:, db, tok], kv_rot[:, s, db, :], False, True),
                           done=("out", s, u) if t == 1 and db == CB - 1 else None)
            yd = y[:, 2 * u:2 * u + 2, :]
            zb = z[:, 2 * u:2 * u + 2, :].rearrange("p t n -> p (t n)").unsqueeze(2).broadcast_to([P, 2 * NH, HD])
            free_y = [("ln", 0, u // 2)] if s else [Prev(("ln", 1, u // 2))]
            lay.do("vector", lambda e: e.tensor_tensor(
                yd.rearrange("p t (n d) -> p (t n) d", d=HD), bank[:, :].rearrange("p (n d) -> p n d", d=HD), zb, ALU.mult),
                done=("att", s, u), after=[("out", s, u), ("z", s)] + free_y)
            lay.do("gpsimd", lambda e: e.tensor_tensor(yd, yd, h[s][:, 2 * u:2 * u + 2, 0:H], ALU.add),
                   done=("y", s, u), after=[("att", s, u)])

        def norm(s, half):
            tiles = range(4 * half, 4 * half + 4)
            sl = slice(4 * half, 4 * half + 4)
            layernorm(lay, ("b", s, half), [y[:, t, :] for t in tiles], [h[s][:, t, 0:H] for t in tiles],
                      stats[:, sl], moments[:, sl], var_eps[:, sl], rstd[:, sl], minus_half, 1e-12,
                      row(GAIN), row(SHIFT), ready=[("y", s, 2 * half + 1)],
                      free=[("G", s, DUOS - 1)],
                      done=("ln", s, half), first=[At(setup, "half", 0)])

        def key_side(s, between):
            for n in range(DUOS + 2):
                if n < DUOS:
                    h_cols(s, n)
                if 0 <= n - 1 < DUOS:
                    keys(s, n - 1)
                if 0 <= n - 2 < DUOS:
                    gram(s, n - 2)
                if n in between:
                    between[n](1 - s)

        key_side(0, {})
        queries(0)
        key_side(1, {1: chain_1, 2: chain_2, 3: chain_3})
        denominators(0)
        outputs(0, 0)
        outputs(0, 1)
        norm(0, 0)
        chain_1(1)
        outputs(0, 2)
        chain_2(1)
        outputs(0, 3)
        norm(0, 1)
        chain_3(1)
        queries(1)
        lay.do("sync", lambda e: e.dma_start(w_raw[:, :, :].rearrange("p c n -> p (c n)"),
                                             wqkv[bass.ds(reg[e][1] + 1, 1)].rearrange("a p n -> (a p) n")),
               dma="w_raw", after=[("kv_ps", 1), At(setup, "w_lo", 0), Prev("w_next")])
        lay.do("scalar", lambda e: e.activation(w_hi[:, :, :], w_raw[:, :, 0:2 * H], ACT.Copy), done="w_next_hi",
               after=["w_raw", ("q", 1, CB * QH - 1)])
        lay.do("vector", lambda e: e.tensor_tensor(w_lo[:, :, :], w_raw[:, :, 0:2 * H], w_hi[:, :, :].bitcast(F32),
                                                   ALU.subtract), done="w_next", after=["w_next_hi"])
        denominators(1)
        for half in range(2):
            outputs(1, 2 * half)
            outputs(1, 2 * half + 1)
            norm(1, half)

        for s in range(LANES):
            def store(e, s=s):
                return e.dma_start(batch(e, h_out, s), h[s][:, :, 0:H])
            pair.do("sync", store, dma=("sent", s), after=[At(lay, ("ln", s, 1), "last layer")])

        with nc.Block() as block:
            def body(name):
                def program(eng):
                    setup.credit(name, eng)
                    setup.emit(name, eng, 0)
                    pair.credit(name, eng)
                    lay.credit(name, eng)
                    with eng.Fori(0, B // LANES) as i:
                        where = {"pair": i, "last layer": i * L + (L - 1)}
                        reg[eng] = (i, None)
                        loads = pair.queue[name][:LANES]
                        pair.emit(name, eng, i, where, loads)
                        if lay.queue[name]:
                            with eng.Fori(0, L) as l:
                                reg[eng] = (i, l)
                                lay.emit(name, eng, i * L + l, {"pair": i})
                        reg[eng] = (i, None)
                        pair.emit(name, eng, i, where, pair.queue[name][LANES:])
                    if name == "sync":
                        for s in range(LANES):
                            sem, per, const = pair.value(("sent", s), 0)
                            eng.wait_ge(sem, (B // LANES - 1) * per + const)
                return program
            for name in ENGINES:
                getattr_block(block, name)(body(name))


def ffn_phase(nc, x, h_in, out, w1, b1, w2, rows2, comp, eye, tri):
    B, T, H = x.shape
    F = w1.shape[1] // (H // P)
    CB, FB = H // P, F // P
    LANES = 2
    TOK = T // LANES
    TILES = TOK // P
    B2, GAIN, SHIFT = range(3)

    ctx = ExitStack()
    with ctx:
        sb = lambda n, s, d=F32: ctx.enter_context(nc.sbuf_tensor(n, s, d))
        split = lambda n, s: (sb(n + "_hi", s, F32R), sb(n + "_lo", s, F32R))

        up = [split("up0", [P, CB, F]), split("up1", [P, CB, F])]
        down = [split("down0", [P, FB, H]), split("down1", [P, FB, H])]
        identity = sb("identityC", [P, P])
        compose_phase(nc, up[1], down[1], comp, identity, eye, tri)

        pb = lambda n, s: ctx.enter_context(nc.psum_tensor(n, s, F32))
        b1s = sb("b1s", [P, FB])
        vec = sb("vecC", [P, 3 * H])
        minus_half = sb("minus_halfC", [P, TILES])
        hs = [sb(f"hC{s}", [P, TILES, H]) for s in range(LANES)]
        xs = [sb(f"xC{s}", [P, TILES, H]) for s in range(LANES)]
        y = [sb(f"yC{s}", [P, TILES, H]) for s in range(LANES)]
        x1 = [sb(f"x1{s}", [P, TILES, H]) for s in range(LANES)]
        res = [sb(f"resC{s}", [P, TILES, H]) for s in range(LANES)]
        aT = [split(f"aT{s}", [P, CB, TOK]) for s in range(LANES)]
        act = [split(f"act{s}", [P, FB, TOK]) for s in range(LANES)]
        gel = sb("gel", [P, 3, TOK])
        w_in = gel[:, :, :].rearrange("p a t -> p (a t)")[:, 0:1024]
        stats = sb("statsC", [P, LANES, TILES, 6])
        moments = sb("momentsC", [P, LANES, TILES, 2])
        var_eps = sb("var_epsC", [P, LANES, TILES])
        rstd = sb("rstdC", [P, LANES, TILES])
        banks = Banks([pb(f"bankC{i}", [P, 512]) for i in range(8)])

        setup = Stage(nc, ctx, "ffnset")
        work = Stage(nc, ctx, "ffn")
        reg = {}

        setup.do("scalar", lambda e: e.dma_start(b1s[:, :], b1), dma="consts")
        setup.do("scalar", lambda e: e.dma_start(vec[:, :], rows2.partition_broadcast(P)), dma="consts")
        setup.do("gpsimd", lambda e: e.memset(minus_half[:, :], -0.5), done="half")
        n = 0
        for src, (hi, lo) in ((w1, up[0]), (w2, down[0])):
            for part in range(2):
                cols = slice(part * 1024, (part + 1) * 1024)
                fl = lambda t: t[:, :, :].rearrange("p a b -> p (a b)")[:, cols]
                setup.do("sync", lambda e, src=src, cols=cols: e.dma_start(w_in, src[:, cols]), dma=("w", n),
                         after=[("w_lo", n - 1)] if n else [])
                setup.do("scalar", lambda e, d=fl(hi): e.activation(d, w_in, ACT.Copy), done=("w_hi", n), after=[("w", n)])
                setup.do("vector", lambda e, d=fl(lo), g=fl(hi): e.tensor_tensor(d, w_in, g.bitcast(F32), ALU.subtract),
                         done=("w_lo", n), after=[("w_hi", n)])
                n += 1
        weights = [At(setup, ("w_lo", n - 1), 0)]
        consts = [At(setup, "consts", 0), At(setup, "half", 0)]
        vrow = lambda k: vec[:, k * H:(k + 1) * H]

        h_rows = h_in.rearrange("b p (m f) -> b m p f", m=LANES)
        x_rows = x.rearrange("b (m p s) c -> b m p (s c)", m=LANES, p=P)
        o_rows = out.rearrange("b (m p s) c -> b m p (s c)", m=LANES, p=P)
        flat = lambda t: t[:, :, :].rearrange("p t c -> p (t c)")
        pick = lambda e, a, s: a[bass.ds(reg[e], 1), s].rearrange("a p f -> (a p) f")
        for s in range(LANES):
            work.do("sync", lambda e, s=s: e.dma_start(flat(hs[s]), pick(e, h_rows, s)), dma=("h", s),
                    after=[Prev(("res", 0, s)), Prev(("aT_ps", 0, s, CB - 1))])
            work.do("sync", lambda e, s=s: e.dma_start(flat(xs[s]), pick(e, x_rows, s)), dma=("x", s),
                    after=[Prev(("sum", s))])

        def transposes(k, s):
            src = (hs, x1)[k][s]
            ready = [("h", s)] if k == 0 else [("ln1", s)]
            hi, lo = aT[s]
            for cb in range(CB):
                bank, free = banks.take(("aT_lo", k, s, cb))
                for t in range(TILES):
                    work.do("tensor", lambda e, t=t, cb=cb, bank=bank: e.transpose(
                        bank[:, t * P:(t + 1) * P], src[:, t, cb * P:(cb + 1) * P], identity[:, :]),
                        done=("aT_ps", k, s, cb) if t == TILES - 1 else None, after=ready + [free])
                used = [("up", 0, s, FB - 1)] if k else [Prev(("up", 1, s, FB - 1))]
                work.do("scalar", lambda e, cb=cb, bank=bank: e.activation(hi[:, cb, :], bank[:, :], ACT.Copy),
                        done=("aT_hi", k, s, cb), after=[("aT_ps", k, s, cb)] + used)
                work.do("vector", lambda e, cb=cb, bank=bank: e.tensor_tensor(
                    lo[:, cb, :], bank[:, :], hi[:, cb, :].bitcast(F32), ALU.subtract),
                    done=("aT_lo", k, s, cb), after=[("aT_hi", k, s, cb)])
            if k == 0:
                b2 = vrow(B2).unsqueeze(1).broadcast_to([P, TILES, H])
                work.do("gpsimd", lambda e: e.tensor_tensor(res[s][:, :, :], hs[s][:, :, :], b2, ALU.add),
                        done=("res", 0, s), after=[("h", s), Prev(("y", 0, s, TILES // 2 - 1))] + consts)

        gel_turn = [0]
        gel_last = {}

        def up_product(k, s):
            hi, lo = aT[s]
            a_hi, a_lo = act[s]
            for fb in range(FB):
                g = gel_turn[0] % 3
                gel_turn[0] += 1
                bank, free = banks.take(("gelu", k, s, fb))
                f = slice(fb * P, (fb + 1) * P)
                parts = [(bank[:, :], (up[k][0][:, cb, f], up[k][1][:, cb, f]), (hi[:, cb, :], lo[:, cb, :]),
                          cb == 0, cb == CB - 1) for cb in range(CB)]
                work.do("tensor", mm3(parts), done=("up", k, s, fb), after=[("aT_lo", k, s, CB - 1), free] + weights)
                before = gel_last.get(g)
                gel_last[g] = ("act_lo", k, s, fb)
                work.do("scalar", lambda e, fb=fb, g=g, bank=bank: e.activation(
                    gel[:, g, :], bank[:, :], ACT.Gelu if k == 0 else ACT.Gelu_apprx_tanh,
                    bias=b1s[:, fb:fb + 1] if k == 0 else 0.0), done=("gelu", k, s, fb),
                    after=[("up", k, s, fb), before if before else gel_first(g)] + consts + weights)
                used = [("down", 0, s, TILES // 2 - 1)] if k else [Prev(("down", 1, s, TILES // 2 - 1))]
                work.do("vector", lambda e, fb=fb, g=g: e.tensor_copy(a_hi[:, fb, :], gel[:, g, :]),
                        done=("act_hi", k, s, fb), after=[("gelu", k, s, fb)] + used)
                work.do("vector", lambda e, fb=fb, g=g: e.tensor_tensor(
                    a_lo[:, fb, :], gel[:, g, :], a_hi[:, fb, :].bitcast(F32), ALU.subtract),
                    done=("act_lo", k, s, fb), after=[("act_hi", k, s, fb)])

        def gel_first(g):
            class Slot:
                banks = type("Last", (), {"last": gel_last})
                bank = g
            return BankFree(Slot.banks, g)

        def down_product(k, s):
            a_hi, a_lo = act[s]
            add = (res, x1)[k][s]
            for u in range(TILES // 2):
                bank, free = banks.take(("y", k, s, u))
                parts = []
                for t in range(2):
                    tok = slice((2 * u + t) * P, (2 * u + t + 1) * P)
                    parts += [(bank[:, t * H:(t + 1) * H], (a_hi[:, fb, tok], a_lo[:, fb, tok]),
                               (down[k][0][:, fb, :], down[k][1][:, fb, :]), fb == 0, fb == FB - 1) for fb in range(FB)]
                work.do("tensor", mm3(parts), done=("down", k, s, u), after=[("act_lo", k, s, FB - 1), free])
                two = lambda t, u=u: t[:, 2 * u:2 * u + 2, :].rearrange("p t c -> p (t c)")
                ready = [("res", 0, s)] if k == 0 else [("ln1", s)]
                used = [("ln1", s)] if k else [Prev(("out_sent", s)), Prev(("ln3", s))]
                work.do("vector", lambda e, bank=bank, two=two: e.tensor_tensor(
                    two(y[s]), bank[:, :], two(add), ALU.add), done=("y", k, s, u),
                    after=[("down", k, s, u)] + ready + used)

        def norms(k, s):
            tiles = lambda t: [t[s][:, i, :] for i in range(TILES)]
            st = (stats[:, s], moments[:, s], var_eps[:, s], rstd[:, s], minus_half)
            if k == 0:
                layernorm(work, ("first", s), tiles(y), tiles(y), *st, 1e-12, vrow(GAIN), vrow(SHIFT),
                          ready=[("y", 0, s, TILES // 2 - 1)], free=[], done=("ln0", s), first=consts)
                work.do("gpsimd", lambda e: e.tensor_tensor(y[s][:, :, :], y[s][:, :, :], xs[s][:, :, :], ALU.add),
                        done=("sum", s), after=[("ln0", s), ("x", s)])
                layernorm(work, ("second", s), tiles(y), tiles(x1), *st, 1e-5, None, None,
                          ready=[("sum", s)], free=[Prev(("y", 1, s, TILES // 2 - 1))], done=("ln1", s))
            else:
                layernorm(work, ("third", s), tiles(y), tiles(y), *st, 1e-5, None, None,
                          ready=[("y", 1, s, TILES // 2 - 1)], free=[], done=("ln3", s))
                work.do("sync", lambda e: e.dma_start(pick(e, o_rows, s), flat(y[s])), dma=("out_sent", s),
                        after=[("ln3", s)])

        transposes(0, 0)
        up_product(0, 0)
        transposes(0, 1)
        down_product(0, 0)
        norms(0, 0)
        up_product(0, 1)
        down_product(0, 1)
        transposes(1, 0)
        norms(0, 1)
        up_product(1, 0)
        transposes(1, 1)
        down_product(1, 0)
        norms(1, 0)
        up_product(1, 1)
        down_product(1, 1)
        norms(1, 1)
        run_loop(nc, setup, work, B, reg, waits=[("out_sent", s) for s in range(LANES)])


def compose_phase(nc, up, down, comp, identity, eye, tri):
    logits, bases, R = comp["logits"], (("A1", "B1"), ("A2", "B2")), 64
    N = 64
    K = 32
    ctx = ExitStack()
    with ctx:
        sb = lambda n, s, d=F32: ctx.enter_context(nc.sbuf_tensor(n, s, d))
        pb = lambda n, s: ctx.enter_context(nc.psum_tensor(n, s, F32))
        row = sb("logit_row", [N, 2, N])
        col = sb("logit_col", [N, 2])
        before = sb("before", [N, N])
        index = sb("index", [N, 1 + K])
        more = sb("more", [N, 2, N])
        same = sb("same", [N, 2, N])
        rank2 = sb("rank2", [N, 2, 2])
        rank = sb("rank", [N, 2])
        top = sb("top", [N, 2])
        expo = sb("expo", [N, 2])
        chosen = sb("chosen", [N, 2])
        onesN = sb("onesN", [N, P])
        weight = sb("weight", [N, 2, P])
        place = sb("place", [N, 2, K])
        inv_sum = sb("inv_sum", [P, 2])
        total = sb("total", [P, 2])
        w_row = sb("w_row", [P, 2, K])
        w_col = sb("w_col", [P, 2, K // 2])
        picks_f = sb("picks_f", [1, 2 * K])
        picks = sb("picks", [1, 2 * K], I32)
        zero = sb("zero", [P, 512], F32R)
        A = sb("Abuf", [P, 2, 8, 2, R])
        Bm = sb("Bbuf", [P, 2, 1024])
        AT = (sb("AT_hi", [P, 2, 1024], F32R), sb("AT_lo", [P, 2, 1024], F32R))
        Bs = (sb("Bs_hi", [P, 2, 1024], F32R), sb("Bs_lo", [P, 2, 1024], F32R))
        acc = [pb(f"acc{i}", [P, 512]) for i in range(4)]
        t_ps = [pb(f"t_ps{i}", [P, 512]) for i in range(4)]

        pre = Stage(nc, ctx, "rank")
        pre.do("sync", lambda e: e.dma_start(row[:, :, :].rearrange("n a b -> n (a b)"), logits.partition_broadcast(N)), dma="in")
        pre.do("sync", lambda e: e.dma_start(col[:, :], comp["logit_col"]), dma="in")
        pre.do("sync", lambda e: e.dma_start(before[:, :], tri), dma="in")
        pre.do("sync", lambda e: e.dma_start(index[:, :], comp["index"]), dma="in")
        pre.do("sync", lambda e: e.dma_start(identity[:, :], eye), dma="in")
        pre.do("gpsimd", lambda e: e.memset(onesN[:, :], 1.0), done="ones")
        pre.do("gpsimd", lambda e: e.memset(zero[:, :].bitcast(F32), 0.0), done="zero")
        V = lambda make, done=None, after=(): pre.do("vector", make, done=done, after=after)
        for f in range(2):
            V(lambda e, f=f: e.tensor_scalar(more[:, f, :], row[:, f, :], col[:, f:f + 1], None, ALU.is_gt), ("more", f), ["in"])
            V(lambda e, f=f: e.scalar_tensor_tensor(same[:, f, :], row[:, f, :], col[:, f:f + 1], before[:, :],
                                                    ALU.is_equal, ALU.mult), ("same", f), [])
        X = mybir.AxisListType.X
        V(lambda e: e.tensor_tensor(more[:, :, :], more[:, :, :], same[:, :, :], ALU.add), "both", [("same", 1)])
        V(lambda e: e.tensor_reduce(rank[:, :], more[:, :, :], X, ALU.add), "rank", ["both"])
        V(lambda e: e.tensor_reduce(top[:, :], row[:, :, :], X, ALU.max), "top", [])
        V(lambda e: e.tensor_scalar(chosen[:, :], rank[:, :], float(K), None, ALU.is_lt), "chosen", ["rank"])
        V(lambda e: e.tensor_tensor(expo[:, :], col[:, :], top[:, :], ALU.subtract), "less_top", ["top"])
        pre.do("scalar", lambda e: e.activation(expo[:, :], expo[:, :], ACT.Exp), done="exp", after=["less_top"])
        V(lambda e: e.tensor_tensor(expo[:, :], expo[:, :], chosen[:, :], ALU.mult), "kept", ["exp", "chosen"])
        for f in range(2):
            V(lambda e, f=f: e.tensor_scalar(weight[:, f, :], onesN[:, :], expo[:, f:f + 1], None, ALU.mult), ("weight", f), ["kept", "ones"])
            V(lambda e, f=f: e.tensor_scalar(place[:, f, :], index[:, 1:1 + K], rank[:, f:f + 1], None, ALU.is_equal), ("place", f), ["in"])
        for f in range(2):
            pre.do("tensor", mm(t_ps[0][:, f * K:(f + 1) * K], weight[:, f, :], place[:, f, :]), done=("w_row", f),
                   after=[("place", 1)])
            pre.do("tensor", mm(t_ps[1][0:1, f * K:(f + 1) * K], index[:, 0:1], place[:, f, :]), done=("pick", f),
                   after=[])
        V(lambda e: e.tensor_copy(w_row[:, :, :].rearrange("p a b -> p (a b)"), t_ps[0][:, 0:2 * K]), "w_row", [("pick", 1)])
        V(lambda e: e.tensor_copy(picks[:, :], t_ps[1][0:1, 0:2 * K]), "picks", [])
        V(lambda e: e.tensor_reduce(total[:, :], w_row[:, :, :], X, ALU.add), "total", ["w_row"])
        V(lambda e: e.reciprocal(inv_sum[:, :], total[:, :]), "inv", ["total"])
        for f in range(2):
            for half in range(2):
                rows = slice(R * half, R * half + R)
                V(lambda e, f=f, half=half, rows=rows: e.tensor_scalar(
                    w_col[rows, f, :], w_row[rows, f, :].rearrange("p (a two) -> p a two", two=2)[:, :, half],
                    inv_sum[rows, f:f + 1], None, ALU.mult), ("w_col", f, half), ["inv"])

        stages, reg, cache = [], {}, {}
        for f in range(2):
            A_d, B_d = comp[bases[f][0]], comp[bases[f][1]]
            d_in, d_out = A_d.shape[1], B_d.shape[2]
            MB = d_in // P
            NW = min(512, d_out)
            work = Stage(nc, ctx, f"comp{f}")
            a_rows = A_d.rearrange("k (o p) r -> k p o r", p=P)

            def out_of(m, n):
                at = m * d_out + n * NW
                return acc[at // 512][:, at % 512:at % 512 + NW]

            for q in range(2):
                for half in range(2):
                    def loads(e, q=q, half=half, f=f, a_rows=a_rows, B_d=B_d, MB=MB, d_out=d_out, which=0):
                        k = reg_pick(e, f, q, half)
                        if which == 0:
                            return e.dma_start(A[:, q, 0:MB, half, :], a_rows[bass.ds(k, 1)].rearrange("a p o r -> (a p) o r"))
                        return e.dma_start(Bm[R * half:R * half + R, q, 0:d_out], B_d[bass.ds(k, 1)].rearrange("a r n -> (a r) n"))
                    for which in range(2):
                        work.do("sync", lambda e, g=loads, w=which: g(e, which=w), dma=("AB", q),
                                after=[Prev(("AT_lo", q)), Prev(("Bs_lo", q)), Prev(("AT_ps", q))])

            def reg_pick(e, f, q, half):
                key = (id(e), f, q, half)
                if key not in cache:
                    cache[key] = e.value_load(picks[0:1, bass.ds(reg[e] * 4 + (f * K + 2 * q + half), 1)],
                                              min_val=0, max_val=N - 1)
                return cache[key]
            for q in range(2):
                wq = lambda e, f=f, q=q: w_col[:, f, bass.ds(reg[e] * 2 + q, 1)]
                n_banks = max(1, d_in // 512)
                for m in range(MB):
                    bank = t_ps[2 * q + m // 4]
                    work.do("tensor", lambda e, m=m, q=q, bank=bank: e.transpose(
                        bank[:, (m % 4) * P:(m % 4 + 1) * P], A[:, q, m, :, :].rearrange("p h r -> p (h r)"), identity[:, :]),
                        done=("AT_ps", q) if m == MB - 1 else None, after=[("AB", q), Prev(("AT_lo", q))])
                wd = min(512, d_in)
                small_a = d_in < d_out
                for i in range(n_banks):
                    bank = t_ps[2 * q + i]
                    dst = [t[:, q, i * wd:(i + 1) * wd] for t in AT]
                    if small_a:
                        work.do("scalar", lambda e, dst=dst, bank=bank, wq=wq, wd=wd: e.activation(dst[0], bank[:, 0:wd], ACT.Copy, scale=wq(e)),
                                done=("AT_hi", q, i), after=[("AT_ps", q), Prev(("mm", q))], apart=True)
                        work.do("vector", lambda e, dst=dst, bank=bank, wq=wq, wd=wd: e.scalar_tensor_tensor(
                            dst[1], bank[:, 0:wd], wq(e), dst[0].bitcast(F32), ALU.mult, ALU.subtract),
                            done=("AT_lo", q) if i == n_banks - 1 else ("AT_lo", q, i), after=[("AT_hi", q, i)])
                    else:
                        work.do("scalar", lambda e, dst=dst, bank=bank, wd=wd: e.activation(dst[0], bank[:, 0:wd], ACT.Copy),
                                done=("AT_hi", q, i), after=[("AT_ps", q), Prev(("mm", q))])
                        work.do("vector", lambda e, dst=dst, bank=bank, wd=wd: e.tensor_tensor(
                            dst[1], bank[:, 0:wd], dst[0].bitcast(F32), ALU.subtract),
                            done=("AT_lo", q) if i == n_banks - 1 else ("AT_lo", q, i), after=[("AT_hi", q, i)])
                bd = [t[:, q, 0:d_out] for t in Bs]
                bsrc = Bm[:, q, 0:d_out]
                if small_a:
                    work.do("scalar", lambda e, bd=bd, bsrc=bsrc: e.activation(bd[0], bsrc, ACT.Copy), done=("Bs_hi", q),
                            after=[("AB", q), Prev(("mm", q))])
                    work.do("vector", lambda e, bd=bd, bsrc=bsrc: e.tensor_tensor(bd[1], bsrc, bd[0].bitcast(F32), ALU.subtract),
                            done=("Bs_lo", q), after=[("Bs_hi", q)])
                else:
                    work.do("scalar", lambda e, bd=bd, bsrc=bsrc, wq=wq: e.activation(bd[0], bsrc, ACT.Copy, scale=wq(e)), done=("Bs_hi", q),
                            after=[("AB", q), Prev(("mm", q))], apart=True)
                    work.do("vector", lambda e, bd=bd, bsrc=bsrc, wq=wq: e.scalar_tensor_tensor(
                        bd[1], bsrc, wq(e), bd[0].bitcast(F32), ALU.mult, ALU.subtract),
                        done=("Bs_lo", q), after=[("Bs_hi", q)])
                parts = [(out_of(m, n), (AT[0][:, q, m * P:(m + 1) * P], AT[1][:, q, m * P:(m + 1) * P]),
                          (Bs[0][:, q, n * NW:(n + 1) * NW], Bs[1][:, q, n * NW:(n + 1) * NW]), False, False)
                         for m in range(MB) for n in range(d_out // NW)]
                work.do("tensor", mm3(parts), done=("mm", q), after=[("AT_lo", q), ("Bs_lo", q)])
            stages.append(work)

        post = [Stage(nc, ctx, f"compout{f}") for f in range(2)]
        for f, (hi, lo) in enumerate((up, down)):
            for i in range(4):
                cols = slice(i * 512, (i + 1) * 512)
                fl = lambda t: t[:, :, :].rearrange("p a b -> p (a b)")[:, cols]
                last = At(stages[f], ("mm", 1), K // 4 - 1)
                post[f].do("tensor", lambda e, i=i: e.matmul(acc[i][:, :], zero[:, 0:P], zero[:, :], start=False, stop=True),
                           done=("closed", i), after=[last])
                post[f].do("scalar", lambda e, i=i, d=fl(hi): e.activation(d, acc[i][:, :], ACT.Copy), done=("hi", i),
                           after=[("closed", i)])
                post[f].do("vector", lambda e, i=i, d=fl(lo), g=fl(hi): e.tensor_tensor(d, acc[i][:, :], g.bitcast(F32), ALU.subtract),
                           done=("lo", i), after=[("hi", i)])

        with nc.Block() as block:
            def body(name):
                def program(eng):
                    pre.credit(name, eng)
                    pre.emit(name, eng, 0)
                    for f in range(2):
                        work = stages[f]
                        work.credit(name, eng)
                        post[f].credit(name, eng)
                        if name == "tensor":
                            if f == 1:
                                sem, per, const = post[0].value(("lo", 3), 0)
                                eng.wait_ge(sem, const)
                            else:
                                sem, per, const = pre.value("zero", 0)
                                eng.wait_ge(sem, const)
                                sem, per, const = pre.value("picks", 0)
                                eng.wait_ge(sem, const)
                            for i in range(4):
                                eng.matmul(acc[i][:, :], zero[:, 0:P], zero[:, :], start=True, stop=False)
                        if name in ("scalar", "vector"):
                            sem, per, const = pre.value(("w_col", 1, 1), 0)
                            eng.wait_ge(sem, const)
                        if name == "sync":
                            sem, per, const = pre.value("picks", 0)
                            eng.wait_ge(sem, const)
                            if f == 1:
                                sem, per, const = post[0].value(("lo", 3), 0)
                                eng.wait_ge(sem, const)
                        if work.queue[name]:
                            with eng.Fori(0, K // 4) as i:
                                reg[eng] = i
                                work.emit(name, eng, i)
                        post[f].emit(name, eng, 0)
                return program
            for name in ENGINES:
                getattr_block(block, name)(body(name))


def layernorm(stage, key, ins, outs, stats, moments, var_eps, rstd, minus_half, eps, gain, shift,
              ready, free, done, first=()):
    n = len(ins)
    for t in range(n):
        stage.do("vector", lambda e, t=t: e.bn_stats(stats[:, t, :], ins[t]), done=("stats", key, t),
                 after=list(ready) + list(first) if t == 0 else [])
    for t in range(n):
        stage.do("vector", lambda e, t=t: e.bn_aggr(moments[:, t, :], stats[:, t, :]), done=("moments", key, t),
                 after=[("stats", key, t)], apart=True)
    stage.do("vector", lambda e: e.tensor_scalar(var_eps, moments[:, :, 1], eps, None, ALU.add),
             done=("var", key), after=[("moments", key, n - 1)])
    stage.do("gpsimd", lambda e: e.tensor_tensor(rstd, var_eps, minus_half[:, 0:n], ALU.pow),
             done=("rstd", key), after=[("var", key)])
    for t in range(n):
        if gain is not None:
            stage.do("vector", lambda e, t=t: e.scalar_tensor_tensor(
                ins[t], ins[t], moments[:, t, 0:1], fixed(gain, e), ALU.subtract, ALU.mult), done=("centred", key, t),
                after=[("rstd", key)])
    for t in range(n):
        if gain is not None:
            stage.do("vector", lambda e, t=t: e.scalar_tensor_tensor(
                outs[t], ins[t], rstd[:, t:t + 1], fixed(shift, e), ALU.mult, ALU.add),
                done=done if t == n - 1 else (done, t),
                after=[("centred", key, t)] + (list(free) if t == 0 else []))
        else:
            stage.do("vector", lambda e, t=t: e.tensor_scalar(
                outs[t], ins[t], moments[:, t, 0:1], rstd[:, t:t + 1], ALU.subtract, ALU.mult),
                done=done if t == n - 1 else (done, t),
                after=[("rstd", key)] + (list(free) if t == 0 else []))


def fixed(operand, e):
    return operand(e) if callable(operand) else operand


def run_loop(nc, setup, work, trips, reg, waits):
    with nc.Block() as block:
        def body(name):
            def program(eng):
                setup.credit(name, eng)
                setup.emit(name, eng, 0)
                work.credit(name, eng)
                if work.queue[name]:
                    with eng.Fori(0, trips) as i:
                        reg[eng] = i
                        work.emit(name, eng, i)
                if name == "sync":
                    for w in waits:
                        sem, per, const = work.value(w, 0)
                        eng.wait_ge(sem, (trips - 1) * per + const)
            return program
        for name in ENGINES:
            getattr_block(block, name)(body(name))


def getattr_block(block, name):
    return {"tensor": block.tensor, "vector": block.vector, "scalar": block.scalar,
            "gpsimd": block.gpsimd, "sync": block.sync}[name]


def build(nc, t):
    conv_phase(nc, t["x"], t["bands1"], t["bands2"], t["bias1"], t["bias2"], t["ln0"], t["eye"], t["h0"])
    attention_phase(nc, t["h0"], t["h4"], t["x"].shape[1], t["x"].shape[2], t["wqkv"], t["rows"], t["bq"],
                    {n: t[n] for n in ("cos_k", "sin_k", "cos_q", "sin_q")}, t)
    comp = {n: t[n] for n in ("logits", "logit_col", "index", "A1", "B1", "A2", "B2")}
    ffn_phase(nc, t["x"], t["h4"], t["out"], t["w1"], t["b1"], t["w2"], t["rows2"], comp, t["eye"], t["tri"])


def layout(inputs):
    import numpy as np
    f = lambda n: np.ascontiguousarray(inputs["L0_attn_" + n])
    x = f("x")
    H = x.shape[2]
    c1, c2 = f("conv1_w"), f("conv2_w")
    d = {"x": x}
    w1 = c1.reshape(H // 16, 2, 8, 4, 5)
    b1 = np.zeros((8, 2, 8, H // 16, 2, 4, 8, 4), c1.dtype)
    for k in range(2):
        for c in range(8):
            for s in range(4):
                for tap in range(5):
                    b1[s + tap, k, c, :, k, s, c, :] = w1[:, k, c, :, tap]
    d["bands1"] = b1.reshape(128, -1)
    w2 = c2.reshape(H // 8, 8, 4, 5)
    b2 = np.zeros((4, 8, 4, H // 8, 3, 4, 8), c2.dtype)
    for s in range(4):
        for c in range(8):
            for g in range(3):
                for so in range(4):
                    tap = 4 * (g - 1) + s - so + 2
                    if 0 <= tap < 5:
                        b2[s, c, :, :, g, so, c] = w2[:, c, :, tap].T
    d["bands2"] = b2.reshape(128, -1)
    bias1 = f("conv1_b").reshape(H // 8, 32).T
    d["bias1"] = np.ascontiguousarray(np.tile(bias1, (4, 1)))
    bias2 = f("conv2_b").reshape(H // 32, 4, 1, 8)
    d["bias2"] = np.ascontiguousarray(np.broadcast_to(bias2, (H // 32, 4, 4, 8)).reshape(H // 32, 128).T)
    d["ln0"] = np.stack([f("ln0_g"), f("ln0_b")])
    w = np.concatenate([f("Wq"), f("Wk"), f("Wv")], axis=2)
    L, T = w.shape[0], x.shape[1]
    w = w.reshape(L, 2, 128, 3 * H).transpose(0, 2, 1, 3).reshape(L, 128, 6 * H)
    d["wqkv"] = np.ascontiguousarray(np.concatenate([w, w[:1]]))
    d["rows"] = np.stack([f("bk"), f("bv"), f("lnA_g"), f("lnA_b")], axis=1).reshape(1, -1)
    d["bq"] = np.ascontiguousarray(f("bq").reshape(L * 2, 128).T)
    inv = (np.float32(1) / np.float32(10000) ** (np.arange(0, H, 2, dtype=np.float32) / np.float32(H))).astype(np.float32)
    angle = np.repeat(np.arange(T, dtype=np.float32)[:, None] * inv[None, :], 2, axis=1).astype(np.float64)
    cos, sin = np.cos(angle).astype(np.float32), np.sin(angle).astype(np.float32)
    sign = np.tile(np.array([-1, 1], np.float32), H // 2)
    order = lambda a: a.reshape(T // 512, 128, 4, H).transpose(0, 2, 1, 3)
    rows = lambda a: np.ascontiguousarray(order(a).reshape(T // 128, 128, H).transpose(1, 0, 2).reshape(128, -1))
    cols = lambda a: np.ascontiguousarray(order(a).reshape(T, H).T.reshape(2, 128, T).transpose(1, 0, 2).reshape(128, -1))
    d["cos_k"], d["sin_k"] = rows(cos), rows(sin * sign)
    d["cos_q"], d["sin_q"] = cols(cos), cols(sin)
    i = np.arange(0, 128, 2)
    rot = np.zeros((128, 128), np.float32)
    rot[i + 1, i], rot[i, i + 1] = 1, -1
    d["rot"] = rot
    head = np.arange(128) // 16
    d["kv_mask"] = ((head[:, None] == head[None, :]) / T).astype(np.float32)
    d["head_mask"] = (head[:, None] == np.arange(8)[None, :]).astype(np.float32)
    d["w1"] = np.ascontiguousarray(f("W1").reshape(2, 128, 4 * H).transpose(1, 0, 2).reshape(128, 8 * H))
    d["w2"] = np.ascontiguousarray(f("W2").reshape(8, 128, H).transpose(1, 0, 2).reshape(128, 8 * H))
    d["b1"] = np.ascontiguousarray(f("b1").reshape(8, 128).T)
    d["rows2"] = np.concatenate([f("b2"), f("ln2_g"), f("ln2_b")])[None, :]
    g = lambda n: np.ascontiguousarray(inputs["L0_ffn_" + n])
    d["A1"], d["B1"], d["A2"], d["B2"] = g("fc1_A"), g("fc1_B"), g("fc2_A"), g("fc2_B")
    logits = np.stack([g("fc1_logits"), g("fc2_logits")])
    d["logits"], d["logit_col"] = logits.reshape(1, -1), np.ascontiguousarray(logits.T)
    n = np.arange(64, dtype=np.float32)
    d["index"] = np.concatenate([n[:, None], np.tile(n[None, :32], (64, 1))], axis=1)
    d["tri"] = (n[None, :] < n[:, None]).astype(np.float32)
    d["eye"] = np.eye(128, dtype=np.float32)
    return d


def kernel(**inputs):
    import numpy as _np
    import concourse.bacc as _bacc
    from concourse import mybir as _mybir
    from concourse.bass_utils import run_bass_kernel_spmd as _run

    nc = _bacc.Bacc("TRN2", target_bir_lowering=False, num_devices=1)
    arrays, t = {}, {}
    for name, a in layout(inputs).items():
        arrays[f"in_{name}"] = a
        t[name] = nc.dram_tensor(f"in_{name}", a.shape, _mybir.dt.from_np(a.dtype), kind="ExternalInput").ap()
    shape = inputs["L0_attn_x"].shape
    t["out"] = nc.dram_tensor("out_0", shape, _mybir.dt.float32, kind="ExternalOutput").ap()
    rows = (shape[0], 128, shape[1] * shape[2] // 128)
    t["h0"] = nc.dram_tensor("h0", rows, _mybir.dt.float32, kind="Internal").ap()
    t["h4"] = nc.dram_tensor("h4", rows, _mybir.dt.float32, kind="Internal").ap()
    build(nc, t)
    r = _run(nc, [arrays], core_ids=[0])
    return r.results[0]["out_0"]
```

```python
import concourse.bass as bass
from concourse import mybir
from contextlib import ExitStack

F32 = mybir.dt.float32
F32R = mybir.dt.float32r
U32 = mybir.dt.uint32
I32 = mybir.dt.int32
ALU = mybir.AluOpType
ACT = mybir.ActivationFunctionType

P = 128
ENGINES = ("tensor", "vector", "scalar", "gpsimd", "sync")


class Stage:

    def __init__(self, nc, ctx, label):
        self.nc, self.ctx, self.label = nc, ctx, label
        self.queue = {e: [] for e in ENGINES}
        self.sem, self.count, self.event = {}, {}, {}
        self.dma_sem, self.dma_count, self.dma_engine = {}, {}, {}
        self.relay = {}

    def do(self, engine, make, done=None, after=(), dma=None, apart=False):
        if done is not None:
            if engine not in self.sem:
                self.sem[engine] = self.ctx.enter_context(self.nc.semaphore(f"{self.label}_{engine}"))
                self.count[engine] = 0
            self.count[engine] += 1
            assert done not in self.event, done
            self.event[done] = (engine, self.count[engine])
        if dma is not None:
            if dma not in self.dma_sem:
                tag = "_".join(str(x) for x in dma) if isinstance(dma, tuple) else dma
                self.dma_sem[dma] = self.ctx.enter_context(self.nc.semaphore(f"{self.label}_dma_{tag}"))
                self.dma_count[dma] = 0
                self.dma_engine[dma] = engine
            self.dma_count[dma] += 1
        apart = apart or engine in ("gpsimd", "sync")
        if apart and engine not in self.relay:
            self.relay[engine] = self.ctx.enter_context(self.nc.semaphore(f"{self.label}_relay_{engine}"))
        self.queue[engine].append((make, done, after, dma, apart))

    def value(self, name, iteration, back=0):
        if name in self.dma_sem:
            n = 16 * self.dma_count[name]
            return self.dma_sem[name], n, n * (2 - back)
        engine, k = self.event[name]
        n = self.count[engine]
        return self.sem[engine], n, n * (1 - back) + k

    def credit(self, engine, eng):
        if engine in self.sem:
            eng.sem_inc(self.sem[engine], self.count[engine])
        for name, count in self.dma_count.items():
            if self.dma_engine[name] == engine:
                eng.sem_inc(self.dma_sem[name], 16 * count)

    def emit(self, engine, eng, iteration, where_is=None, ops=None):
        seen = {}
        for make, done, after, dma, apart in (self.queue[engine] if ops is None else ops):
            waited = False
            for item in after:
                if isinstance(item, At):
                    stage, name, where, back = item.stage, item.name, item.iteration, 0
                    if isinstance(where, str):
                        where = where_is[where]
                elif isinstance(item, LastUse):
                    stage, name, where, back = item.stage, item.banks.last[item.bank], where_is[item.iteration], 0
                elif isinstance(item, BankFree):
                    stage, name, where, back = self, item.banks.last[item.bank], iteration, 1
                elif isinstance(item, Prev):
                    stage, name, where, back = self, item.name, iteration, 1
                else:
                    stage, name, where, back = self, item, iteration, 0
                sem, per, const = stage.value(name, where, back)
                spot = (stage.label, id(sem), id(where))
                if seen.get(spot, -1) >= const:
                    continue
                seen[spot] = const
                eng.wait_ge(sem, where * per + const)
                waited = True
                if engine == "sync" and not isinstance(iteration, int):
                    eng.sem_inc(self.relay[engine], 1)
                    waited = False
            if waited and apart and not isinstance(iteration, int):
                eng.sem_inc(self.relay[engine], 1)
            inst = make(eng)
            if done is not None:
                inst.then_inc(self.sem[engine], 1)
            if dma is not None:
                inst.then_inc(self.dma_sem[dma], 16)


class Prev:
    def __init__(self, name):
        self.name = name


class At:
    def __init__(self, stage, name, iteration):
        self.stage, self.name, self.iteration = stage, name, iteration


class Banks:

    def __init__(self, tensors):
        self.tensors, self.turn, self.last = tensors, 0, {}

    def take(self, reader):
        b = self.turn % len(self.tensors)
        self.turn += 1
        free = self.last.get(b, None)
        self.last[b] = reader
        return self.tensors[b], (free if free is not None else BankFree(self, b))


class BankFree:

    def __init__(self, banks, bank):
        self.banks, self.bank = banks, bank


class LastUse:

    def __init__(self, stage, banks, bank, iteration):
        self.stage, self.banks, self.bank, self.iteration = stage, banks, bank, iteration


def mm(out, lhsT, rhs, start=True, stop=True):
    return lambda e: e.matmul(out, lhsT, rhs, start=start, stop=stop)


def mm3(parts):
    def make(e):
        for out, (wh, wl), (xh, xl), start, stop in parts:
            e.matmul(out, wh, xh, start=start, stop=False)
            e.matmul(out, wh, xl, start=False, stop=False)
            last = e.matmul(out, wl, xh, start=False, stop=stop)
        return last
    return make


def conv_phase(nc, x, bands1, bands2, conv1_b, conv2_b, ln0, eye, h0):
    B, N, H = x.shape
    S, W, TAPS_AHEAD = 4, 8, 2
    G = N // S
    MT = G // P
    CP = H // 32
    TILES = MT * S
    LANES = 2
    HB = 4

    xg = x.rearrange("b (g s) c -> b g s c", s=S)

    ctx = ExitStack()
    with ctx:
        sb = lambda n, s, d=F32: ctx.enter_context(nc.sbuf_tensor(n, s, d))
        pb = lambda n, s: ctx.enter_context(nc.psum_tensor(n, s, F32))

        band1 = sb("band1", [P, CP * HB * P])
        band1_hi = sb("band1_hi", [P, CP * HB, P], F32R)
        band1_lo = sb("band1_lo", [P, CP * HB, P], F32R)
        band2 = sb("band2", [P, CP * HB, 3, 32])
        bias1 = sb("bias1", [P, CP * HB])
        bias2 = sb("bias2", [P, CP])
        gain = sb("gain0", [P, H])
        shift = sb("shift0", [P, H])
        identity = sb("identityA", [P, P])
        minus_half = sb("minus_halfA", [P, TILES])
        xw = [sb(f"xw{l}", [P, MT, W, H]) for l in range(LANES)]
        xr = sb("xr", [P, 2, 2, MT, P])
        xt_hi = sb("xt_hi", [P, 2, 2, G], F32R)
        xt_lo = sb("xt_lo", [P, 2, 2, G], F32R)
        hidden = sb("hidden", [P, 2, HB, G + 2])
        convT = sb("convT", [P, 2, G])
        y = [sb(f"yA{l}", [P, TILES, H]) for l in range(LANES)]
        h = [sb(f"hA{l}", [P, TILES, H]) for l in range(LANES)]
        stats = sb("statsA", [P, LANES, TILES, 6])
        moments = sb("momentsA", [P, LANES, TILES, 2])
        var_eps = sb("var_epsA", [P, LANES, TILES])
        rstd = sb("rstdA", [P, LANES, TILES])

        xt_ps = [pb(f"xt_ps{i}", [P, 2, G]) for i in range(2)]
        hid_ps = [pb(f"hid_ps{i}", [P, 2, G]) for i in range(3)]
        conv_ps = pb("conv_ps", [P, 512])
        back_ps = [pb(f"back_ps{i}", [P, MT, P]) for i in range(2)]

        setup = Stage(nc, ctx, "convset")
        work = Stage(nc, ctx, "conv")

        setup.do("sync", lambda e: e.dma_start(band1[:, :], bands1), dma="band1")
        setup.do("sync", lambda e: e.dma_start(identity[:, :], eye), dma="small")
        setup.do("sync", lambda e: e.dma_start(bias1[:, :], conv1_b), dma="small")
        setup.do("scalar", lambda e: e.dma_start(band2[:, :, :, :].rearrange("p b d n -> p (b d n)"), bands2), dma="small")
        setup.do("scalar", lambda e: e.dma_start(bias2[:, :], conv2_b), dma="small")
        setup.do("scalar", lambda e: e.dma_start(gain[:, :], ln0[0:1, :].partition_broadcast(P)), dma="small")
        setup.do("scalar", lambda e: e.dma_start(shift[:, :], ln0[1:2, :].partition_broadcast(P)), dma="small")
        b1f = lambda t: t[:, :, :].rearrange("p b n -> p (b n)")
        setup.do("vector", lambda e: e.tensor_copy(b1f(band1_hi), band1[:, :]), done="hi", after=["band1"])
        setup.do("vector", lambda e: e.tensor_tensor(b1f(band1_lo), band1[:, :], b1f(band1_hi).bitcast(F32),
                                                     ALU.subtract), done="lo", after=["hi"])
        setup.do("gpsimd", lambda e: e.memset(minus_half[:, :], -0.5), done="half")
        for l in range(LANES):
            setup.do("gpsimd", lambda e, l=l: e.memset(xw[l][:, 0, 0:2, :], 0.0), done=("pad0", l))
            setup.do("gpsimd", lambda e, l=l: e.memset(xw[l][:, MT - 1, W - 2:W, :], 0.0), done=("pad1", l))
        setup.do("gpsimd", lambda e: e.memset(hidden[:, :, :, 0:1], 0.0), done="pad2")
        setup.do("gpsimd", lambda e: e.memset(hidden[:, :, :, G + 1:G + 2], 0.0), done="pad3")

        def load(l, reg):
            tile = xw[l]
            b = lambda e: reg[e] * LANES + l
            q = "sync"

            def copy(p0, p1, mt, w0, w1, s0, g0):
                def make(e):
                    src = xg[bass.ds(b(e), 1), g0:g0 + p1 - p0, s0:s0 + w1 - w0, :]
                    return e.dma_start(tile[p0:p1, mt, w0:w1, :], src.rearrange("a g s c -> (a g) s c"))
                free = [Prev(("x_read", l)), Prev(("x_sent", l))]
                work.do(q, make, dma=("x", l), after=free + [At(setup, ("pad0", l), 0), At(setup, ("pad1", l), 0)])

            cut = 112
            for mt in range(MT):
                g = mt * P
                copy(0, P, mt, 2, 6, 0, g)
                if mt == 0:
                    copy(1, 1 + cut, mt, 0, 2, 2, 0)
                    copy(1 + cut, P, mt, 0, 2, 2, cut)
                else:
                    copy(0, P, mt, 0, 2, 2, g - 1)
                if mt == MT - 1:
                    copy(0, cut, mt, 6, 8, 0, g + 1)
                    copy(cut, P - 1, mt, 6, 8, 0, g + 1 + cut)
                else:
                    copy(0, P, mt, 6, 8, 0, g + 1)

        steps = [(l, cp) for l in range(LANES) for cp in range(CP)]
        n_steps = len(steps)

        def earlier(kind, n, ring):
            return [(kind, n - ring)] if n >= ring else [Prev((kind, n - ring + n_steps))]

        def to_channels(n):
            l, cp = steps[n]
            bank = xt_ps[n % 2]
            for mt in range(MT):
                work.do("gpsimd", lambda e, mt=mt: e.tensor_copy(
                    xr[:, n % 2, :, mt, :].rearrange("p a (w c) -> p w a c", w=W),
                    xw[l][:, mt, :, 32 * cp:32 * cp + 32].rearrange("p w (a c) -> p w a c", a=2)),
                    done=("xr", n) if mt == MT - 1 else None,
                    after=[("x", l)] + earlier("xt", n, 2))
            for cg in range(2):
                for mt in range(MT):
                    last = cg == 1 and mt == MT - 1
                    work.do("tensor", lambda e, cg=cg, mt=mt: e.transpose(
                        bank[:, cg, mt * P:(mt + 1) * P], xr[:, n % 2, cg, mt, :], identity[:, :]),
                        done=("xt", n) if last else None,
                        after=[("xr", n), At(setup, "small", 0)] + earlier("xt_lo", n, 2))
            r = n % 2
            flat = lambda t: t[:, :, :].rearrange("p a g -> p (a g)")
            hi = xt_hi[:, r, :, :].rearrange("p a g -> p (a g)")
            lo = xt_lo[:, r, :, :].rearrange("p a g -> p (a g)")
            work.do("scalar", lambda e: e.activation(hi, flat(bank), ACT.Copy), done=("xt_hi", n),
                    after=[("xt", n)] + earlier("conv1", n, 2))
            work.do("vector", lambda e: e.tensor_tensor(lo, flat(bank), hi.bitcast(F32), ALU.subtract),
                    done=("xt_lo", n), after=[("xt_hi", n)])

        def conv1(n):
            l, cp = steps[n]
            r = n % 2
            for cg in range(2):
                k = 2 * n + cg
                bank = hid_ps[k % 3]
                parts = [(bank[:, j, :], (band1_hi[:, 4 * cp + 2 * cg + j, :], band1_lo[:, 4 * cp + 2 * cg + j, :]),
                          (xt_hi[:, r, cg, :], xt_lo[:, r, cg, :]), True, True) for j in range(2)]
                free = [("hidden", k - 3)] if k >= 3 else [Prev(("hidden", k - 3 + 2 * n_steps))]
                work.do("tensor", mm3(parts), done=("hid", k),
                        after=[("xt_lo", n), At(setup, "lo", 0)] + free)
                if cg == 1:
                    work.event[("conv1", n)] = work.event[("hid", k)]
                for j in range(2):
                    blk = 2 * cg + j
                    work.do("scalar", lambda e, j=j, blk=blk, bank=bank: e.activation(
                        hidden[:, r, blk, 1:1 + G], bank[:, j, :], ACT.Gelu,
                        bias=bias1[:, 4 * cp + blk:4 * cp + blk + 1]),
                        done=("hidden", k) if j else None,
                        after=[("hid", k)] + earlier("conv", n, 2))

        def conv2(n):
            l, cp = steps[n]
            r = n % 2
            for d in range(3):
                for blk in range(HB):
                    work.do("tensor", mm(conv_ps[32 * blk:32 * blk + 32, 0:G], band2[:, 4 * cp + blk, d, :],
                                         hidden[:, r, blk, d:d + G], d == 0, d == 2),
                            done=("conv", n) if d == 2 and blk == HB - 1 else None,
                            after=[("hidden", 2 * n + 1), At(setup, "pad2", 0), At(setup, "pad3", 0)] + earlier("convT", n, 1))
            work.do("vector", lambda e: e.tensor_scalar(convT[:, r, :], conv_ps[:, 0:G], bias2[:, cp:cp + 1], None,
                                                        ALU.add),
                    done=("convT", n), after=[("conv", n), At(setup, "small", 0)] + earlier("back", n, 2))

        def to_tokens(n):
            l, cp = steps[n]
            r = n % 2
            bank = back_ps[r]
            for mt in range(MT):
                work.do("tensor", lambda e, mt=mt: e.transpose(bank[:, mt, :], convT[:, r, mt * P:(mt + 1) * P],
                                                               identity[:, :]),
                        done=("back", n) if mt == MT - 1 else None,
                        after=[("convT", n)] + earlier("y", n, 2))
            for mt in range(MT):
                ins = bank[:, mt, :].rearrange("p (j s c) -> p j s c", j=4, s=S)
                res = xw[l][:, mt, 2:2 + S, 32 * cp:32 * cp + 32].rearrange("p s (j c) -> p j s c", j=4)
                out = y[l][:, mt * S:(mt + 1) * S, 32 * cp:32 * cp + 32].rearrange("p s (j c) -> p j s c", j=4)
                work.do("vector", lambda e, i=ins, q=res, o=out: e.tensor_tensor(o, i, q, ALU.add),
                        done=("y", n) if mt == MT - 1 else None,
                        after=[("back", n), Prev(("ln", l))])
            if cp == CP - 1:
                work.event[("x_read", l)] = work.event[("y", n)]
                work.event[("x_sent", l)] = work.event[("xr", n)]

        def finish(l):
            layernorm(work, l, [y[l][:, t, :] for t in range(TILES)], [h[l][:, t, :] for t in range(TILES)],
                      stats[:, l], moments[:, l], var_eps[:, l], rstd[:, l], minus_half, 1e-12,
                      gain[:, :], shift[:, :], ready=[("y", (l + 1) * CP - 1)], free=[Prev(("h0", l))],
                      done=("ln", l), first=[At(setup, "small", 0), At(setup, "half", 0)])

            def store(e):
                b = reg[e] * LANES + l
                return e.dma_start(h0[bass.ds(b, 1), :, :].rearrange("a p f -> (a p) f"),
                                   h[l][:, :, :].rearrange("p t c -> p (t c)"))
            work.do("sync", store, dma=("h0", l), after=[("ln", l)])

        reg = {}
        for n in range(n_steps + 3):
            if n < n_steps:
                to_channels(n)
            if 0 <= n - 1 < n_steps:
                conv1(n - 1)
            if 0 <= n - 2 < n_steps:
                conv2(n - 2)
            if 0 <= n - 3 < n_steps:
                to_tokens(n - 3)
                if (n - 3) % CP == CP - 1:
                    finish((n - 3) // CP)
        stores, work.queue["sync"] = work.queue["sync"], []
        turns, first_loads = [], []
        for l in range(LANES):
            load(l, reg)
            loads, work.queue["sync"] = work.queue["sync"], []
            first_loads += loads
            turns += [(loads, 1), ([stores[l]], 0)]
        work.queue["sync"] = first_loads + stores

        def transfers(eng):
            reg[eng] = 0
            work.emit("sync", eng, 0, ops=first_loads)
            with eng.Fori(0, B // LANES - 1) as i:
                for ops, lead in turns:
                    reg[eng] = i + lead
                    work.emit("sync", eng, i + lead, ops=ops)
            reg[eng] = B // LANES - 1
            work.emit("sync", eng, B // LANES - 1, ops=stores)

        run_loop(nc, setup, work, B // LANES, reg, waits=[("h0", l) for l in range(LANES)], sync_loop=transfers)


def attention_phase(nc, h_in, h_out, T, H, wqkv, rows, bq, bk, rope, tables):
    B = h_in.shape[0]
    L = wqkv.shape[0] - 1
    TILES = T // P
    DUOS = TILES // 2
    CB = H // P
    NH = 16
    HD = H // NH
    HB = P // HD
    LANES = 2
    TQ = 512
    QH = T // TQ
    BV, GAIN, SHIFT = range(3)

    ROWS = 3
    HT = TILES // QH

    ctx = ExitStack()
    with ctx:
        sb = lambda n, s, d=F32: ctx.enter_context(nc.sbuf_tensor(n, s, d))
        pb = lambda n, s: ctx.enter_context(nc.psum_tensor(n, s, F32))

        w_raw = sb("w_raw", [P, CB, 2 * H])
        wv = sb("wv", [P, CB, H])
        w_hi = sb("w_hi", [P, CB, 2 * H], F32R)
        w_lo = sb("w_lo", [P, CB, 2 * H], F32R)
        vec = sb("vec", [P, L * ROWS * H])
        bqs = sb("bqs", [P, L * CB])
        bks = sb("bks", [P, L * CB])
        cos_k = sb("cos_k", [P, TILES, H])
        sin_k = sb("sin_k", [P, TILES, H])
        cos_q = sb("cos_q", [P, CB, T])
        sin_q = sb("sin_q", [P, CB, T])
        identity = sb("identityB", [P, P])
        rot = sb("rot", [P, P])
        kv_mask = sb("kv_mask", [P, P])
        head_mask = sb("head_mask", [P, HB])
        ones = sb("onesB", [P, P])
        minus_half = sb("minus_halfB", [P, TILES])

        h = [sb(f"hB{s}", [P, TILES, H + 1]) for s in range(LANES)]
        y = sb("yB", [P, TILES, H])
        hT_hi = sb("hT_hi", [P, CB, T], F32R)
        hT_lo = sb("hT_lo", [P, CB, T], F32R)
        gkT = sb("gkT", [P, CB, T])
        k_sums = sb("k_sums", [P, QH, CB])
        km_sum = sb("km_sum", [P, CB])
        offset = sb("offset", [P, TILES])
        kc = sb("kc", [P, 2, 2 * H])
        ks = sb("ks", [P, 2, 2 * H])
        kr = sb("kr", [P, 2, 2 * H])
        gT = [sb(f"gT{s}", [P, CB, T]) for s in range(LANES)]
        qc = [sb(f"qc{s}", [P, CB, T]) for s in range(LANES)]
        qs = [sb(f"qs{s}", [P, CB, T]) for s in range(LANES)]
        G = sb("G", [P, CB, H + 1])
        GT = sb("GT", [P, CB, H])
        kv_raw = sb("kv_raw", [P, CB, P])
        kv = sb("kv", [P, LANES, CB, P])
        kv_rot = sb("kv_rot", [P, LANES, CB, P])
        km = sb("km", [P, CB])
        kmb = sb("kmb", [P, LANES, CB, HB])
        c21 = sb("c21", [P, CB, HB])
        cst = sb("cst", [P, NH])
        den = sb("den", [P, TILES, NH])
        z = sb("z", [P, LANES, TILES, NH])
        stats = sb("statsB", [P, TILES, 6])
        moments = sb("momentsB", [P, TILES, 2])
        var_eps = sb("var_epsB", [P, TILES])
        rstd = sb("rstdB", [P, TILES])

        banks = Banks([pb(f"bank{i}", [P, 512]) for i in range(5)])
        g_ps = [pb(f"g_ps{i}", [P, 512]) for i in range(CB)]
        m_ps = pb("m_ps", [P, 512])

        setup = Stage(nc, ctx, "attset")
        pair = Stage(nc, ctx, "attpair")
        lay = Stage(nc, ctx, "att")
        k_bank = {}
        reg = {}

        two = lambda a: a.unsqueeze(1).broadcast_to([P, 2, a.shape[-1]])

        for dst, src in ((identity, tables["eye"]), (bqs, bq), (bks, bk)):
            setup.do("scalar", lambda e, d=dst, s=src: e.dma_start(d[:, :], s), dma="first")
        setup.do("scalar", lambda e: e.activation(w_hi[:, :, :], w_raw[:, :, :], ACT.Copy), done="w_hi", after=["w0"])
        for name, dst, src in (("cos_k", cos_k, rope["cos_k"]), ("sin_k", sin_k, rope["sin_k"]),
                               ("cos_q", cos_q, rope["cos_q"]), ("sin_q", sin_q, rope["sin_q"])):
            setup.do("scalar", lambda e, d=dst, s=src: e.dma_start(d[:, :, :].rearrange("p a b -> p (a b)"), s), dma=name)
        for dst, src in ((rot, tables["rot"]), (kv_mask, tables["kv_mask"]), (head_mask, tables["head_mask"])):
            setup.do("scalar", lambda e, d=dst, s=src: e.dma_start(d[:, :], s), dma="consts")
        setup.do("scalar", lambda e: e.dma_start(vec[:, :], rows.partition_broadcast(P)), dma="consts")
        w3 = wqkv.rearrange("l p (c n) -> l p c n", c=CB)
        setup.do("sync", lambda e: e.dma_start(w_raw[:, :, :], w3[0, :, :, 0:2 * H]), dma="w0")
        setup.do("sync", lambda e: e.dma_start(wv[:, :, :], w3[0, :, :, 2 * H:3 * H]), dma="wv0")
        setup.do("gpsimd", lambda e: e.memset(minus_half[:, :], -0.5), done="half")
        setup.do("gpsimd", lambda e: e.memset(ones[:, :], 1.0), done="ones")
        for s in range(LANES):
            setup.do("gpsimd", lambda e, s=s: e.memset(h[s][:, :, H:H + 1], 1.0), done=("ones", s))
        setup.do("vector", lambda e: e.tensor_tensor(w_lo[:, :, :], w_raw[:, :, :], w_hi[:, :, :].bitcast(F32),
                                                     ALU.subtract), done="w_lo", after=["w_hi"])
        first, consts = [At(setup, "first", 0)], [At(setup, "consts", 0)]
        k_tables = [At(setup, "cos_k", 0), At(setup, "sin_k", 0)]
        q_tables = [At(setup, "cos_q", 0), At(setup, "sin_q", 0)]
        w_now = [Prev("w_next"), At(setup, "w_lo", 0)]
        the_ones = [At(setup, "ones", 0)]

        def row(which, at=0, n=H):
            return lambda e: vec[:, bass.ds(reg[e][1] * (ROWS * H) + (which * H + at), n)]

        batch = lambda e, h, s: h[bass.ds(reg[e][0] * LANES + s, 1)].rearrange("a p (t c) -> (a p) t c", c=H)
        for s in range(LANES):
            def load(e, s=s):
                return e.dma_start(h[s][:, :, 0:H], batch(e, h_in, s))
            pair.do("sync", load, dma=("h", s), after=[
                Prev(("sent", s))] + ([] if s else [At(lay, ("hT", 0, QH - 1, CB - 1), "layer before")]))

        def other(kind, s, *rest):
            return (kind, 0, *rest) if s else Prev((kind, 1, *rest))

        def split_h(s, half, stage=None):
            tok = slice(half * TQ, (half + 1) * TQ)
            stage = stage or lay
            for cb in range(CB):
                if stage is pair:
                    b = half * CB + cb
                    bank, free = banks.tensors[b], LastUse(lay, banks, b, "layer before")
                    ready, used = [("h", s)], At(lay, ("q", 1, CB * QH - 1), "layer before")
                else:
                    bank, free = banks.take(("hT_lo", s, half, cb))
                    ready = [At(pair, ("h", s), "pair")] + [Prev(("ln", s, half)) if s else ("ln", s, half)]
                    used = ("q", 1 - s, CB * QH - 1)
                for t in range(HT):
                    stage.do("tensor", lambda e, cb=cb, t=t, bank=bank: e.transpose(
                        bank[:, t * P:(t + 1) * P], h[s][:, HT * half + t, cb * P:(cb + 1) * P], identity[:, :]),
                        done=("hT", s, half, cb) if t == HT - 1 else None, after=[free] + ready + first)
                stage.do("scalar", lambda e, cb=cb, bank=bank: e.activation(hT_hi[:, cb, tok], bank[:, :], ACT.Copy),
                         done=("hT_hi", s, half, cb), after=[("hT", s, half, cb), used])
                stage.do("vector", lambda e, cb=cb, bank=bank: e.tensor_tensor(
                    hT_lo[:, cb, tok], bank[:, :], hT_hi[:, cb, tok].bitcast(F32), ALU.subtract),
                    done=("hT_lo", s, half, cb), after=[("hT_hi", s, half, cb)])

        def project(s, half, which, col, bias, dst, used, sums=None):
            tok = slice(half * TQ, (half + 1) * TQ)
            for db in range(CB):
                k = half * CB + db
                c = slice(col + db * P, col + (db + 1) * P)
                bank, free = banks.take(("g" + which, s, k))
                parts = [(bank[:, :], (w_hi[:, cb, c], w_lo[:, cb, c]), (hT_hi[:, cb, tok], hT_lo[:, cb, tok]),
                          cb == 0, cb == CB - 1) for cb in range(CB)]
                lay.do("tensor", mm3(parts), done=(which, s, k), after=[free, *w_now] + (
                    [("hT_lo", s, half, CB - 1)] if s else
                    [Prev(("hT_lo", s, half, CB - 1)), At(pair, ("hT_lo", s, QH - 1, CB - 1), "pair")]))

                def make(e, db=db, bank=bank):
                    kw = {} if sums is None else {"accum_out": sums[:, half, db:db + 1]}
                    return e.activation(dst[:, db, tok], bank[:, :], ACT.Gelu,
                                        bias=bias[:, bass.ds(reg[e][1] * CB + db, 1)], **kw)
                lay.do("scalar", make, done=("g" + which, s, k), after=[(which, s, k)] + used + first, apart=True)

        def keys(s, half):
            project(s, half, "k", H, bks, gkT, [other("kt", s, DUOS - 1)] + ([other("km", s)]), k_sums)

        def queries(s, half):
            project(s, half, "q", 0, bqs, gT[s], [Prev(("out", s, DUOS - 1))])

        def rotate_q(s, half):
            tok = slice(half * TQ, (half + 1) * TQ)
            for db in range(CB):
                k = half * CB + db
                for nm, dst, tab in (("qc", qc[s], cos_q), ("qs", qs[s], sin_q)):
                    lay.do("vector", lambda e, dst=dst, tab=tab, db=db: e.scalar_tensor_tensor(
                        dst[:, db, tok], gT[s][:, db, tok], 0.21, tab[:, db, tok], ALU.add, ALU.mult),
                        done=(nm, s, k), after=[("gq", s, k), Prev(("out", s, DUOS - 1))] + q_tables)

        def k_rows(s, u):
            bank, free = banks.take(("ks", s, u))
            k_bank[s, u] = bank
            for t in range(2):
                for db in range(CB):
                    lay.do("tensor", lambda e, t=t, db=db: e.transpose(
                        bank[:, t * H + db * P:t * H + (db + 1) * P], gkT[:, db, (2 * u + t) * P:(2 * u + t + 1) * P],
                        identity[:, :]), done=("kt", s, u) if t == 1 and db == CB - 1 else None,
                        after=[("gk", s, (u // 2) * CB + CB - 1), free])

        def rotate_k(s, u):
            bank, r = k_bank[s, u], u % 2
            ring = lambda kind: (kind, s, u - 2) if u >= 2 else other(kind, s, DUOS - 2 + u)
            flat = lambda t: t[:, 2 * u:2 * u + 2, :].rearrange("p t n -> p (t n)")
            lay.do("vector", lambda e: e.scalar_tensor_tensor(kc[:, r, :], bank[:, :], 0.21, flat(cos_k), ALU.add, ALU.mult),
                   done=("kc", s, u), after=[("kt", s, u), ring("kr")] + k_tables)
            pairs = lambda a: a.rearrange("p (i two) -> p i two", two=2)
            for k in range(2):
                lay.do("vector", lambda e, k=k: e.scalar_tensor_tensor(
                    pairs(ks[:, r, :])[:, :, k], pairs(bank[:, :])[:, :, 1 - k], 0.21, pairs(flat(sin_k))[:, :, k],
                    ALU.add, ALU.mult), done=("ks", s, u) if k else None)
            lay.do("gpsimd", lambda e: e.tensor_tensor(kr[:, r, :], kc[:, r, :], ks[:, r, :], ALU.add),
                   done=("kr", s, u), after=[("ks", s, u), ring("G")])

        def gram(s, u):
            r = u % 2
            for t in range(2):
                for db in range(CB):
                    lay.do("tensor", mm(g_ps[db][:, 0:H + 1], kr[:, r, t * H + db * P:t * H + (db + 1) * P],
                                        h[s][:, 2 * u + t, :], u == 0 and t == 0, u == DUOS - 1 and t == 1),
                           done=("G", s, u) if t == 1 and db == CB - 1 else None,
                           after=[("kr", s, u), At(setup, ("ones", s), 0), other("G_out", s)])

        def k_mean(s):
            lay.do("vector", lambda e: e.tensor_tensor(km_sum[:, :], k_sums[:, 0, :], k_sums[:, 1, :], ALU.add),
                   done=("km_sum", s), after=[("gk", s, CB * QH - 1)])
            lay.do("vector", lambda e: e.tensor_scalar(km[:, :], km_sum[:, :], 1.0 / T, 0.21, ALU.mult, ALU.add),
                   done=("km", s), after=[("km_sum", s)])
            for db in range(CB):
                lay.do("vector", lambda e, db=db: e.tensor_scalar(kmb[:, s, db, :], head_mask[:, :], km[:, db:db + 1], None,
                                                                  ALU.mult), done=("kmb", s) if db == CB - 1 else None,
                       after=[("km", s), Prev(("D", s))] + consts)
            lay.do("vector", lambda e: e.tensor_scalar(c21[:, :, :], kmb[:, s, :, :], 0.21, 1e-6 / P, ALU.mult, ALU.add),
                   done=("c21", s), after=[("kmb", s), other("cst_ps", s)])

        def denominators(s):
            bank, free = banks.take(("cst", s))
            for db in range(CB):
                lay.do("tensor", mm(bank[:, TILES * NH + db * HB:TILES * NH + (db + 1) * HB], ones[:, :], c21[:, db, :]),
                       done=("cst_ps", s) if db == CB - 1 else None, after=[("c21", s), free])
            for t in range(TILES):
                for db in range(CB):
                    lay.do("tensor", mm(bank[:, t * NH + db * HB:t * NH + (db + 1) * HB],
                                        gT[s][:, db, t * P:(t + 1) * P], kmb[:, s, db, :]),
                           done=("D", s) if t == TILES - 1 and db == CB - 1 else None,
                           after=[("gq", s, CB * QH - 1), ("kmb", s)])
            dview = bank[:, 0:TILES * NH].rearrange("p (t n) -> p t n", t=TILES)
            add = cst[:, :].unsqueeze(1).broadcast_to([P, TILES, NH])
            lay.do("vector", lambda e: e.tensor_copy(cst[:, :], bank[:, TILES * NH:(TILES + 1) * NH]), done=("cst0", s),
                   after=[("D", s)])
            lay.do("vector", lambda e: e.tensor_tensor(den[:, :, :], dview, add, ALU.add), done=("cst", s), after=[("cst0", s)])
            lay.do("vector", lambda e: e.reciprocal(z[:, s, :, :], den[:, :, :]), done=("z", s), after=[("cst", s)])

        def gram_rows(s):
            for db in range(CB):
                lay.do("scalar", lambda e, db=db: e.activation(G[:, db, :], g_ps[db][:, 0:H + 1], ACT.Copy),
                       done=("G_out", s) if db == CB - 1 else None, after=[("G", s, DUOS - 1), other("kv_raw", s)])
            for db in range(CB):
                for cb in range(CB):
                    lay.do("tensor", lambda e, db=db, cb=cb: e.transpose(
                        m_ps[:, cb * H + db * P:cb * H + (db + 1) * P], G[:, db, cb * P:(cb + 1) * P], identity[:, :]),
                        done=("GT_ps", s) if db == CB - 1 and cb == CB - 1 else None,
                        after=[("G_out", s), other("kv_rot", s)])
            lay.do("scalar", lambda e: e.activation(GT[:, :, :].rearrange("p c n -> p (c n)"), m_ps[:, :], ACT.Copy),
                   done=("GT", s), after=[("GT_ps", s), other("kv_ps", s)])

        def key_value(s):
            for db in range(CB):
                for cb in range(CB):
                    lay.do("tensor", mm(m_ps[:, db * P:(db + 1) * P], GT[:, cb, db * P:(db + 1) * P],
                                        wv[:, cb, db * P:(db + 1) * P], cb == 0, cb == CB - 1),
                           done=("kv_ps", s) if db == CB - 1 and cb == CB - 1 else None, after=[("GT", s), Prev("wv"), At(setup, "wv0", 0)])
            for db in range(CB):
                lay.do("vector", lambda e, db=db: e.scalar_tensor_tensor(
                    kv_raw[:, db, :], row(BV, db * P, P)(e), G[:, db, H:H + 1], m_ps[:, db * P:(db + 1) * P],
                    ALU.mult, ALU.add), done=("kv_raw", s) if db == CB - 1 else None, after=[("kv_ps", s)] + consts)
            mask = kv_mask[:, :].unsqueeze(1).broadcast_to([P, CB, P])
            lay.do("vector", lambda e: e.tensor_tensor(kv[:, s, :, :], kv_raw[:, :, :], mask, ALU.mult),
                   done=("kv", s), after=[("kv_raw", s), Prev(("out", s, DUOS - 1))])

        def turned_kv(s):
            lay.do("tensor", mm(m_ps[:, 0:CB * P], rot[:, :], kv[:, s, :, :].rearrange("p c n -> p (c n)")),
                   done=("rot_ps", s), after=[("kv", s)] + consts)
            lay.do("scalar", lambda e: e.activation(kv_rot[:, s, :, :].rearrange("p c n -> p (c n)"), m_ps[:, 0:CB * P],
                                                    ACT.Copy),
                   done=("kv_rot", s), after=[("rot_ps", s), Prev(("out", s, DUOS - 1))])

        def outputs(s, u):
            bank, free = banks.take(("att", s, u))
            for t in range(2):
                tok = slice((2 * u + t) * P, (2 * u + t + 1) * P)
                for db in range(CB):
                    o = bank[:, t * H + db * P:t * H + (db + 1) * P]
                    lay.do("tensor", mm(o, qc[s][:, db, tok], kv[:, s, db, :], True, False), after=[
                        ("qs", s, CB * QH - 1), ("kv_rot", s), free])
                    lay.do("tensor", mm(o, qs[s][:, db, tok], kv_rot[:, s, db, :], False, True),
                           done=("out", s, u) if t == 1 and db == CB - 1 else None)
            yd = y[:, 2 * u:2 * u + 2, :]
            zb = z[:, s, 2 * u:2 * u + 2, :].rearrange("p t n -> p (t n)").unsqueeze(2).broadcast_to([P, 2 * NH, HD])
            lay.do("vector", lambda e: e.tensor_tensor(
                yd.rearrange("p t (n d) -> p (t n) d", d=HD), bank[:, :].rearrange("p (n d) -> p n d", d=HD), zb, ALU.mult),
                done=("att", s, u), after=[("out", s, u), ("z", s), other("ln", s, u // 2)])
            lay.do("gpsimd", lambda e: e.tensor_tensor(yd, yd, h[s][:, 2 * u:2 * u + 2, 0:H], ALU.add),
                   done=("y", s, u), after=[("att", s, u)])

        def moments_of(s, half):
            sl = slice(HT * half, HT * (half + 1))
            for t in range(HT * half, HT * (half + 1)):
                lay.do("vector", lambda e, t=t: e.bn_stats(stats[:, t, :], y[:, t, :]), done=("stats", s, t),
                       after=[("y", s, t // 2)])
            for t in range(HT * half, HT * (half + 1)):
                lay.do("vector", lambda e, t=t: e.bn_aggr(moments[:, t, :], stats[:, t, :]), done=("mom", s, t),
                       after=[("stats", s, t)], apart=True)
            lay.do("vector", lambda e: e.tensor_scalar(var_eps[:, sl], moments[:, sl, 1], 1e-12, None, ALU.add),
                   done=("var", s, half), after=[("mom", s, HT * (half + 1) - 1)])
            lay.do("gpsimd", lambda e: e.tensor_tensor(rstd[:, sl], var_eps[:, sl], minus_half[:, 0:HT], ALU.pow),
                   done=("rstd", s, half), after=[("var", s, half), At(setup, "half", 0)])

        def normalise(s, half):
            sl = slice(HT * half, HT * (half + 1))
            lay.do("vector", lambda e: e.scalar_tensor_tensor(
                offset[:, sl], moments[:, sl, 0], -1.0, rstd[:, sl], ALU.mult, ALU.mult), done=("offset", s, half),
                after=[("rstd", s, half)])
            for t in range(HT * half, HT * (half + 1)):
                lay.do("scalar", lambda e, t=t: e.activation(y[:, t, :], y[:, t, :], ACT.Identity,
                                                             bias=offset[:, t:t + 1], scale=rstd[:, t:t + 1]),
                       done=("unit", s, t), after=[("offset", s, half)])

        def affine(s, half):
            for u in range(2 * half, 2 * half + 2):
                yd = y[:, 2 * u:2 * u + 2, :]
                lay.do("vector", lambda e, yd=yd: e.tensor_tensor(yd, yd, two(row(GAIN)(e)), ALU.mult),
                       done=("gained", s, u), after=[("unit", s, 2 * u + 1)])
                lay.do("gpsimd", lambda e, yd=yd, u=u: e.tensor_tensor(h[s][:, 2 * u:2 * u + 2, 0:H], yd, two(row(SHIFT)(e)),
                                                                      ALU.add),
                       done=("ln", s, half) if u % 2 else ("ln_part", s, half), after=[("gained", s, u), ("G", s, DUOS - 1)])

        def fetch_weights():
            lay.do("sync", lambda e: e.dma_start(w_raw[:, :, :], next_w(e)[:, :, 0:2 * H]), dma="w_raw", after=w_now)

        def split_weights():
            lay.do("scalar", lambda e: e.activation(w_hi[:, :, :], w_raw[:, :, :], ACT.Copy), done="w_next_hi",
                   after=["w_raw", ("q", 1, CB * QH - 1)])
            lay.do("vector", lambda e: e.tensor_tensor(w_lo[:, :, :], w_raw[:, :, :], w_hi[:, :, :].bitcast(F32),
                                                       ALU.subtract), done="w_next", after=["w_next_hi"])

        def fetch_wv():
            lay.do("sync", lambda e: e.dma_start(wv[:, :, :], next_w(e)[:, :, 2 * H:3 * H]), dma="wv",
                   after=[("kv_ps", 1)])

        next_w = lambda e: w3[bass.ds(reg[e][1] + 1, 1)].rearrange("a p c n -> (a p) c n")

        fetch_weights()
        keys(0, 0)
        queries(0, 0)
        keys(0, 1)
        k_rows(0, 0)
        k_rows(0, 1)
        rotate_k(0, 0)
        rotate_k(0, 1)
        rotate_q(0, 0)
        queries(0, 1)
        gram(0, 0)
        k_rows(0, 2)
        rotate_k(0, 2)
        gram(0, 1)
        k_rows(0, 3)
        rotate_k(0, 3)
        k_mean(0)
        split_h(1, 0)
        split_h(1, 1)
        gram(0, 2)
        gram(0, 3)
        rotate_q(0, 1)
        keys(1, 0)
        gram_rows(0)
        queries(1, 0)
        key_value(0)
        keys(1, 1)
        turned_kv(0)
        denominators(0)
        k_rows(1, 0)
        k_rows(1, 1)
        rotate_k(1, 0)
        rotate_k(1, 1)
        outputs(0, 0)
        outputs(0, 1)
        rotate_q(1, 0)
        moments_of(0, 0)
        queries(1, 1)
        split_weights()
        normalise(0, 0)
        gram(1, 0)
        k_rows(1, 2)
        rotate_k(1, 2)
        gram(1, 1)
        k_rows(1, 3)
        rotate_k(1, 3)
        affine(0, 0)
        k_mean(1)
        outputs(0, 2)
        gram(1, 2)
        gram(1, 3)
        gram_rows(1)
        outputs(0, 3)
        rotate_q(1, 1)
        key_value(1)
        fetch_wv()
        denominators(1)
        moments_of(0, 1)
        turned_kv(1)
        normalise(0, 1)
        outputs(1, 0)
        affine(0, 1)
        outputs(1, 1)
        moments_of(1, 0)
        outputs(1, 2)
        outputs(1, 3)
        split_h(0, 0)
        split_h(0, 1)
        normalise(1, 0)
        affine(1, 0)
        moments_of(1, 1)
        normalise(1, 1)
        affine(1, 1)

        for half in range(QH):
            split_h(0, half, pair)
        before_layers = {e: len(pair.queue[e]) for e in ENGINES}

        for s in range(LANES):
            def store(e, s=s):
                return e.dma_start(batch(e, h_out, s), h[s][:, :, 0:H])
            pair.do("scalar" if s else "sync", store, dma=("sent", s), after=[At(lay, ("ln", s, 1), "last layer")])

        with nc.Block() as block:
            def body(name):
                def program(eng):
                    setup.credit(name, eng)
                    setup.emit(name, eng, 0)
                    pair.credit(name, eng)
                    lay.credit(name, eng)
                    with eng.Fori(0, B // LANES) as i:
                        where = {"pair": i, "last layer": i * L + (L - 1), "layer before": i * L - 1}
                        reg[eng] = (i, None)
                        first = pair.queue[name][:before_layers[name]]
                        pair.emit(name, eng, i, where, first)
                        if lay.queue[name]:
                            with eng.Fori(0, L) as l:
                                reg[eng] = (i, l)
                                lay.emit(name, eng, i * L + l, {"pair": i})
                        reg[eng] = (i, None)
                        pair.emit(name, eng, i, where, pair.queue[name][before_layers[name]:])
                    if name == "sync":
                        for s in range(LANES):
                            sem, per, const = pair.value(("sent", s), 0)
                            eng.wait_ge(sem, (B // LANES - 1) * per + const)
                return program
            for name in ENGINES:
                getattr_block(block, name)(body(name))


def ffn_phase(nc, x, h_in, out, w1, b1, w2, rows2, comp, eye, tri):
    B, T, H = x.shape
    F = w1.shape[1] // (H // P)
    CB, FB = H // P, F // P
    LANES = 2
    TOK = T // LANES
    TILES = TOK // P
    GEL = 5
    B2, GAIN, SHIFT = range(3)

    ctx = ExitStack()
    with ctx:
        sb = lambda n, s, d=F32: ctx.enter_context(nc.sbuf_tensor(n, s, d))
        split = lambda n, s: (sb(n + "_hi", s, F32R), sb(n + "_lo", s, F32R))

        up = [split("up0", [P, CB, F]), split("up1", [P, CB, F])]
        down = [split("down0", [P, FB, H]), split("down1", [P, FB, H])]
        identity = sb("identityC", [P, P])
        compose_phase(nc, up[1], down[1], comp, identity, eye, tri)

        pb = lambda n, s: ctx.enter_context(nc.psum_tensor(n, s, F32))
        b1s = sb("b1s", [P, FB])
        vec = sb("vecC", [P, 3 * H])
        minus_half = sb("minus_halfC", [P, TILES])
        hs = [sb(f"hC{s}", [P, TILES, H]) for s in range(LANES)]
        x_both = sb("xC", [P, LANES, TILES, H])
        xs = [x_both[:, s, :, :] for s in range(LANES)]
        y = [sb(f"yC{s}", [P, TILES, H]) for s in range(LANES)]
        x1 = [sb(f"x1{s}", [P, TILES, H]) for s in range(LANES)]
        aT = [split(f"aT{s}", [P, CB, TOK]) for s in range(LANES)]
        act = [split(f"act{s}", [P, FB, TOK]) for s in range(LANES)]
        gel = sb("gel", [P, GEL, TOK])
        zero = sb("zeroC", [P, 512], F32R)
        stats = sb("statsC", [P, LANES, TILES, 6])
        moments = sb("momentsC", [P, LANES, TILES, 2])
        var_eps = sb("var_epsC", [P, LANES, TILES])
        rstd = sb("rstdC", [P, LANES, TILES])
        turn = [pb(f"turn{i}", [P, TOK]) for i in range(CB)]
        banks = Banks([pb(f"bankC{i}", [P, 512]) for i in range(6)])

        setup = Stage(nc, ctx, "ffnset")
        ahead = Stage(nc, ctx, "ffnahead")
        work = Stage(nc, ctx, "ffn")
        reg = {}

        setup.do("scalar", lambda e: e.dma_start(b1s[:, :], b1), dma="consts")
        setup.do("scalar", lambda e: e.dma_start(vec[:, :], rows2.partition_broadcast(P)), dma="consts")
        setup.do("gpsimd", lambda e: e.memset(minus_half[:, :], -0.5), done="half")
        setup.do("gpsimd", lambda e: e.memset(zero[:, :].bitcast(F32), 0.0), done="zero")
        flat = lambda t: t[:, :, :].rearrange("p a b -> p (a b)")
        for n, (src, (hi, lo)) in enumerate(((w1, up[0]), (w2, down[0]))):
            w_in = (gel[:, :, :].rearrange("p a b -> p (a b)"), x_both[:, :, :, :].rearrange("p s a b -> p (s a b)"))[n]
            w_in = w_in[:, 0:src.shape[1]]
            setup.do("sync", lambda e, src=src, w=w_in: e.dma_start(w, src), dma=("w", n))
            setup.do("scalar", lambda e, d=flat(hi), w=w_in: e.activation(d, w, ACT.Copy), done=("w_hi", n), after=[("w", n)])
            setup.do("vector", lambda e, d=flat(lo), g=flat(hi), w=w_in: e.tensor_tensor(d, w, g.bitcast(F32), ALU.subtract),
                     done=("w_lo", n), after=[("w_hi", n)])
        weights = [At(setup, ("w_lo", 1), 0)]
        consts = [At(setup, "consts", 0), At(setup, "half", 0)]
        vrow = lambda k: vec[:, k * H:(k + 1) * H]

        h_rows = h_in.rearrange("b p (m f) -> b m p f", m=LANES)
        x_rows = x.rearrange("b (m p s) c -> b m p (s c)", m=LANES, p=P)
        o_rows = out.rearrange("b (m p s) c -> b m p (s c)", m=LANES, p=P)
        pick = lambda e, a, s: a[bass.ds(reg[e], 1), s].rearrange("a p f -> (a p) f")
        now = lambda name: At(ahead, name, "this batch")
        before = lambda name: At(work, name, "batch before")
        for s in range(LANES):
            ahead.do("sync", lambda e, s=s: e.dma_start(flat(hs[s]), pick(e, h_rows, s)), dma=("h", s),
                     after=[before(("y", 0, s, TILES // 2 - 1))])
        for s in range(LANES):
            ahead.do("sync", lambda e, s=s: e.dma_start(flat(xs[s]), pick(e, x_rows, s)), dma=("x", s),
                     after=[before(("sum", s))] + weights)

        turn_order = [(0, 0), (0, 1), (1, 0), (1, 1)]

        def transposes(k, s):
            src = (hs, x1)[k][s]
            stage = ahead if (k, s) == (0, 0) else work
            ready = [("h", 0)] if stage is ahead else [now(("h", s))] if k == 0 else [("ln1", s)]
            if stage is ahead:
                used = [before(("up", 1, 0, FB - 1))]
            else:
                used = [("up", 0, s, FB - 1)] if k else [Prev(("up", 1, s, FB - 1))]
            hi, lo = aT[s]
            for cb in range(CB):
                if stage is ahead:
                    free = before(("aT_lo", 1, 1, cb))
                elif (k, s) == (0, 1):
                    free = now(("aT_lo", 0, 0, cb))
                else:
                    free = ("aT_lo", *turn_order[turn_order.index((k, s)) - 1], cb)
                for t in range(TILES):
                    stage.do("tensor", lambda e, t=t, cb=cb: e.transpose(
                        turn[cb][:, t * P:(t + 1) * P], src[:, t, cb * P:(cb + 1) * P], identity[:, :]),
                        done=("aT_ps", k, s, cb) if t == TILES - 1 else None, after=ready + [free])
                stage.do("scalar", lambda e, cb=cb: e.activation(hi[:, cb, :], turn[cb][:, :], ACT.Copy),
                         done=("aT_hi", k, s, cb), after=[("aT_ps", k, s, cb)] + used)
                stage.do("vector", lambda e, cb=cb: e.tensor_tensor(
                    lo[:, cb, :], turn[cb][:, :], hi[:, cb, :].bitcast(F32), ALU.subtract),
                    done=("aT_lo", k, s, cb), after=[("aT_hi", k, s, cb)])

        def add_bias(s):
            b2 = vrow(B2).unsqueeze(1).broadcast_to([P, TILES, H])
            turned = now(("aT_ps", 0, 0, CB - 1)) if s == 0 else ("aT_ps", 0, s, CB - 1)
            work.do("gpsimd", lambda e: e.tensor_tensor(hs[s][:, :, :], hs[s][:, :, :], b2, ALU.add),
                    done=("res", 0, s), after=[turned] + consts)

        gel_ring = Banks([gel[:, g, :] for g in range(GEL)])

        def up_product(k, s):
            hi, lo = aT[s]
            a_hi, a_lo = act[s]
            turned = now(("aT_lo", k, s, CB - 1)) if (k, s) == (0, 0) else ("aT_lo", k, s, CB - 1)

            def piece(fb):
                g, g_free = gel_ring.take(("act_lo", k, s, fb))
                bank, free = banks.take(("gelu", k, s, fb))
                f = slice(fb * P, (fb + 1) * P)
                parts = [(bank[:, :], (up[k][0][:, cb, f], up[k][1][:, cb, f]), (hi[:, cb, :], lo[:, cb, :]),
                          cb == 0, cb == CB - 1) for cb in range(CB)]
                work.do("tensor", mm3(parts), done=("up", k, s, fb), after=[turned, free] + weights)
                work.do("scalar", lambda e: e.activation(
                    g, bank[:, :], ACT.Gelu if k == 0 else ACT.Gelu_apprx_tanh,
                    bias=b1s[:, fb:fb + 1] if k == 0 else 0.0), done=("gelu", k, s, fb),
                    after=[("up", k, s, fb), g_free] + consts)
                used = [("down", 0, s, TILES // 2 - 1)] if k else [Prev(("down", 1, s, TILES // 2 - 1))]
                work.do("vector", lambda e: e.tensor_copy(a_hi[:, fb, :], g),
                        done=("act_hi", k, s, fb), after=[("gelu", k, s, fb)] + used + weights)
                work.do("vector", lambda e: e.tensor_tensor(
                    a_lo[:, fb, :], g, a_hi[:, fb, :].bitcast(F32), ALU.subtract),
                    done=("act_lo", k, s, fb), after=[("act_hi", k, s, fb)])
            return [lambda fb=fb: piece(fb) for fb in range(FB)]

        def down_product(k, s):
            a_hi, a_lo = act[s]
            add = (hs, x1)[k][s]
            pair = [banks.take(("y", k, s, u)) for u in range(TILES // 2)]
            for bank, free in pair:
                work.do("tensor", lambda e, bank=bank: e.matmul(bank[:, :], zero[:, 0:P], zero[:, :], start=True, stop=False),
                        after=[free, At(setup, "zero", 0)])
            for fb in range(FB):
                for u, (bank, free) in enumerate(pair):
                    last = fb == FB - 1
                    parts = [(bank[:, t * H:(t + 1) * H],
                              tuple(a[:, fb, (2 * u + t) * P:(2 * u + t + 1) * P] for a in (a_hi, a_lo)),
                              (down[k][0][:, fb, :], down[k][1][:, fb, :]), False, last and t == 1) for t in range(2)]
                    work.do("tensor", mm3(parts), done=("down", k, s, u) if last else None,
                            after=[("act_lo", k, s, fb)])
            for u, (bank, free) in enumerate(pair):
                two = lambda t, u=u: t[:, 2 * u:2 * u + 2, :].rearrange("p t c -> p (t c)")
                ready = [("res", 0, s)] if k == 0 else [("ln1", s)]
                used = [("ln1", s)] if k else [Prev(("out_sent", s)), Prev(("ln3", s))]
                work.do("vector", lambda e, bank=bank, two=two: e.tensor_tensor(
                    two(y[s]), bank[:, :], two(add), ALU.add), done=("y", k, s, u),
                    after=[("down", k, s, u)] + ready + used)

        def norms(k, s):
            tiles = lambda t: [t[s][:, i, :] for i in range(TILES)]
            st = (stats[:, s], moments[:, s], var_eps[:, s], rstd[:, s], minus_half)

            def plus_x():
                work.do("gpsimd", lambda e: e.tensor_tensor(y[s][:, :, :], y[s][:, :, :], xs[s][:, :, :], ALU.add),
                        done=("sum", s), after=[("ln0", s), now(("x", s))])

            if k == 0:
                return [*layernorm_pieces(work, ("first", s), tiles(y), tiles(y), *st, 1e-12, vrow(GAIN), vrow(SHIFT),
                                          ready=[("y", 0, s, TILES // 2 - 1)], free=[], done=("ln0", s), first=consts),
                        plus_x,
                        *layernorm_pieces(work, ("second", s), tiles(y), tiles(x1), *st, 1e-5, None, None,
                                          ready=[("sum", s)], free=[Prev(("y", 1, s, TILES // 2 - 1))], done=("ln1", s))]
            return layernorm_pieces(work, ("third", s), tiles(y), tiles(y), *st, 1e-5, None, None,
                                    ready=[("y", 1, s, TILES // 2 - 1)], free=[], done=("ln3", s))

        def together(products, layers, at):
            at = dict(zip(at, layers))
            for i, piece in enumerate(products):
                if i in at:
                    at[i]()
                piece()

        for piece in up_product(0, 0):
            piece()
        add_bias(0)
        transposes(0, 1)
        down_product(0, 0)
        add_bias(1)
        together(up_product(0, 1), norms(0, 0), (0, 1, 2, 4, 5))
        down_product(0, 1)
        transposes(1, 0)
        together(up_product(1, 0), norms(0, 1), (0, 1, 2, 4, 5))
        down_product(1, 0)
        transposes(1, 1)
        transposes(0, 0)
        mark = {e: len(work.queue[e]) for e in ENGINES}
        together(up_product(1, 1), norms(1, 0), (0, 1))
        down_product(1, 1)
        for piece in norms(1, 1):
            piece()
        for s in range(LANES):
            work.do("sync", lambda e, s=s: e.dma_start(pick(e, o_rows, s), flat(y[s])), dma=("out_sent", s),
                    after=[("ln3", s)])

        with nc.Block() as block:
            def body(name):
                def batch(eng, i, last=False):
                    reg[eng] = i
                    work.emit(name, eng, i, {"this batch": i}, work.queue[name][:mark[name]])
                    if not last:
                        reg[eng] = i + 1
                        ahead.emit(name, eng, i + 1, {"batch before": i})
                        reg[eng] = i
                    work.emit(name, eng, i, {"this batch": i}, work.queue[name][mark[name]:])

                def program(eng):
                    setup.credit(name, eng)
                    ahead.credit(name, eng)
                    work.credit(name, eng)
                    setup.emit(name, eng, 0)
                    reg[eng] = 0
                    ahead.emit(name, eng, 0, {"batch before": -1})
                    with eng.Fori(0, B - 1) as i:
                        batch(eng, i)
                    batch(eng, B - 1, last=True)
                    if name == "sync":
                        for s in range(LANES):
                            sem, per, const = work.value(("out_sent", s), 0)
                            eng.wait_ge(sem, (B - 1) * per + const)
                return program
            for name in ENGINES:
                getattr_block(block, name)(body(name))


def compose_phase(nc, up, down, comp, identity, eye, tri):
    logits, bases, R = comp["logits"], (("A1", "B1"), ("A2", "B2")), 64
    N = 64
    K = 32
    ctx = ExitStack()
    with ctx:
        sb = lambda n, s, d=F32: ctx.enter_context(nc.sbuf_tensor(n, s, d))
        pb = lambda n, s: ctx.enter_context(nc.psum_tensor(n, s, F32))
        row = sb("logit_row", [N, 2, N])
        col = sb("logit_col", [N, 2])
        before = sb("before", [N, N])
        index = sb("index", [N, 1 + K])
        more = sb("more", [N, 2, N])
        same = sb("same", [N, 2, N])
        rank2 = sb("rank2", [N, 2, 2])
        rank = sb("rank", [N, 2])
        top = sb("top", [N, 2])
        expo = sb("expo", [N, 2])
        chosen = sb("chosen", [N, 2])
        onesN = sb("onesN", [N, P])
        weight = sb("weight", [N, 2, P])
        place = sb("place", [N, 2, K])
        inv_sum = sb("inv_sum", [P, 2])
        total = sb("total", [P, 2])
        w_row = sb("w_row", [P, 2, K])
        w_col = sb("w_col", [P, 2, K // 2])
        picks_f = sb("picks_f", [1, 2 * K])
        picks = sb("picks", [1, 2 * K], I32)
        zero = sb("zero", [P, 512], F32R)
        A = sb("Abuf", [P, 2, 8, 2, R])
        Bm = sb("Bbuf", [P, 2, 1024])
        AT = (sb("AT_hi", [P, 2, 1024], F32R), sb("AT_lo", [P, 2, 1024], F32R))
        Bs = (sb("Bs_hi", [P, 2, 1024], F32R), sb("Bs_lo", [P, 2, 1024], F32R))
        acc = [pb(f"acc{i}", [P, 512]) for i in range(4)]
        t_ps = [pb(f"t_ps{i}", [P, 512]) for i in range(4)]

        pre = Stage(nc, ctx, "rank")
        pre.do("sync", lambda e: e.dma_start(row[:, :, :].rearrange("n a b -> n (a b)"), logits.partition_broadcast(N)), dma="in")
        pre.do("sync", lambda e: e.dma_start(col[:, :], comp["logit_col"]), dma="in")
        pre.do("sync", lambda e: e.dma_start(before[:, :], tri), dma="in")
        pre.do("sync", lambda e: e.dma_start(index[:, :], comp["index"]), dma="in")
        pre.do("sync", lambda e: e.dma_start(identity[:, :], eye), dma="in")
        pre.do("gpsimd", lambda e: e.memset(onesN[:, :], 1.0), done="ones")
        pre.do("gpsimd", lambda e: e.memset(zero[:, :].bitcast(F32), 0.0), done="zero")
        V = lambda make, done=None, after=(): pre.do("vector", make, done=done, after=after)
        for f in range(2):
            V(lambda e, f=f: e.tensor_scalar(more[:, f, :], row[:, f, :], col[:, f:f + 1], None, ALU.is_gt), ("more", f), ["in"])
            V(lambda e, f=f: e.scalar_tensor_tensor(same[:, f, :], row[:, f, :], col[:, f:f + 1], before[:, :],
                                                    ALU.is_equal, ALU.mult), ("same", f), [])
        X = mybir.AxisListType.X
        V(lambda e: e.tensor_tensor(more[:, :, :], more[:, :, :], same[:, :, :], ALU.add), "both", [("same", 1)])
        V(lambda e: e.tensor_reduce(rank[:, :], more[:, :, :], X, ALU.add), "rank", ["both"])
        V(lambda e: e.tensor_reduce(top[:, :], row[:, :, :], X, ALU.max), "top", [])
        V(lambda e: e.tensor_scalar(chosen[:, :], rank[:, :], float(K), None, ALU.is_lt), "chosen", ["rank"])
        V(lambda e: e.tensor_tensor(expo[:, :], col[:, :], top[:, :], ALU.subtract), "less_top", ["top"])
        pre.do("scalar", lambda e: e.activation(expo[:, :], expo[:, :], ACT.Exp), done="exp", after=["less_top"])
        V(lambda e: e.tensor_tensor(expo[:, :], expo[:, :], chosen[:, :], ALU.mult), "kept", ["exp", "chosen"])
        for f in range(2):
            V(lambda e, f=f: e.tensor_scalar(weight[:, f, :], onesN[:, :], expo[:, f:f + 1], None, ALU.mult), ("weight", f), ["kept", "ones"])
            V(lambda e, f=f: e.tensor_scalar(place[:, f, :], index[:, 1:1 + K], rank[:, f:f + 1], None, ALU.is_equal), ("place", f), ["in"])
        for f in range(2):
            pre.do("tensor", mm(t_ps[0][:, f * K:(f + 1) * K], weight[:, f, :], place[:, f, :]), done=("w_row", f),
                   after=[("place", 1)])
            pre.do("tensor", mm(t_ps[1][0:1, f * K:(f + 1) * K], index[:, 0:1], place[:, f, :]), done=("pick", f),
                   after=[])
        V(lambda e: e.tensor_copy(w_row[:, :, :].rearrange("p a b -> p (a b)"), t_ps[0][:, 0:2 * K]), "w_row", [("pick", 1)])
        V(lambda e: e.tensor_copy(picks[:, :], t_ps[1][0:1, 0:2 * K]), "picks", [])
        V(lambda e: e.tensor_reduce(total[:, :], w_row[:, :, :], X, ALU.add), "total", ["w_row"])
        V(lambda e: e.reciprocal(inv_sum[:, :], total[:, :]), "inv", ["total"])
        for f in range(2):
            for half in range(2):
                rows = slice(R * half, R * half + R)
                V(lambda e, f=f, half=half, rows=rows: e.tensor_scalar(
                    w_col[rows, f, :], w_row[rows, f, :].rearrange("p (a two) -> p a two", two=2)[:, :, half],
                    inv_sum[rows, f:f + 1], None, ALU.mult), ("w_col", f, half), ["inv"])

        reg, number = {}, {}
        stages = []
        for f in range(2):
            A_d, B_d = comp[bases[f][0]], comp[bases[f][1]]
            d_in, d_out = A_d.shape[1], B_d.shape[2]
            MB = d_in // P
            NW = min(512, d_out)
            WA = min(512, d_in)
            A_BANKS = d_in // WA
            small_a = d_in < d_out
            slots = (Stage(nc, ctx, f"comp_ahead{f}"), Stage(nc, ctx, f"comp{f}"))
            a_rows = A_d.rearrange("k (o p) r -> k p o r", p=P)

            def chosen_number(e, f, q, half):
                if (e, q, half) not in number:
                    number[e, q, half] = e.value_load(picks[0:1, bass.ds(reg[e] * 4 + (f * K + 2 * q + half), 1)],
                                                      min_val=0, max_val=N - 1)
                return number[e, q, half]

            def load_pair(f, q, stage, a_rows, B_d, MB, d_out):
                for half in range(2):
                    def load_a(e, half=half):
                        k = chosen_number(e, f, q, half)
                        return e.dma_start(A[:, q, 0:MB, half, :], a_rows[bass.ds(k, 1)].rearrange("a p o r -> (a p) o r"))

                    def load_b(e, half=half):
                        k = chosen_number(e, f, q, half)
                        return e.dma_start(Bm[R * half:R * half + R, q, 0:d_out],
                                           B_d[bass.ds(k, 1)].rearrange("a r n -> (a r) n"))
                    for load in (load_a, load_b):
                        stage.do("sync", load, dma=("AB", q), after=[Prev(("AT_ps", q)), Prev(("B_lo", q))])

            def split_with(stage, weight, hi, lo, src, done_hi, done_lo, ready, free):
                if weight:
                    stage.do("scalar", lambda e: e.activation(hi, src, ACT.Copy, scale=weight(e)), done=done_hi,
                             after=[ready, free], apart=True)
                    stage.do("vector", lambda e: e.scalar_tensor_tensor(lo, src, weight(e), hi.bitcast(F32),
                                                                        ALU.mult, ALU.subtract), done=done_lo, after=[done_hi])
                else:
                    stage.do("scalar", lambda e: e.activation(hi, src, ACT.Copy), done=done_hi, after=[ready, free])
                    stage.do("vector", lambda e: e.tensor_tensor(lo, src, hi.bitcast(F32), ALU.subtract), done=done_lo,
                             after=[done_hi])

            def prepare(f, q, stage, MB, WA, A_BANKS, d_out, small_a, work):
                weight = lambda e: w_col[:, f, bass.ds(reg[e] * 2 + q, 1)]
                multiplied = Prev(("mm", 1)) if q else At(work, ("mm", 0), "before")
                for m in range(MB):
                    at = m * P
                    stage.do("tensor", lambda e, m=m, at=at: e.transpose(
                        t_ps[2 * q + at // 512][:, at % 512:at % 512 + P], A[:, q, m, :, :].rearrange("p h r -> p (h r)"),
                        identity[:, :]), done=("AT_ps", q) if m == MB - 1 else None,
                        after=[("AB", q), Prev(("AT_lo", q, A_BANKS - 1))])
                for i in range(A_BANKS):
                    hi, lo = (t[:, q, i * WA:(i + 1) * WA] for t in AT)
                    split_with(stage, weight if small_a else None, hi, lo, t_ps[2 * q + i][:, 0:WA],
                               ("AT_hi", q, i), ("AT_lo", q, i), ("AT_ps", q), multiplied)
                hi, lo = (t[:, q, 0:d_out] for t in Bs)
                split_with(stage, None if small_a else weight, hi, lo, Bm[:, q, 0:d_out],
                           ("B_hi", q), ("B_lo", q), ("AB", q), multiplied)

            def multiply(q, MB, NW, A_BANKS, d_out, slots):
                parts = []
                for m in range(MB):
                    for n in range(d_out // NW):
                        at = m * d_out + n * NW
                        parts.append((acc[at // 512][:, at % 512:at % 512 + NW],
                                      tuple(t[:, q, m * P:(m + 1) * P] for t in AT),
                                      tuple(t[:, q, n * NW:(n + 1) * NW] for t in Bs), False, False))
                event = lambda name: name if q else At(slots[0], name, "this")
                slots[1].do("tensor", mm3(parts), done=("mm", q),
                            after=[event(("AT_lo", q, A_BANKS - 1)), event(("B_lo", q))])

            for q in range(2):
                load_pair(f, q, slots[q], a_rows, B_d, MB, d_out)
            prepare(f, 0, slots[0], MB, WA, A_BANKS, d_out, small_a, slots[1])
            prepare(f, 1, slots[1], MB, WA, A_BANKS, d_out, small_a, slots[1])
            multiply(0, MB, NW, A_BANKS, d_out, slots)
            mark = {e: len(slots[1].queue[e]) for e in ENGINES}
            multiply(1, MB, NW, A_BANKS, d_out, slots)
            stages.append((slots, mark, A_BANKS))

        post = [Stage(nc, ctx, f"compout{f}") for f in range(2)]
        for f, (hi, lo) in enumerate((up, down)):
            for i in range(4):
                cols = slice(i * 512, (i + 1) * 512)
                fl = lambda t: t[:, :, :].rearrange("p a b -> p (a b)")[:, cols]
                last = At(stages[f][0][1], ("mm", 1), K // 4 - 1)
                post[f].do("tensor", lambda e, i=i: e.matmul(acc[i][:, :], zero[:, 0:P], zero[:, :], start=False, stop=True),
                           done=("closed", i), after=[last])
                post[f].do("scalar", lambda e, i=i, d=fl(hi): e.activation(d, acc[i][:, :], ACT.Copy), done=("hi", i),
                           after=[("closed", i)])
                post[f].do("vector", lambda e, i=i, d=fl(lo), g=fl(hi): e.tensor_tensor(d, acc[i][:, :], g.bitcast(F32), ALU.subtract),
                           done=("lo", i), after=[("hi", i)])

        def wait_for(eng, stage, name, iteration=0):
            sem, per, const = stage.value(name, iteration)
            eng.wait_ge(sem, iteration * per + const)

        with nc.Block() as block:
            def body(name):
                def group(eng, f, i, last=False):
                    (ahead, work), mark, _ = stages[f]
                    emit = lambda ops: (number.clear(), work.emit(name, eng, i, {"this": i}, ops))
                    reg[eng] = i
                    emit(work.queue[name][:mark[name]])
                    if not last:
                        reg[eng] = i + 1
                        number.clear()
                        ahead.emit(name, eng, i + 1, {"before": i})
                        reg[eng] = i
                    emit(work.queue[name][mark[name]:])

                def program(eng):
                    pre.credit(name, eng)
                    pre.emit(name, eng, 0)
                    for f in range(2):
                        (ahead, work), mark, _ = stages[f]
                        ahead.credit(name, eng)
                        work.credit(name, eng)
                        post[f].credit(name, eng)
                        if name == "tensor":
                            if f == 0:
                                wait_for(eng, pre, "zero")
                                wait_for(eng, pre, "picks")
                            else:
                                wait_for(eng, post[0], ("lo", 3))
                            for i in range(4):
                                eng.matmul(acc[i][:, :], zero[:, 0:P], zero[:, :], start=True, stop=False)
                        if name in ("scalar", "vector"):
                            wait_for(eng, pre, ("w_col", 1, 1))
                        if name == "scalar" and f == 1:
                            wait_for(eng, stages[0][0][1], ("mm", 1), K // 4 - 1)
                        if name == "sync":
                            wait_for(eng, pre, "picks")
                            if f == 1:
                                (ahead0, work0), _, banks0 = stages[0]
                                for q, stage in enumerate((ahead0, work0)):
                                    wait_for(eng, stage, ("AT_ps", q), K // 4 - 1)
                                    wait_for(eng, stage, ("B_lo", q), K // 4 - 1)
                        reg[eng] = 0
                        number.clear()
                        ahead.emit(name, eng, 0, {"before": -1})
                        with eng.Fori(0, K // 4 - 1) as i:
                            group(eng, f, i)
                        group(eng, f, K // 4 - 1, last=True)
                        post[f].emit(name, eng, 0)
                return program
            for name in ENGINES:
                getattr_block(block, name)(body(name))


def layernorm_pieces(stage, key, ins, outs, stats, moments, var_eps, rstd, minus_half, eps, gain, shift,
                     ready, free, done, first=()):
    n = len(ins)

    def measure():
        for t in range(n):
            stage.do("vector", lambda e, t=t: e.bn_stats(stats[:, t, :], ins[t]), done=("stats", key, t),
                     after=list(ready) + list(first) if t == 0 else [])
        for t in range(n):
            stage.do("vector", lambda e, t=t: e.bn_aggr(moments[:, t, :], stats[:, t, :]), done=("moments", key, t),
                     after=[("stats", key, t)], apart=True)
        stage.do("vector", lambda e: e.tensor_scalar(var_eps, moments[:, :, 1], eps, None, ALU.add),
                 done=("var", key), after=[("moments", key, n - 1)])
        stage.do("gpsimd", lambda e: e.tensor_tensor(rstd, var_eps, minus_half[:, 0:n], ALU.pow),
                 done=("rstd", key), after=[("var", key)])
        if gain is not None:
            for t in range(n):
                stage.do("vector", lambda e, t=t: e.scalar_tensor_tensor(
                    ins[t], ins[t], moments[:, t, 0:1], gain, ALU.subtract, ALU.mult), done=("centred", key, t))

    def apply():
        for t in range(n):
            event = done if t == n - 1 else (done, t)
            ready = [("rstd", key)] + (list(free) if t == 0 else [])
            if gain is not None:
                stage.do("vector", lambda e, t=t: e.scalar_tensor_tensor(
                    outs[t], ins[t], rstd[:, t:t + 1], shift, ALU.mult, ALU.add), done=event,
                    after=[("centred", key, t)] + ready)
            else:
                stage.do("vector", lambda e, t=t: e.tensor_scalar(
                    outs[t], ins[t], moments[:, t, 0:1], rstd[:, t:t + 1], ALU.subtract, ALU.mult), done=event,
                    after=ready)
    return [measure, apply]


def layernorm(*args, **kwargs):
    for piece in layernorm_pieces(*args, **kwargs):
        piece()


def fixed(operand, e):
    return operand(e) if callable(operand) else operand


def run_loop(nc, setup, work, trips, reg, waits, sync_loop):
    with nc.Block() as block:
        def body(name):
            def program(eng):
                setup.credit(name, eng)
                setup.emit(name, eng, 0)
                work.credit(name, eng)
                if name == "sync":
                    sync_loop(eng)
                elif work.queue[name]:
                    with eng.Fori(0, trips) as i:
                        reg[eng] = i
                        work.emit(name, eng, i)
                if name == "sync":
                    for w in waits:
                        sem, per, const = work.value(w, 0)
                        eng.wait_ge(sem, (trips - 1) * per + const)
            return program
        for name in ENGINES:
            getattr_block(block, name)(body(name))


def getattr_block(block, name):
    return {"tensor": block.tensor, "vector": block.vector, "scalar": block.scalar,
            "gpsimd": block.gpsimd, "sync": block.sync}[name]


def build(nc, t):
    conv_phase(nc, t["x"], t["bands1"], t["bands2"], t["bias1"], t["bias2"], t["ln0"], t["eye"], t["h0"])
    attention_phase(nc, t["h0"], t["h4"], t["x"].shape[1], t["x"].shape[2], t["wqkv"], t["rows"], t["bq"], t["bk"],
                    {n: t[n] for n in ("cos_k", "sin_k", "cos_q", "sin_q")}, t)
    comp = {n: t[n] for n in ("logits", "logit_col", "index", "A1", "B1", "A2", "B2")}
    ffn_phase(nc, t["x"], t["h4"], t["out"], t["w1"], t["b1"], t["w2"], t["rows2"], comp, t["eye"], t["tri"])


def layout(inputs):
    import numpy as np
    f = lambda n: np.ascontiguousarray(inputs["L0_attn_" + n])
    x = f("x")
    H = x.shape[2]
    c1, c2 = f("conv1_w"), f("conv2_w")
    d = {"x": x}
    w1 = c1.reshape(H // 16, 2, 8, 4, 5)
    b1 = np.zeros((8, 2, 8, H // 16, 2, 4, 8, 4), c1.dtype)
    for k in range(2):
        for c in range(8):
            for s in range(4):
                for tap in range(5):
                    b1[s + tap, k, c, :, k, s, c, :] = w1[:, k, c, :, tap]
    d["bands1"] = b1.reshape(128, -1)
    w2 = c2.reshape(H // 8, 8, 4, 5)
    b2 = np.zeros((4, 8, 4, H // 8, 3, 4, 8), c2.dtype)
    for s in range(4):
        for c in range(8):
            for g in range(3):
                for so in range(4):
                    tap = 4 * (g - 1) + s - so + 2
                    if 0 <= tap < 5:
                        b2[s, c, :, :, g, so, c] = w2[:, c, :, tap].T
    d["bands2"] = b2.reshape(128, -1)
    bias1 = f("conv1_b").reshape(H // 8, 32).T
    d["bias1"] = np.ascontiguousarray(np.tile(bias1, (4, 1)))
    bias2 = f("conv2_b").reshape(H // 32, 4, 1, 8)
    d["bias2"] = np.ascontiguousarray(np.broadcast_to(bias2, (H // 32, 4, 4, 8)).reshape(H // 32, 128).T)
    d["ln0"] = np.stack([f("ln0_g"), f("ln0_b")])
    w = np.concatenate([f("Wq"), f("Wk"), f("Wv")], axis=2)
    L, T = w.shape[0], x.shape[1]
    w = w.reshape(L, 2, 128, 3 * H).transpose(0, 2, 1, 3).reshape(L, 128, 6 * H)
    d["wqkv"] = np.ascontiguousarray(np.concatenate([w, w[:1]]))
    d["rows"] = np.stack([f("bv"), f("lnA_g"), f("lnA_b")], axis=1).reshape(1, -1)
    d["bq"] = np.ascontiguousarray(f("bq").reshape(L * 2, 128).T)
    d["bk"] = np.ascontiguousarray(f("bk").reshape(L * 2, 128).T)
    inv = (np.float32(1) / np.float32(10000) ** (np.arange(0, H, 2, dtype=np.float32) / np.float32(H))).astype(np.float32)
    angle = np.repeat(np.arange(T, dtype=np.float32)[:, None] * inv[None, :], 2, axis=1).astype(np.float64)
    cos, sin = np.cos(angle).astype(np.float32), np.sin(angle).astype(np.float32)
    sign = np.tile(np.array([-1, 1], np.float32), H // 2)
    order = lambda a: a.reshape(T // 512, 128, 4, H).transpose(0, 2, 1, 3)
    rows = lambda a: np.ascontiguousarray(order(a).reshape(T // 128, 128, H).transpose(1, 0, 2).reshape(128, -1))
    cols = lambda a: np.ascontiguousarray(order(a).reshape(T, H).T.reshape(2, 128, T).transpose(1, 0, 2).reshape(128, -1))
    d["cos_k"], d["sin_k"] = rows(cos), rows(sin * sign)
    d["cos_q"], d["sin_q"] = cols(cos), cols(sin)
    i = np.arange(0, 128, 2)
    rot = np.zeros((128, 128), np.float32)
    rot[i + 1, i], rot[i, i + 1] = 1, -1
    d["rot"] = rot
    head = np.arange(128) // 16
    d["kv_mask"] = ((head[:, None] == head[None, :]) / T).astype(np.float32)
    d["head_mask"] = (head[:, None] == np.arange(8)[None, :]).astype(np.float32)
    d["w1"] = np.ascontiguousarray(f("W1").reshape(2, 128, 4 * H).transpose(1, 0, 2).reshape(128, 8 * H))
    d["w2"] = np.ascontiguousarray(f("W2").reshape(8, 128, H).transpose(1, 0, 2).reshape(128, 8 * H))
    d["b1"] = np.ascontiguousarray(f("b1").reshape(8, 128).T)
    d["rows2"] = np.concatenate([f("b2"), f("ln2_g"), f("ln2_b")])[None, :]
    g = lambda n: np.ascontiguousarray(inputs["L0_ffn_" + n])
    d["A1"], d["B1"], d["A2"], d["B2"] = g("fc1_A"), g("fc1_B"), g("fc2_A"), g("fc2_B")
    logits = np.stack([g("fc1_logits"), g("fc2_logits")])
    d["logits"], d["logit_col"] = logits.reshape(1, -1), np.ascontiguousarray(logits.T)
    n = np.arange(64, dtype=np.float32)
    d["index"] = np.concatenate([n[:, None], np.tile(n[None, :32], (64, 1))], axis=1)
    d["tri"] = (n[None, :] < n[:, None]).astype(np.float32)
    d["eye"] = np.eye(128, dtype=np.float32)
    return d


def kernel(**inputs):
    import numpy as _np
    import concourse.bacc as _bacc
    from concourse import mybir as _mybir
    from concourse.bass_utils import run_bass_kernel_spmd as _run

    nc = _bacc.Bacc("TRN2", target_bir_lowering=False, num_devices=1)
    arrays, t = {}, {}
    for name, a in layout(inputs).items():
        arrays[f"in_{name}"] = a
        t[name] = nc.dram_tensor(f"in_{name}", a.shape, _mybir.dt.from_np(a.dtype), kind="ExternalInput").ap()
    shape = inputs["L0_attn_x"].shape
    t["out"] = nc.dram_tensor("out_0", shape, _mybir.dt.float32, kind="ExternalOutput").ap()
    rows = (shape[0], 128, shape[1] * shape[2] // 128)
    t["h0"] = nc.dram_tensor("h0", rows, _mybir.dt.float32, kind="Internal").ap()
    t["h4"] = nc.dram_tensor("h4", rows, _mybir.dt.float32, kind="Internal").ap()
    build(nc, t)
    r = _run(nc, [arrays], core_ids=[0])
    return r.results[0]["out_0"]
```

```python
import concourse.bass as bass
from concourse import mybir
from contextlib import ExitStack

F32 = mybir.dt.float32
F32R = mybir.dt.float32r
U32 = mybir.dt.uint32
I32 = mybir.dt.int32
ALU = mybir.AluOpType
ACT = mybir.ActivationFunctionType

P = 128
ENGINES = ("tensor", "vector", "scalar", "gpsimd", "sync")


class Stage:

    def __init__(self, nc, ctx, label):
        self.nc, self.ctx, self.label = nc, ctx, label
        self.queue = {e: [] for e in ENGINES}
        self.sem, self.count, self.event = {}, {}, {}
        self.dma_sem, self.dma_count, self.dma_engine = {}, {}, {}
        self.relay = {}

    def do(self, engine, make, done=None, after=(), dma=None, apart=False):
        if done is not None:
            if engine not in self.sem:
                self.sem[engine] = self.ctx.enter_context(self.nc.semaphore(f"{self.label}_{engine}"))
                self.count[engine] = 0
            self.count[engine] += 1
            assert done not in self.event, done
            self.event[done] = (engine, self.count[engine])
        if dma is not None:
            if dma not in self.dma_sem:
                tag = "_".join(str(x) for x in dma) if isinstance(dma, tuple) else dma
                self.dma_sem[dma] = self.ctx.enter_context(self.nc.semaphore(f"{self.label}_dma_{tag}"))
                self.dma_count[dma] = 0
                self.dma_engine[dma] = engine
            self.dma_count[dma] += 1
        apart = apart or engine in ("gpsimd", "sync")
        if apart and engine not in self.relay:
            self.relay[engine] = self.ctx.enter_context(self.nc.semaphore(f"{self.label}_relay_{engine}"))
        self.queue[engine].append((make, done, after, dma, apart))

    def value(self, name, iteration, back=0):
        if name in self.dma_sem:
            n = 16 * self.dma_count[name]
            return self.dma_sem[name], n, n * (2 - back)
        engine, k = self.event[name]
        n = self.count[engine]
        return self.sem[engine], n, n * (1 - back) + k

    def credit(self, engine, eng):
        if engine in self.sem:
            eng.sem_inc(self.sem[engine], self.count[engine])
        for name, count in self.dma_count.items():
            if self.dma_engine[name] == engine:
                eng.sem_inc(self.dma_sem[name], 16 * count)

    def emit(self, engine, eng, iteration, where_is=None, ops=None):
        seen = {}
        for make, done, after, dma, apart in (self.queue[engine] if ops is None else ops):
            waited = False
            for item in after:
                if isinstance(item, At):
                    stage, name, where, back = item.stage, item.name, item.iteration, 0
                    if isinstance(where, str):
                        where = where_is[where]
                elif isinstance(item, LastUse):
                    stage, name, where, back = item.stage, item.banks.last[item.bank], where_is[item.iteration], 0
                elif isinstance(item, BankFree):
                    stage, name, where, back = self, item.banks.last[item.bank], iteration, 1
                elif isinstance(item, Prev):
                    stage, name, where, back = self, item.name, iteration, 1
                else:
                    stage, name, where, back = self, item, iteration, 0
                sem, per, const = stage.value(name, where, back)
                spot = (stage.label, id(sem), id(where))
                if seen.get(spot, -1) >= const:
                    continue
                seen[spot] = const
                eng.wait_ge(sem, where * per + const)
                waited = True
                if engine == "sync" and not isinstance(iteration, int):
                    eng.sem_inc(self.relay[engine], 1)
                    waited = False
            if waited and apart and not isinstance(iteration, int):
                eng.sem_inc(self.relay[engine], 1)
            inst = make(eng)
            if done is not None:
                inst.then_inc(self.sem[engine], 1)
            if dma is not None:
                inst.then_inc(self.dma_sem[dma], 16)


class Prev:
    def __init__(self, name):
        self.name = name


class At:
    def __init__(self, stage, name, iteration):
        self.stage, self.name, self.iteration = stage, name, iteration


class Banks:

    def __init__(self, tensors):
        self.tensors, self.turn, self.last = tensors, 0, {}

    def take(self, reader):
        b = self.turn % len(self.tensors)
        self.turn += 1
        free = self.last.get(b, None)
        self.last[b] = reader
        return self.tensors[b], (free if free is not None else BankFree(self, b))


class BankFree:

    def __init__(self, banks, bank):
        self.banks, self.bank = banks, bank


class LastUse:

    def __init__(self, stage, banks, bank, iteration):
        self.stage, self.banks, self.bank, self.iteration = stage, banks, bank, iteration


def mm(out, lhsT, rhs, start=True, stop=True):
    return lambda e: e.matmul(out, lhsT, rhs, start=start, stop=stop)


def mm3(parts):
    def make(e):
        for out, (wh, wl), (xh, xl), start, stop in parts:
            e.matmul(out, wh, xh, start=start, stop=False)
            e.matmul(out, wh, xl, start=False, stop=False)
            last = e.matmul(out, wl, xh, start=False, stop=stop)
        return last
    return make


def conv_phase(nc, x, bands1, bands2, conv1_b, conv2_b, ln0, eye, h0):
    B, N, H = x.shape
    S, W, TAPS_AHEAD = 4, 8, 2
    G = N // S
    MT = G // P
    CP = H // 32
    TILES = MT * S
    LANES = 2
    HB = 4

    xg = x.rearrange("b (g s) c -> b g s c", s=S)

    ctx = ExitStack()
    with ctx:
        sb = lambda n, s, d=F32: ctx.enter_context(nc.sbuf_tensor(n, s, d))
        pb = lambda n, s: ctx.enter_context(nc.psum_tensor(n, s, F32))

        band1 = sb("band1", [P, CP * HB * P])
        band1_hi = sb("band1_hi", [P, CP * HB, P], F32R)
        band1_lo = sb("band1_lo", [P, CP * HB, P], F32R)
        band2 = sb("band2", [P, CP * HB, 3, 32])
        bias1 = sb("bias1", [P, CP * HB])
        bias2 = sb("bias2", [P, CP])
        gain = sb("gain0", [P, H])
        shift = sb("shift0", [P, H])
        identity = sb("identityA", [P, P])
        minus_half = sb("minus_halfA", [P, TILES])
        xw = [sb(f"xw{l}", [P, MT, W, H]) for l in range(LANES)]
        xr = sb("xr", [P, 2, 2, MT, P])
        xt_hi = sb("xt_hi", [P, 2, 2, G], F32R)
        xt_lo = sb("xt_lo", [P, 2, 2, G], F32R)
        hidden = sb("hidden", [P, 2, HB, G + 2])
        convT = sb("convT", [P, 2, G])
        y = [sb(f"yA{l}", [P, TILES, H]) for l in range(LANES)]
        h = [sb(f"hA{l}", [P, TILES, H]) for l in range(LANES)]
        stats = sb("statsA", [P, LANES, TILES, 6])
        moments = sb("momentsA", [P, LANES, TILES, 2])
        var_eps = sb("var_epsA", [P, LANES, TILES])
        rstd = sb("rstdA", [P, LANES, TILES])

        xt_ps = [pb(f"xt_ps{i}", [P, 2, G]) for i in range(2)]
        hid_ps = [pb(f"hid_ps{i}", [P, 2, G]) for i in range(3)]
        conv_ps = pb("conv_ps", [P, 512])
        back_ps = [pb(f"back_ps{i}", [P, MT, P]) for i in range(2)]

        setup = Stage(nc, ctx, "convset")
        work = Stage(nc, ctx, "conv")
        tail = Stage(nc, ctx, "convtail")

        PARTS = 4
        width = CP * HB * P // PARTS
        setup.do("scalar", lambda e: e.dma_start(identity[:, :], eye), dma="identity")
        setup.do("scalar", lambda e: e.dma_start(bias1[:, :], conv1_b), dma="bias1")
        for k in range(PARTS):
            cols = slice(k * width, (k + 1) * width)
            setup.do("scalar", lambda e, c=cols: e.dma_start(band1[:, c], bands1[:, c]), dma=("band1", k))
        setup.do("scalar", lambda e: e.dma_start(band2[:, :, :, :].rearrange("p b d n -> p (b d n)"), bands2), dma="small")
        setup.do("scalar", lambda e: e.dma_start(bias2[:, :], conv2_b), dma="small")
        setup.do("scalar", lambda e: e.dma_start(gain[:, :], ln0[0:1, :].partition_broadcast(P)), dma="small")
        setup.do("scalar", lambda e: e.dma_start(shift[:, :], ln0[1:2, :].partition_broadcast(P)), dma="small")
        b1f = lambda t: t[:, :, :].rearrange("p b n -> p (b n)")
        for k in range(PARTS):
            cols = slice(k * width, (k + 1) * width)
            setup.do("vector", lambda e, c=cols: e.tensor_copy(b1f(band1_hi)[:, c], band1[:, c]), done=("hi", k),
                     after=[("band1", k)])
            setup.do("vector", lambda e, c=cols: e.tensor_tensor(
                b1f(band1_lo)[:, c], band1[:, c], b1f(band1_hi)[:, c].bitcast(F32), ALU.subtract), done=("lo", k),
                after=[("hi", k)])
        setup.do("gpsimd", lambda e: e.memset(minus_half[:, :], -0.5), done="half")
        for l in range(LANES):
            setup.do("gpsimd", lambda e, l=l: e.memset(xw[l][:, 0, 0:2, :], 0.0), done=("pad0", l))
            setup.do("gpsimd", lambda e, l=l: e.memset(xw[l][:, MT - 1, W - 2:W, :], 0.0), done=("pad1", l))
        setup.do("gpsimd", lambda e: e.memset(hidden[:, :, :, 0:1], 0.0), done="pad2")
        setup.do("gpsimd", lambda e: e.memset(hidden[:, :, :, G + 1:G + 2], 0.0), done="pad3")

        def load(l, reg):
            tile = xw[l]
            b = lambda e: reg[e] * LANES + l
            q = "sync"

            def copy(p0, p1, mt, w0, w1, s0, g0):
                def make(e):
                    src = xg[bass.ds(b(e), 1), g0:g0 + p1 - p0, s0:s0 + w1 - w0, :]
                    return e.dma_start(tile[p0:p1, mt, w0:w1, :], src.rearrange("a g s c -> (a g) s c"))
                free = [Prev(("x_read", l)), Prev(("x_sent", l))]
                work.do(q, make, dma=("x", l), after=free + [At(setup, ("pad0", l), 0), At(setup, ("pad1", l), 0)])

            cut = 112
            for mt in range(MT):
                g = mt * P
                copy(0, P, mt, 2, 6, 0, g)
                if mt == 0:
                    copy(1, 1 + cut, mt, 0, 2, 2, 0)
                    copy(1 + cut, P, mt, 0, 2, 2, cut)
                else:
                    copy(0, P, mt, 0, 2, 2, g - 1)
                if mt == MT - 1:
                    copy(0, cut, mt, 6, 8, 0, g + 1)
                    copy(cut, P - 1, mt, 6, 8, 0, g + 1 + cut)
                else:
                    copy(0, P, mt, 6, 8, 0, g + 1)

        steps = [(l, cp) for l in range(LANES) for cp in range(CP)]
        n_steps = len(steps)

        def earlier(kind, n, ring):
            return [(kind, n - ring)] if n >= ring else [Prev((kind, n - ring + n_steps))]

        def to_channels(n):
            l, cp = steps[n]
            bank = xt_ps[n % 2]
            for mt in range(MT):
                work.do("gpsimd", lambda e, mt=mt: e.tensor_copy(
                    xr[:, n % 2, :, mt, :].rearrange("p a (w c) -> p w a c", w=W),
                    xw[l][:, mt, :, 32 * cp:32 * cp + 32].rearrange("p w (a c) -> p w a c", a=2)),
                    done=("xr", n) if mt == MT - 1 else None,
                    after=[("x", l)] + earlier("xt", n, 2))
            for cg in range(2):
                for mt in range(MT):
                    last = cg == 1 and mt == MT - 1
                    work.do("tensor", lambda e, cg=cg, mt=mt: e.transpose(
                        bank[:, cg, mt * P:(mt + 1) * P], xr[:, n % 2, cg, mt, :], identity[:, :]),
                        done=("xt", n) if last else None,
                        after=[("xr", n), At(setup, "identity", 0)] + earlier("xt_lo", n, 2))
            r = n % 2
            flat = lambda t: t[:, :, :].rearrange("p a g -> p (a g)")
            hi = xt_hi[:, r, :, :].rearrange("p a g -> p (a g)")
            lo = xt_lo[:, r, :, :].rearrange("p a g -> p (a g)")
            work.do("scalar", lambda e: e.activation(hi, flat(bank), ACT.Copy), done=("xt_hi", n),
                    after=[("xt", n)] + earlier("conv1", n, 2))
            work.do("vector", lambda e: e.tensor_tensor(lo, flat(bank), hi.bitcast(F32), ALU.subtract),
                    done=("xt_lo", n), after=[("xt_hi", n)])

        def conv1(n):
            l, cp = steps[n]
            r = n % 2
            for cg in range(2):
                k = 2 * n + cg
                bank = hid_ps[k % 3]
                parts = [(bank[:, j, :], (band1_hi[:, 4 * cp + 2 * cg + j, :], band1_lo[:, 4 * cp + 2 * cg + j, :]),
                          (xt_hi[:, r, cg, :], xt_lo[:, r, cg, :]), True, True) for j in range(2)]
                free = [("hidden", k - 3)] if k >= 3 else [Prev(("hidden", k - 3 + 2 * n_steps))]
                work.do("tensor", mm3(parts), done=("hid", k),
                        after=[("xt_lo", n), At(setup, ("lo", cp * PARTS // CP), 0)] + free)
                if cg == 1:
                    work.event[("conv1", n)] = work.event[("hid", k)]
                for j in range(2):
                    blk = 2 * cg + j
                    work.do("scalar", lambda e, j=j, blk=blk, bank=bank: e.activation(
                        hidden[:, r, blk, 1:1 + G], bank[:, j, :], ACT.Gelu,
                        bias=bias1[:, 4 * cp + blk:4 * cp + blk + 1]),
                        done=("hidden", k) if j else None,
                        after=[("hid", k), At(setup, "bias1", 0)] + earlier("conv", n, 2))

        def conv2(n):
            l, cp = steps[n]
            r = n % 2
            for d in range(3):
                for blk in range(HB):
                    work.do("tensor", mm(conv_ps[32 * blk:32 * blk + 32, 0:G], band2[:, 4 * cp + blk, d, :],
                                         hidden[:, r, blk, d:d + G], d == 0, d == 2),
                            done=("conv", n) if d == 2 and blk == HB - 1 else None,
                            after=[("hidden", 2 * n + 1), At(setup, "small", 0), At(setup, "pad2", 0), At(setup, "pad3", 0)] + earlier("convT", n, 1))
            work.do("vector", lambda e: e.tensor_scalar(convT[:, r, :], conv_ps[:, 0:G], bias2[:, cp:cp + 1], None,
                                                        ALU.add),
                    done=("convT", n), after=[("conv", n), At(setup, "small", 0)] + earlier("back", n, 2))

        def to_tokens(n):
            l, cp = steps[n]
            r = n % 2
            bank = back_ps[r]
            for mt in range(MT):
                work.do("tensor", lambda e, mt=mt: e.transpose(bank[:, mt, :], convT[:, r, mt * P:(mt + 1) * P],
                                                               identity[:, :]),
                        done=("back", n) if mt == MT - 1 else None,
                        after=[("convT", n)] + earlier("y", n, 2))
            for mt in range(MT):
                ins = bank[:, mt, :].rearrange("p (j s c) -> p j s c", j=4, s=S)
                res = xw[l][:, mt, 2:2 + S, 32 * cp:32 * cp + 32].rearrange("p s (j c) -> p j s c", j=4)
                out = y[l][:, mt * S:(mt + 1) * S, 32 * cp:32 * cp + 32].rearrange("p s (j c) -> p j s c", j=4)
                work.do("vector", lambda e, i=ins, q=res, o=out: e.tensor_tensor(o, i, q, ALU.add),
                        done=("y", n) if mt == MT - 1 else None,
                        after=[("back", n), At(tail, ("ln", 1), "iteration before") if l else Prev(("ln", 0))])
            if cp == CP - 1:
                work.event[("x_read", l)] = work.event[("y", n)]
                work.event[("x_sent", l)] = work.event[("xr", n)]

        def finish(l):
            stage = (work, tail)[l]
            last = ("y", (l + 1) * CP - 1)
            return layernorm_pieces(
                stage, l, [y[l][:, t, :] for t in range(TILES)], [h[l][:, t, :] for t in range(TILES)],
                stats[:, l], moments[:, l], var_eps[:, l], rstd[:, l], minus_half, 1e-12, gain[:, :], shift[:, :],
                ready=[At(work, last, "same iteration") if l else last], free=[Prev(("h0", l))], done=("ln", l),
                first=[At(setup, "small", 0), At(setup, "half", 0)], step=TILES // 2)

        for l in range(LANES):
            def store(e, l=l):
                b = reg[e] * LANES + l
                return e.dma_start(h0[bass.ds(b, 1), :, :].rearrange("a p f -> (a p) f"),
                                   h[l][:, :, :].rearrange("p t c -> p (t c)"))
            (work, tail)[l].do("sync", store, dma=("h0", l), after=[("ln", l)])

        reg = {}
        pieces = finish(0)
        pieces.insert(4, lambda: None)
        marks = []
        for n in range(n_steps + 3):
            if n < n_steps:
                to_channels(n)
            if 0 <= n - 1 < n_steps:
                conv1(n - 1)
            if 0 <= n - 2 < n_steps:
                conv2(n - 2)
            if 0 <= n - 3 < n_steps:
                to_tokens(n - 3)
            if n - 3 >= CP and pieces:
                pieces.pop(0)()
            if 1 <= n <= 7:
                marks.append({e: len(work.queue[e]) for e in ENGINES})
        parts = []
        pieces = finish(1)
        pieces.insert(4, lambda: None)
        for piece in pieces:
            before = {e: len(tail.queue[e]) for e in ENGINES if e != "sync"}
            piece()
            parts.append({e: tail.queue[e][before[e]:] for e in before})

        (store_0,), (store_1,) = work.queue["sync"], tail.queue["sync"]
        loads = []
        for l in range(LANES):
            work.queue["sync"] = []
            load(l, reg)
            loads.append(work.queue["sync"])

        trips = B // LANES
        with nc.Block() as block:
            def body(name):
                def put(eng, stage, i, ops):
                    reg[eng] = i
                    stage.emit(name, eng, i, {"iteration before": i - 1, "same iteration": i}, ops)

                def steps(eng, i, first=False):
                    at = 0
                    for mark, part in zip(marks, parts):
                        put(eng, work, i, work.queue[name][at:mark[name]])
                        at = mark[name]
                        if not first:
                            put(eng, tail, i - 1, part[name])
                    put(eng, work, i, work.queue[name][at:])

                def transfers(eng):
                    for l in range(LANES):
                        put(eng, work, 0, loads[l])
                    put(eng, work, 1, loads[0])
                    put(eng, work, 0, [store_0])
                    put(eng, work, 1, loads[1])
                    with eng.Fori(1, trips - 1) as i:
                        put(eng, tail, i - 1, [store_1])
                        put(eng, work, i + 1, loads[0])
                        put(eng, work, i, [store_0])
                        put(eng, work, i + 1, loads[1])
                    put(eng, tail, trips - 2, [store_1])
                    put(eng, work, trips - 1, [store_0])
                    put(eng, tail, trips - 1, [store_1])
                    for stage, l in ((work, 0), (tail, 1)):
                        sem, per, const = stage.value(("h0", l), 0)
                        eng.wait_ge(sem, (trips - 1) * per + const)

                def program(eng):
                    for stage in (setup, work, tail):
                        stage.credit(name, eng)
                    setup.emit(name, eng, 0)
                    if name == "sync":
                        transfers(eng)
                        return
                    steps(eng, 0, first=True)
                    with eng.Fori(1, trips) as i:
                        steps(eng, i)
                    for part in parts:
                        put(eng, tail, trips - 1, part[name])
                return program
            for name in ENGINES:
                getattr_block(block, name)(body(name))


def attention_phase(nc, h_in, h_out, T, H, wqkv, rows, bq, bk, rope, tables):
    B = h_in.shape[0]
    L = wqkv.shape[0] - 1
    TILES = T // P
    DUOS = TILES // 2
    CB = H // P
    NH = 16
    HD = H // NH
    HB = P // HD
    LANES = 2
    TQ = 512
    QH = T // TQ
    BV, GAIN, SHIFT = range(3)

    ROWS = 3
    HT = TILES // QH

    ctx = ExitStack()
    with ctx:
        sb = lambda n, s, d=F32: ctx.enter_context(nc.sbuf_tensor(n, s, d))
        pb = lambda n, s: ctx.enter_context(nc.psum_tensor(n, s, F32))

        w_raw = sb("w_raw", [P, CB, 2 * H])
        wv = sb("wv", [P, CB, H])
        w_hi = sb("w_hi", [P, CB, 2 * H], F32R)
        w_lo = sb("w_lo", [P, CB, 2 * H], F32R)
        vec = sb("vec", [P, L * ROWS * H])
        bqs = sb("bqs", [P, L * CB])
        bks = sb("bks", [P, L * CB])
        cos_k = sb("cos_k", [P, TILES, H])
        sin_k = sb("sin_k", [P, TILES, H])
        cos_q = sb("cos_q", [P, CB, T])
        sin_q = sb("sin_q", [P, CB, T])
        identity = sb("identityB", [P, P])
        rot = sb("rot", [P, P])
        kv_mask = sb("kv_mask", [P, P])
        head_mask = sb("head_mask", [P, HB])
        ones = sb("onesB", [P, P])
        minus_half = sb("minus_halfB", [P, TILES])

        h = [sb(f"hB{s}", [P, TILES, H + 1]) for s in range(LANES)]
        h_next = sb("h_next", [P, TILES, H])
        y = sb("yB", [P, TILES, H])
        hT_hi = sb("hT_hi", [P, CB, T], F32R)
        hT_lo = sb("hT_lo", [P, CB, T], F32R)
        gkT = sb("gkT", [P, CB, T])
        k_sums = sb("k_sums", [P, QH, CB])
        km_sum = sb("km_sum", [P, CB])
        offset = sb("offset", [P, TILES])
        kc = sb("kc", [P, 2, 2 * H])
        ks = sb("ks", [P, 2, 2 * H])
        kr = sb("kr", [P, 2, 2 * H])
        gT = [sb(f"gT{s}", [P, CB, T]) for s in range(LANES)]
        qc = [sb(f"qc{s}", [P, CB, T]) for s in range(LANES)]
        qs = [sb(f"qs{s}", [P, CB, T]) for s in range(LANES)]
        G = sb("G", [P, CB, H + 1])
        GT = sb("GT", [P, CB, H])
        kv_raw = sb("kv_raw", [P, CB, P])
        kv = sb("kv", [P, LANES, CB, P])
        kv_rot = sb("kv_rot", [P, LANES, CB, P])
        km = sb("km", [P, CB])
        kmb = sb("kmb", [P, LANES, CB, HB])
        c21 = sb("c21", [P, CB, HB])
        cst = sb("cst", [P, NH])
        den = sb("den", [P, TILES, NH])
        z = sb("z", [P, LANES, TILES, NH])
        stats = sb("statsB", [P, TILES, 6])
        moments = sb("momentsB", [P, TILES, 2])
        var_eps = sb("var_epsB", [P, TILES])
        rstd = sb("rstdB", [P, TILES])

        banks = Banks([pb(f"bank{i}", [P, 512]) for i in range(5)])
        g_ps = [pb(f"g_ps{i}", [P, 512]) for i in range(CB)]
        m_ps = pb("m_ps", [P, 512])

        setup = Stage(nc, ctx, "attset")
        pair = Stage(nc, ctx, "attpair")
        lay = Stage(nc, ctx, "att")
        k_bank = {}
        reg = {}

        two = lambda a: a.unsqueeze(1).broadcast_to([P, 2, a.shape[-1]])

        w3 = wqkv.rearrange("l p (c n) -> l p c n", c=CB)
        for dst, src in ((identity, tables["eye"]), (bqs, bq), (bks, bk)):
            setup.do("scalar", lambda e, d=dst, s=src: e.dma_start(d[:, :], s), dma="first")
        setup.do("scalar", lambda e: e.dma_start(w_raw[:, :, :], w3[0, :, :, 0:2 * H]), dma="w0")
        for name, dst, src in (("cos_k", cos_k, rope["cos_k"]), ("sin_k", sin_k, rope["sin_k"]),
                               ("cos_q", cos_q, rope["cos_q"]), ("sin_q", sin_q, rope["sin_q"])):
            setup.do("scalar", lambda e, d=dst, s=src: e.dma_start(d[:, :, :].rearrange("p a b -> p (a b)"), s), dma=name)
        for dst, src in ((rot, tables["rot"]), (kv_mask, tables["kv_mask"]), (head_mask, tables["head_mask"])):
            setup.do("scalar", lambda e, d=dst, s=src: e.dma_start(d[:, :], s), dma="consts")
        setup.do("scalar", lambda e: e.dma_start(vec[:, :], rows.partition_broadcast(P)), dma="consts")
        setup.do("scalar", lambda e: e.dma_start(wv[:, :, :], w3[0, :, :, 2 * H:3 * H]), dma="wv0")
        setup.do("scalar", lambda e: e.activation(w_hi[:, :, :], w_raw[:, :, :], ACT.Copy), done="w_hi", after=["w0"])
        setup.do("gpsimd", lambda e: e.memset(minus_half[:, :], -0.5), done="half")
        setup.do("gpsimd", lambda e: e.memset(ones[:, :], 1.0), done="ones")
        for s in range(LANES):
            setup.do("gpsimd", lambda e, s=s: e.memset(h[s][:, :, H:H + 1], 1.0), done=("ones", s))
        setup.do("vector", lambda e: e.tensor_tensor(w_lo[:, :, :], w_raw[:, :, :], w_hi[:, :, :].bitcast(F32),
                                                     ALU.subtract), done="w_lo", after=["w_hi"])
        first, consts = [At(setup, "first", 0)], [At(setup, "consts", 0)]
        k_tables = [At(setup, "cos_k", 0), At(setup, "sin_k", 0)]
        q_tables = [At(setup, "cos_q", 0), At(setup, "sin_q", 0)]
        w_now = [Prev("w_next"), At(setup, "w_lo", 0)]
        the_ones = [At(setup, "ones", 0)]

        def row(which, at=0, n=H):
            return lambda e: vec[:, bass.ds(reg[e][1] * (ROWS * H) + (which * H + at), n)]

        batch = lambda e, h, s: h[bass.ds(reg[e][0] * LANES + s, 1)].rearrange("a p (t c) -> (a p) t c", c=H)
        pair.do("sync", lambda e: e.dma_start(h_next[:, :, :], batch(e, h_in, 0)), dma="next",
                after=[Prev(("h", 0)), Prev(("hT", 0, QH - 1, CB - 1))])
        pair.do("sync", lambda e: e.dma_start(h[1][:, :, 0:H], batch(e, h_in, 1)), dma=("h", 1), after=[Prev(("sent", 1))])
        pair.do("gpsimd", lambda e: e.tensor_copy(h[0][:, :, 0:H], h_next[:, :, :]), done=("h", 0),
                after=["next", Prev(("sent", 0)), At(lay, ("hT", 0, QH - 1, CB - 1), "layer before")])

        def other(kind, s, *rest):
            return (kind, 0, *rest) if s else Prev((kind, 1, *rest))

        def split_h(s, half, stage=None, blocks=range(CB)):
            tok = slice(half * TQ, (half + 1) * TQ)
            stage = stage or lay
            for cb in blocks:
                if stage is pair:
                    b = half * CB + cb
                    bank, free = banks.tensors[b], LastUse(lay, banks, b, "layer before")
                    ready, used = ["next"], At(lay, ("q", 1, CB * QH - 1), "layer before")
                else:
                    bank, free = banks.take(("hT_lo", s, half, cb))
                    ready = [At(pair, ("h", s), "pair")] + [Prev(("ln", s, half)) if s else ("ln", s, half)]
                    used = ("q", 1 - s, CB * QH - 1)
                src = h_next if stage is pair else h[s]
                for t in range(HT):
                    stage.do("tensor", lambda e, cb=cb, t=t, bank=bank, src=src: e.transpose(
                        bank[:, t * P:(t + 1) * P], src[:, HT * half + t, cb * P:(cb + 1) * P], identity[:, :]),
                        done=("hT", s, half, cb) if t == HT - 1 else None, after=[free] + ready + first)
                stage.do("scalar", lambda e, cb=cb, bank=bank: e.activation(hT_hi[:, cb, tok], bank[:, :], ACT.Copy),
                         done=("hT_hi", s, half, cb), after=[("hT", s, half, cb), used])
                stage.do("vector", lambda e, cb=cb, bank=bank: e.tensor_tensor(
                    hT_lo[:, cb, tok], bank[:, :], hT_hi[:, cb, tok].bitcast(F32), ALU.subtract),
                    done=("hT_lo", s, half, cb), after=[("hT_hi", s, half, cb)])

        def between(pieces, n=2):
            for _ in range(min(n, len(pieces))):
                pieces.pop(0)()

        def project(s, half, which, col, bias, dst, used, sums=None, small=()):
            tok = slice(half * TQ, (half + 1) * TQ)
            for db in range(CB):
                k = half * CB + db
                c = slice(col + db * P, col + (db + 1) * P)
                bank, free = banks.take(("g" + which, s, k))
                parts = [(bank[:, :], (w_hi[:, cb, c], w_lo[:, cb, c]), (hT_hi[:, cb, tok], hT_lo[:, cb, tok]),
                          cb == 0, cb == CB - 1) for cb in range(CB)]
                ready = [free, *w_now] + (
                    [("hT_lo", s, half, CB - 1)] if s else
                    [Prev(("hT_lo", s, half, CB - 1)), At(pair, ("hT_lo", s, QH - 1, CB - 1), "pair")])
                for cb in range(CB):
                    lay.do("tensor", mm3(parts[cb:cb + 1]), done=(which, s, k) if cb == CB - 1 else None, after=ready)
                    between(small, 5)

                def make(e, db=db, bank=bank):
                    kw = {} if sums is None else {"accum_out": sums[:, half, db:db + 1]}
                    return e.activation(dst[:, db, tok], bank[:, :], ACT.Gelu,
                                        bias=bias[:, bass.ds(reg[e][1] * CB + db, 1)], **kw)
                lay.do("scalar", make, done=("g" + which, s, k), after=[(which, s, k)] + used + first, apart=True)

        def keys(s, half, small=()):
            project(s, half, "k", H, bks, gkT, [other("kt", s, DUOS - 1), other("km", s)], k_sums, small)

        def queries(s, half):
            project(s, half, "q", 0, bqs, gT[s], [Prev(("out", s, DUOS - 1))])

        def rotate_q(s, half):
            tok = slice(half * TQ, (half + 1) * TQ)
            for db in range(CB):
                k = half * CB + db
                for nm, dst, tab in (("qc", qc[s], cos_q), ("qs", qs[s], sin_q)):
                    lay.do("vector", lambda e, dst=dst, tab=tab, db=db: e.scalar_tensor_tensor(
                        dst[:, db, tok], gT[s][:, db, tok], 0.21, tab[:, db, tok], ALU.add, ALU.mult),
                        done=(nm, s, k), after=[("gq", s, k), Prev(("out", s, DUOS - 1))] + q_tables)

        def k_rows(s, u):
            bank, free = banks.take(("ks", s, u))
            k_bank[s, u] = bank
            for t in range(2):
                for db in range(CB):
                    lay.do("tensor", lambda e, t=t, db=db: e.transpose(
                        bank[:, t * H + db * P:t * H + (db + 1) * P], gkT[:, db, (2 * u + t) * P:(2 * u + t + 1) * P],
                        identity[:, :]), done=("kt", s, u) if t == 1 and db == CB - 1 else None,
                        after=[("gk", s, (u // 2) * CB + CB - 1), free])

        def rotate_k(s, u):
            bank, r = k_bank[s, u], u % 2
            ring = lambda kind: (kind, s, u - 2) if u >= 2 else other(kind, s, DUOS - 2 + u)
            flat = lambda t: t[:, 2 * u:2 * u + 2, :].rearrange("p t n -> p (t n)")
            lay.do("vector", lambda e: e.scalar_tensor_tensor(kc[:, r, :], bank[:, :], 0.21, flat(cos_k), ALU.add, ALU.mult),
                   done=("kc", s, u), after=[("kt", s, u), ring("kr")] + k_tables)
            pairs = lambda a: a.rearrange("p (i two) -> p i two", two=2)
            for k in range(2):
                lay.do("vector", lambda e, k=k: e.scalar_tensor_tensor(
                    pairs(ks[:, r, :])[:, :, k], pairs(bank[:, :])[:, :, 1 - k], 0.21, pairs(flat(sin_k))[:, :, k],
                    ALU.add, ALU.mult), done=("ks", s, u) if k else None)
            lay.do("gpsimd", lambda e: e.tensor_tensor(kr[:, r, :], kc[:, r, :], ks[:, r, :], ALU.add),
                   done=("kr", s, u), after=[("ks", s, u), ring("G")])

        def gram(s, u, small=()):
            r = u % 2
            for t in range(2):
                for db in range(CB):
                    lay.do("tensor", mm(g_ps[db][:, 0:H + 1], kr[:, r, t * H + db * P:t * H + (db + 1) * P],
                                        h[s][:, 2 * u + t, :], u == 0 and t == 0, u == DUOS - 1 and t == 1),
                           done=("G", s, u) if t == 1 and db == CB - 1 else None,
                           after=[("kr", s, u), At(setup, ("ones", s), 0), At(pair, ("h", s), "pair"),
                                  other("G_out", s), other("cst", s)])
                    between(small)

        def k_mean(s):
            lay.do("vector", lambda e: e.tensor_tensor(km_sum[:, :], k_sums[:, 0, :], k_sums[:, 1, :], ALU.add),
                   done=("km_sum", s), after=[("gk", s, CB * QH - 1)])
            lay.do("vector", lambda e: e.tensor_scalar(km[:, :], km_sum[:, :], 1.0 / T, 0.21, ALU.mult, ALU.add),
                   done=("km", s), after=[("km_sum", s)])
            for db in range(CB):
                lay.do("vector", lambda e, db=db: e.tensor_scalar(kmb[:, s, db, :], head_mask[:, :], km[:, db:db + 1], None,
                                                                  ALU.mult), done=("kmb", s) if db == CB - 1 else None,
                       after=[("km", s), Prev(("D", s))] + consts)
            lay.do("vector", lambda e: e.tensor_scalar(c21[:, :, :], kmb[:, s, :, :], 0.21, 1e-6 / P, ALU.mult, ALU.add),
                   done=("c21", s), after=[("kmb", s), other("cst_ps", s)])

        def denominators(s):
            bank = g_ps[0]
            ready = [("gq", s, CB * QH - 1), ("kmb", s), ("c21", s), ("G_out", s)]
            pieces = []
            for db in range(CB):
                pieces.append(lambda db=db: lay.do("tensor", mm(
                    bank[:, TILES * NH + db * HB:TILES * NH + (db + 1) * HB], ones[:, :], c21[:, db, :]),
                    done=("cst_ps", s) if db == CB - 1 else None, after=ready))
            for t in range(TILES):
                for db in range(CB):
                    pieces.append(lambda t=t, db=db: lay.do("tensor", mm(
                        bank[:, t * NH + db * HB:t * NH + (db + 1) * HB], gT[s][:, db, t * P:(t + 1) * P], kmb[:, s, db, :]),
                        done=("D", s) if t == TILES - 1 and db == CB - 1 else None, after=ready))

            def invert():
                dview = bank[:, 0:TILES * NH].rearrange("p (t n) -> p t n", t=TILES)
                add = cst[:, :].unsqueeze(1).broadcast_to([P, TILES, NH])
                lay.do("vector", lambda e: e.tensor_copy(cst[:, :], bank[:, TILES * NH:(TILES + 1) * NH]),
                       done=("cst0", s), after=[("D", s)])
                lay.do("vector", lambda e: e.tensor_tensor(den[:, :, :], dview, add, ALU.add), done=("cst", s),
                       after=[("cst0", s)])
                lay.do("vector", lambda e: e.reciprocal(z[:, s, :, :], den[:, :, :]), done=("z", s), after=[("cst", s)])
            pieces.append(invert)
            return pieces

        def gram_copy(s):
            for db in range(CB):
                lay.do("scalar", lambda e, db=db: e.activation(G[:, db, :], g_ps[db][:, 0:H + 1], ACT.Copy),
                       done=("G_out", s) if db == CB - 1 else None, after=[("G", s, DUOS - 1), other("kv_raw", s)])

        def gram_rows(s):
            for db in range(CB):
                for cb in range(CB):
                    lay.do("tensor", lambda e, db=db, cb=cb: e.transpose(
                        m_ps[:, cb * H + db * P:cb * H + (db + 1) * P], G[:, db, cb * P:(cb + 1) * P], identity[:, :]),
                        done=("GT_ps", s) if db == CB - 1 and cb == CB - 1 else None,
                        after=[("G_out", s), other("kv_rot", s)])
            lay.do("scalar", lambda e: e.activation(GT[:, :, :].rearrange("p c n -> p (c n)"), m_ps[:, :], ACT.Copy),
                   done=("GT", s), after=[("GT_ps", s), other("kv_ps", s)])

        def key_value(s):
            for db in range(CB):
                for cb in range(CB):
                    lay.do("tensor", mm(m_ps[:, db * P:(db + 1) * P], GT[:, cb, db * P:(db + 1) * P],
                                        wv[:, cb, db * P:(db + 1) * P], cb == 0, cb == CB - 1),
                           done=("kv_ps", s) if db == CB - 1 and cb == CB - 1 else None, after=[("GT", s), Prev("wv"), At(setup, "wv0", 0)])
            for db in range(CB):
                lay.do("vector", lambda e, db=db: e.scalar_tensor_tensor(
                    kv_raw[:, db, :], row(BV, db * P, P)(e), G[:, db, H:H + 1], m_ps[:, db * P:(db + 1) * P],
                    ALU.mult, ALU.add), done=("kv_raw", s) if db == CB - 1 else None, after=[("kv_ps", s)] + consts)
            mask = kv_mask[:, :].unsqueeze(1).broadcast_to([P, CB, P])
            lay.do("vector", lambda e: e.tensor_tensor(kv[:, s, :, :], kv_raw[:, :, :], mask, ALU.mult),
                   done=("kv", s), after=[("kv_raw", s), Prev(("out", s, DUOS - 1))])

        def turned_kv(s):
            lay.do("tensor", mm(m_ps[:, 0:CB * P], rot[:, :], kv[:, s, :, :].rearrange("p c n -> p (c n)")),
                   done=("rot_ps", s), after=[("kv", s)] + consts)
            lay.do("scalar", lambda e: e.activation(kv_rot[:, s, :, :].rearrange("p c n -> p (c n)"), m_ps[:, 0:CB * P],
                                                    ACT.Copy),
                   done=("kv_rot", s), after=[("rot_ps", s), Prev(("out", s, DUOS - 1))])

        def outputs(s, u, small=(), adder="gpsimd"):
            bank, free = banks.take(("att", s, u))
            for t in range(2):
                tok = slice((2 * u + t) * P, (2 * u + t + 1) * P)
                for db in range(CB):
                    o = bank[:, t * H + db * P:t * H + (db + 1) * P]
                    lay.do("tensor", mm(o, qc[s][:, db, tok], kv[:, s, db, :], True, False), after=[
                        ("qs", s, CB * QH - 1), ("kv", s), free])
                    lay.do("tensor", mm(o, qs[s][:, db, tok], kv_rot[:, s, db, :], False, True),
                           done=("out", s, u) if t == 1 and db == CB - 1 else None, after=[("kv_rot", s)])
                    between(small, 3)
            yd = y[:, 2 * u:2 * u + 2, :]
            zb = z[:, s, 2 * u:2 * u + 2, :].rearrange("p t n -> p (t n)").unsqueeze(2).broadcast_to([P, 2 * NH, HD])
            lay.do("vector", lambda e: e.tensor_tensor(
                yd.rearrange("p t (n d) -> p (t n) d", d=HD), bank[:, :].rearrange("p (n d) -> p n d", d=HD), zb, ALU.mult),
                done=("att", s, u), after=[("out", s, u), ("z", s), other("ln", s, u // 2)])
            lay.do(adder, lambda e: e.tensor_tensor(yd, yd, h[s][:, 2 * u:2 * u + 2, 0:H], ALU.add),
                   done=("y", s, u), after=[("att", s, u)])

        def moments_of(s, half):
            sl = slice(HT * half, HT * (half + 1))
            for t in range(HT * half, HT * (half + 1)):
                lay.do("vector", lambda e, t=t: e.bn_stats(stats[:, t, :], y[:, t, :]), done=("stats", s, t),
                       after=[("y", s, t // 2)])
            for t in range(HT * half, HT * (half + 1)):
                lay.do("vector", lambda e, t=t: e.bn_aggr(moments[:, t, :], stats[:, t, :]), done=("mom", s, t),
                       after=[("stats", s, t)], apart=True)
            lay.do("vector", lambda e: e.tensor_scalar(var_eps[:, sl], moments[:, sl, 1], 1e-12, None, ALU.add),
                   done=("var", s, half), after=[("mom", s, HT * (half + 1) - 1)])
            lay.do("gpsimd", lambda e: e.tensor_tensor(rstd[:, sl], var_eps[:, sl], minus_half[:, 0:HT], ALU.pow),
                   done=("rstd", s, half), after=[("var", s, half), At(setup, "half", 0)])

        def normalise(s, half):
            sl = slice(HT * half, HT * (half + 1))
            lay.do("vector", lambda e: e.scalar_tensor_tensor(
                offset[:, sl], moments[:, sl, 0], -1.0, rstd[:, sl], ALU.mult, ALU.mult), done=("offset", s, half),
                after=[("rstd", s, half)])
            for t in range(HT * half, HT * (half + 1)):
                lay.do("scalar", lambda e, t=t: e.activation(y[:, t, :], y[:, t, :], ACT.Identity,
                                                             bias=offset[:, t:t + 1], scale=rstd[:, t:t + 1]),
                       done=("unit", s, t), after=[("offset", s, half)])

        def finish_on_vector(s, half):
            tiles = range(HT * half, HT * (half + 1))
            for t in tiles:
                lay.do("vector", lambda e, t=t: e.scalar_tensor_tensor(
                    y[:, t, :], y[:, t, :], moments[:, t, 0:1], row(GAIN)(e), ALU.subtract, ALU.mult),
                    done=("centred", s, t), after=[("mom", s, t)])
            for t in tiles:
                lay.do("vector", lambda e, t=t: e.scalar_tensor_tensor(
                    h[s][:, t, 0:H], y[:, t, :], rstd[:, t:t + 1], row(SHIFT)(e), ALU.mult, ALU.add),
                    done=("ln", s, half) if t == tiles[-1] else ("ln_part", s, t),
                    after=[("rstd", s, half), ("centred", s, t), ("G", s, DUOS - 1)])

        def affine(s, half):
            for u in range(2 * half, 2 * half + 2):
                yd = y[:, 2 * u:2 * u + 2, :]
                lay.do("vector", lambda e, yd=yd: e.tensor_tensor(yd, yd, two(row(GAIN)(e)), ALU.mult),
                       done=("gained", s, u), after=[("unit", s, 2 * u + 1)])
                lay.do("gpsimd", lambda e, yd=yd, u=u: e.tensor_tensor(h[s][:, 2 * u:2 * u + 2, 0:H], yd, two(row(SHIFT)(e)),
                                                                      ALU.add),
                       done=("ln", s, half) if u % 2 else ("ln_part", s, half), after=[("gained", s, u), ("G", s, DUOS - 1)])

        def fetch_weights():
            lay.do("sync", lambda e: e.dma_start(w_raw[:, :, :], next_w(e)[:, :, 0:2 * H]), dma="w_raw", after=w_now)

        def split_weights():
            lay.do("scalar", lambda e: e.activation(w_hi[:, :, :], w_raw[:, :, :], ACT.Copy), done="w_next_hi",
                   after=["w_raw", ("q", 1, CB * QH - 1)])
            lay.do("vector", lambda e: e.tensor_tensor(w_lo[:, :, :], w_raw[:, :, :], w_hi[:, :, :].bitcast(F32),
                                                       ALU.subtract), done="w_next", after=["w_next_hi"])

        def fetch_wv():
            lay.do("sync", lambda e: e.dma_start(wv[:, :, :], next_w(e)[:, :, 2 * H:3 * H]), dma="wv",
                   after=[("kv_ps", 1)])

        next_w = lambda e: w3[bass.ds(reg[e][1] + 1, 1)].rearrange("a p c n -> (a p) c n")

        fetch_weights()
        keys(0, 0)
        queries(0, 0)
        keys(0, 1)
        k_rows(0, 0)
        k_rows(0, 1)
        rotate_k(0, 0)
        rotate_k(0, 1)
        rotate_q(0, 0)
        queries(0, 1)
        split_h(1, 0)
        gram(0, 0)
        k_rows(0, 2)
        rotate_k(0, 2)
        gram(0, 1)
        k_rows(0, 3)
        rotate_k(0, 3)
        k_mean(0)
        split_h(1, 1)
        gram(0, 2)
        gram(0, 3)
        gram_copy(0)
        rotate_q(0, 1)
        keys(1, 0)
        gram_rows(0)
        queries(1, 0)
        key_value(0)
        small = denominators(0)
        keys(1, 1, small)
        between(small, len(small))
        turned_kv(0)
        k_rows(1, 0)
        k_rows(1, 1)
        rotate_k(1, 0)
        rotate_k(1, 1)
        outputs(0, 0)
        outputs(0, 1)
        rotate_q(1, 0)
        moments_of(0, 0)
        queries(1, 1)
        split_weights()
        normalise(0, 0)
        gram(1, 0)
        k_rows(1, 2)
        rotate_k(1, 2)
        gram(1, 1)
        k_rows(1, 3)
        rotate_k(1, 3)
        affine(0, 0)
        k_mean(1)
        outputs(0, 2)
        gram(1, 2)
        gram(1, 3)
        gram_copy(1)
        rotate_q(1, 1)
        split_h(0, 0, blocks=range(1))
        gram_rows(1)
        key_value(1)
        fetch_wv()
        small = denominators(1)
        outputs(0, 3, small, adder="vector")
        between(small, len(small))
        turned_kv(1)
        split_h(0, 0, blocks=range(1, CB))
        moments_of(0, 1)
        finish_on_vector(0, 1)
        outputs(1, 0)
        outputs(1, 1)
        moments_of(1, 0)
        outputs(1, 2, adder="vector")
        outputs(1, 3, adder="vector")
        split_h(0, 1)
        normalise(1, 0)
        affine(1, 0)
        moments_of(1, 1)
        finish_on_vector(1, 1)

        for half in range(QH):
            split_h(0, half, pair)

        for s in range(LANES):
            def store(e, s=s):
                return e.dma_start(batch(e, h_out, s), h[s][:, :, 0:H])
            pair.do("sync", store, dma=("sent", s), after=[At(lay, ("ln", s, 1), "last layer")])

        with nc.Block() as block:
            def body(name):
                def emit_pair(eng, i, ops, layer=None):
                    where = {"pair": i, "last layer": i * L + (L - 1), "layer before": i * L - 1}
                    reg[eng] = (i, layer)
                    pair.emit(name, eng, i, where, ops)

                def layers(eng, i):
                    if lay.queue[name]:
                        with eng.Fori(0, L) as l:
                            reg[eng] = (i, l)
                            lay.emit(name, eng, i * L + l, {"pair": i})

                def transfers(eng):
                    fetch_next, load_1, *stores = pair.queue[name]
                    emit_pair(eng, 0, [fetch_next, load_1])

                    def pass_pair(i, last=False):
                        if not last:
                            emit_pair(eng, i + 1, [fetch_next])
                        layers(eng, i)
                        emit_pair(eng, i, stores)
                        if not last:
                            emit_pair(eng, i + 1, [load_1])
                    with eng.Fori(0, B // LANES - 1) as i:
                        pass_pair(i)
                    pass_pair(B // LANES - 1, last=True)
                    for s in range(LANES):
                        sem, per, const = pair.value(("sent", s), 0)
                        eng.wait_ge(sem, (B // LANES - 1) * per + const)

                def program(eng):
                    setup.credit(name, eng)
                    pair.credit(name, eng)
                    lay.credit(name, eng)
                    setup.emit(name, eng, 0)
                    if name == "sync":
                        transfers(eng)
                    else:
                        with eng.Fori(0, B // LANES) as i:
                            emit_pair(eng, i, pair.queue[name])
                            layers(eng, i)
                return program
            for name in ENGINES:
                getattr_block(block, name)(body(name))


def ffn_phase(nc, x, h_in, out, w1, b1, w2, rows2, comp, eye, tri):
    B, T, H = x.shape
    F = w1.shape[1] // (H // P)
    CB, FB = H // P, F // P
    LANES = 2
    TOK = T // LANES
    TILES = TOK // P
    GEL = 5
    B2, GAIN, SHIFT = range(3)

    ctx = ExitStack()
    with ctx:
        sb = lambda n, s, d=F32: ctx.enter_context(nc.sbuf_tensor(n, s, d))
        split = lambda n, s: (sb(n + "_hi", s, F32R), sb(n + "_lo", s, F32R))

        up = [split("up0", [P, CB, F]), split("up1", [P, CB, F])]
        down = [split("down0", [P, FB, H]), split("down1", [P, FB, H])]
        identity = sb("identityC", [P, P])
        compose_phase(nc, up[1], down[1], comp, identity, eye, tri)

        pb = lambda n, s: ctx.enter_context(nc.psum_tensor(n, s, F32))
        b1s = sb("b1s", [P, FB])
        vec = sb("vecC", [P, 3 * H])
        minus_half = sb("minus_halfC", [P, TILES])
        hs = [sb(f"hC{s}", [P, TILES, H]) for s in range(LANES)]
        x_both = sb("xC", [P, LANES, TILES, H])
        xs = [x_both[:, s, :, :] for s in range(LANES)]
        y = [sb(f"yC{s}", [P, TILES, H]) for s in range(LANES)]
        x1 = [sb(f"x1{s}", [P, TILES, H]) for s in range(LANES)]
        aT = [split(f"aT{s}", [P, CB, TOK]) for s in range(LANES)]
        act = [split(f"act{s}", [P, FB, TOK]) for s in range(LANES)]
        gel = sb("gel", [P, GEL, TOK])
        zero = sb("zeroC", [P, 512], F32R)
        stats = sb("statsC", [P, LANES, TILES, 6])
        moments = sb("momentsC", [P, LANES, TILES, 2])
        var_eps = sb("var_epsC", [P, LANES, TILES])
        rstd = sb("rstdC", [P, LANES, TILES])
        turn = [pb(f"turn{i}", [P, TOK]) for i in range(CB)]
        banks = Banks([pb(f"bankC{i}", [P, 512]) for i in range(6)])

        setup = Stage(nc, ctx, "ffnset")
        ahead = Stage(nc, ctx, "ffnahead")
        work = Stage(nc, ctx, "ffn")
        reg = {}

        setup.do("scalar", lambda e: e.dma_start(b1s[:, :], b1), dma="consts")
        setup.do("scalar", lambda e: e.dma_start(vec[:, :], rows2.partition_broadcast(P)), dma="consts")
        setup.do("gpsimd", lambda e: e.memset(minus_half[:, :], -0.5), done="half")
        setup.do("gpsimd", lambda e: e.memset(zero[:, :].bitcast(F32), 0.0), done="zero")
        flat = lambda t: t[:, :, :].rearrange("p a b -> p (a b)")
        for n, (src, (hi, lo)) in enumerate(((w1, up[0]), (w2, down[0]))):
            w_in = (gel[:, :, :].rearrange("p a b -> p (a b)"), x_both[:, :, :, :].rearrange("p s a b -> p (s a b)"))[n]
            w_in = w_in[:, 0:src.shape[1]]
            setup.do("sync", lambda e, src=src, w=w_in: e.dma_start(w, src), dma=("w", n))
            setup.do("scalar", lambda e, d=flat(hi), w=w_in: e.activation(d, w, ACT.Copy), done=("w_hi", n), after=[("w", n)])
            setup.do("vector", lambda e, d=flat(lo), g=flat(hi), w=w_in: e.tensor_tensor(d, w, g.bitcast(F32), ALU.subtract),
                     done=("w_lo", n), after=[("w_hi", n)])
        weights = [At(setup, ("w_lo", 1), 0)]
        consts = [At(setup, "consts", 0), At(setup, "half", 0)]
        vrow = lambda k: vec[:, k * H:(k + 1) * H]

        h_rows = h_in.rearrange("b p (m f) -> b m p f", m=LANES)
        x_rows = x.rearrange("b (m p s) c -> b m p (s c)", m=LANES, p=P)
        o_rows = out.rearrange("b (m p s) c -> b m p (s c)", m=LANES, p=P)
        pick = lambda e, a, s: a[bass.ds(reg[e], 1), s].rearrange("a p f -> (a p) f")
        now = lambda name: At(ahead, name, "this batch")
        before = lambda name: At(work, name, "batch before")
        for s in range(LANES):
            ahead.do("sync", lambda e, s=s: e.dma_start(flat(hs[s]), pick(e, h_rows, s)), dma=("h", s),
                     after=[before(("y", 0, s, TILES // 2 - 1))])
        for s in range(LANES):
            ahead.do("sync", lambda e, s=s: e.dma_start(flat(xs[s]), pick(e, x_rows, s)), dma=("x", s),
                     after=[before(("sum", s))] + weights)

        turn_order = [(0, 0), (0, 1), (1, 0), (1, 1)]

        def transposes(k, s):
            src = (hs, x1)[k][s]
            stage = ahead if (k, s) == (0, 0) else work
            ready = [("h", 0)] if stage is ahead else [now(("h", s))] if k == 0 else [("ln1", s)]
            if stage is ahead:
                used = [before(("up", 1, 0, FB - 1))]
            else:
                used = [("up", 0, s, FB - 1)] if k else [Prev(("up", 1, s, FB - 1))]
            hi, lo = aT[s]
            for cb in range(CB):
                if stage is ahead:
                    free = before(("aT_lo", 1, 1, cb))
                elif (k, s) == (0, 1):
                    free = now(("aT_lo", 0, 0, cb))
                else:
                    free = ("aT_lo", *turn_order[turn_order.index((k, s)) - 1], cb)
                for t in range(TILES):
                    stage.do("tensor", lambda e, t=t, cb=cb: e.transpose(
                        turn[cb][:, t * P:(t + 1) * P], src[:, t, cb * P:(cb + 1) * P], identity[:, :]),
                        done=("aT_ps", k, s, cb) if t == TILES - 1 else None, after=ready + [free])
                stage.do("scalar", lambda e, cb=cb: e.activation(hi[:, cb, :], turn[cb][:, :], ACT.Copy),
                         done=("aT_hi", k, s, cb), after=[("aT_ps", k, s, cb)] + used)
                stage.do("vector", lambda e, cb=cb: e.tensor_tensor(
                    lo[:, cb, :], turn[cb][:, :], hi[:, cb, :].bitcast(F32), ALU.subtract),
                    done=("aT_lo", k, s, cb), after=[("aT_hi", k, s, cb)])

        def add_bias(s):
            b2 = vrow(B2).unsqueeze(1).broadcast_to([P, TILES, H])
            turned = now(("aT_ps", 0, 0, CB - 1)) if s == 0 else ("aT_ps", 0, s, CB - 1)
            work.do("gpsimd", lambda e: e.tensor_tensor(hs[s][:, :, :], hs[s][:, :, :], b2, ALU.add),
                    done=("res", 0, s), after=[turned] + consts)

        gel_ring = Banks([gel[:, g, :] for g in range(GEL)])

        def up_product(k, s):
            hi, lo = aT[s]
            a_hi, a_lo = act[s]
            turned = now(("aT_lo", k, s, CB - 1)) if (k, s) == (0, 0) else ("aT_lo", k, s, CB - 1)

            def piece(fb):
                g, g_free = gel_ring.take(("act_lo", k, s, fb))
                bank, free = banks.take(("gelu", k, s, fb))
                f = slice(fb * P, (fb + 1) * P)
                parts = [(bank[:, :], (up[k][0][:, cb, f], up[k][1][:, cb, f]), (hi[:, cb, :], lo[:, cb, :]),
                          cb == 0, cb == CB - 1) for cb in range(CB)]
                work.do("tensor", mm3(parts), done=("up", k, s, fb), after=[turned, free] + weights)
                work.do("scalar", lambda e: e.activation(
                    g, bank[:, :], ACT.Gelu if k == 0 else ACT.Gelu_apprx_tanh,
                    bias=b1s[:, fb:fb + 1] if k == 0 else 0.0), done=("gelu", k, s, fb),
                    after=[("up", k, s, fb), g_free] + consts)
                used = [("down", 0, s, TILES // 2 - 1)] if k else [Prev(("down", 1, s, TILES // 2 - 1))]
                work.do("vector", lambda e: e.tensor_copy(a_hi[:, fb, :], g),
                        done=("act_hi", k, s, fb), after=[("gelu", k, s, fb)] + used + weights)
                work.do("vector", lambda e: e.tensor_tensor(
                    a_lo[:, fb, :], g, a_hi[:, fb, :].bitcast(F32), ALU.subtract),
                    done=("act_lo", k, s, fb), after=[("act_hi", k, s, fb)])
            return [lambda fb=fb: piece(fb) for fb in range(FB)]

        def down_product(k, s):
            a_hi, a_lo = act[s]
            add = (hs, x1)[k][s]
            pair = [banks.take(("y", k, s, u)) for u in range(TILES // 2)]
            for bank, free in pair:
                work.do("tensor", lambda e, bank=bank: e.matmul(bank[:, :], zero[:, 0:P], zero[:, :], start=True, stop=False),
                        after=[free, At(setup, "zero", 0)])
            for fb in range(FB):
                for u, (bank, free) in enumerate(pair):
                    last = fb == FB - 1
                    parts = [(bank[:, t * H:(t + 1) * H],
                              tuple(a[:, fb, (2 * u + t) * P:(2 * u + t + 1) * P] for a in (a_hi, a_lo)),
                              (down[k][0][:, fb, :], down[k][1][:, fb, :]), False, last and t == 1) for t in range(2)]
                    work.do("tensor", mm3(parts), done=("down", k, s, u) if last else None,
                            after=[("act_lo", k, s, fb)])
            for u, (bank, free) in enumerate(pair):
                two = lambda t, u=u: t[:, 2 * u:2 * u + 2, :].rearrange("p t c -> p (t c)")
                ready = [("res", 0, s)] if k == 0 else [("ln1", s)]
                used = [("ln1", s)] if k else [Prev(("out_sent", s)), Prev(("ln3", s))]
                work.do("vector", lambda e, bank=bank, two=two: e.tensor_tensor(
                    two(y[s]), bank[:, :], two(add), ALU.add), done=("y", k, s, u),
                    after=[("down", k, s, u)] + ready + used)

        def norms(k, s):
            tiles = lambda t: [t[s][:, i, :] for i in range(TILES)]
            st = (stats[:, s], moments[:, s], var_eps[:, s], rstd[:, s], minus_half)

            def plus_x():
                work.do("gpsimd", lambda e: e.tensor_tensor(y[s][:, :, :], y[s][:, :, :], xs[s][:, :, :], ALU.add),
                        done=("sum", s), after=[("ln0", s), now(("x", s))])

            if k == 0:
                return [*layernorm_pieces(work, ("first", s), tiles(y), tiles(y), *st, 1e-12, vrow(GAIN), vrow(SHIFT),
                                          ready=[("y", 0, s, TILES // 2 - 1)], free=[], done=("ln0", s), first=consts),
                        plus_x,
                        *layernorm_pieces(work, ("second", s), tiles(y), tiles(x1), *st, 1e-5, None, None,
                                          ready=[("sum", s)], free=[Prev(("y", 1, s, TILES // 2 - 1))], done=("ln1", s))]
            return layernorm_pieces(work, ("third", s), tiles(y), tiles(y), *st, 1e-5, None, None,
                                    ready=[("y", 1, s, TILES // 2 - 1)], free=[], done=("ln3", s))

        def together(products, layers, at):
            at = dict(zip(at, layers))
            for i, piece in enumerate(products):
                if i in at:
                    at[i]()
                piece()

        for piece in up_product(0, 0):
            piece()
        add_bias(0)
        transposes(0, 1)
        down_product(0, 0)
        add_bias(1)
        together(up_product(0, 1), norms(0, 0), (0, 1, 2, 3, 5, 6))
        down_product(0, 1)
        transposes(1, 0)
        together(up_product(1, 0), norms(0, 1), (0, 1, 2, 3, 5, 6))
        down_product(1, 0)
        transposes(1, 1)
        transposes(0, 0)
        mark = {e: len(work.queue[e]) for e in ENGINES}
        together(up_product(1, 1), norms(1, 0), (0, 1))
        down_product(1, 1)
        for piece in norms(1, 1):
            piece()
        for s in range(LANES):
            work.do("sync", lambda e, s=s: e.dma_start(pick(e, o_rows, s), flat(y[s])), dma=("out_sent", s),
                    after=[("ln3", s)])

        with nc.Block() as block:
            def body(name):
                def batch(eng, i, last=False):
                    reg[eng] = i
                    work.emit(name, eng, i, {"this batch": i}, work.queue[name][:mark[name]])
                    if not last:
                        reg[eng] = i + 1
                        ahead.emit(name, eng, i + 1, {"batch before": i})
                        reg[eng] = i
                    work.emit(name, eng, i, {"this batch": i}, work.queue[name][mark[name]:])

                def program(eng):
                    setup.credit(name, eng)
                    ahead.credit(name, eng)
                    work.credit(name, eng)
                    setup.emit(name, eng, 0)
                    reg[eng] = 0
                    ahead.emit(name, eng, 0, {"batch before": -1})
                    with eng.Fori(0, B - 1) as i:
                        batch(eng, i)
                    batch(eng, B - 1, last=True)
                    if name == "sync":
                        for s in range(LANES):
                            sem, per, const = work.value(("out_sent", s), 0)
                            eng.wait_ge(sem, (B - 1) * per + const)
                return program
            for name in ENGINES:
                getattr_block(block, name)(body(name))


def compose_phase(nc, up, down, comp, identity, eye, tri):
    logits, bases, R = comp["logits"], (("A1", "B1"), ("A2", "B2")), 64
    N = 64
    K = 32
    ctx = ExitStack()
    with ctx:
        sb = lambda n, s, d=F32: ctx.enter_context(nc.sbuf_tensor(n, s, d))
        pb = lambda n, s: ctx.enter_context(nc.psum_tensor(n, s, F32))
        row = sb("logit_row", [N, 2, N])
        col = sb("logit_col", [N, 2])
        before = sb("before", [N, N])
        index = sb("index", [N, 1 + K])
        more = sb("more", [N, 2, N])
        same = sb("same", [N, 2, N])
        rank2 = sb("rank2", [N, 2, 2])
        rank = sb("rank", [N, 2])
        top = sb("top", [N, 2])
        expo = sb("expo", [N, 2])
        chosen = sb("chosen", [N, 2])
        onesN = sb("onesN", [N, P])
        weight = sb("weight", [N, 2, P])
        place = sb("place", [N, 2, K])
        inv_sum = sb("inv_sum", [P, 2])
        total = sb("total", [P, 2])
        w_row = sb("w_row", [P, 2, K])
        w_col = sb("w_col", [P, 2, K // 2])
        picks_f = sb("picks_f", [1, 2 * K])
        picks = sb("picks", [1, 2 * K], I32)
        zero = sb("zero", [P, 512], F32R)
        A = sb("Abuf", [P, 2, 8, 2, R])
        Bm = sb("Bbuf", [P, 2, 1024])
        AT = (sb("AT_hi", [P, 2, 1024], F32R), sb("AT_lo", [P, 2, 1024], F32R))
        Bs = (sb("Bs_hi", [P, 2, 1024], F32R), sb("Bs_lo", [P, 2, 1024], F32R))
        acc = [pb(f"acc{i}", [P, 512]) for i in range(4)]
        t_ps = [pb(f"t_ps{i}", [P, 512]) for i in range(4)]

        pre = Stage(nc, ctx, "rank")
        pre.do("sync", lambda e: e.dma_start(row[:, :, :].rearrange("n a b -> n (a b)"), logits.partition_broadcast(N)), dma="in")
        pre.do("sync", lambda e: e.dma_start(col[:, :], comp["logit_col"]), dma="in")
        pre.do("sync", lambda e: e.dma_start(before[:, :], tri), dma="in")
        pre.do("sync", lambda e: e.dma_start(index[:, :], comp["index"]), dma="in")
        pre.do("sync", lambda e: e.dma_start(identity[:, :], eye), dma="in")
        pre.do("gpsimd", lambda e: e.memset(onesN[:, :], 1.0), done="ones")
        pre.do("gpsimd", lambda e: e.memset(zero[:, :].bitcast(F32), 0.0), done="zero")
        V = lambda make, done=None, after=(): pre.do("vector", make, done=done, after=after)
        for f in range(2):
            V(lambda e, f=f: e.tensor_scalar(more[:, f, :], row[:, f, :], col[:, f:f + 1], None, ALU.is_gt), ("more", f), ["in"])
            V(lambda e, f=f: e.scalar_tensor_tensor(same[:, f, :], row[:, f, :], col[:, f:f + 1], before[:, :],
                                                    ALU.is_equal, ALU.mult), ("same", f), [])
        X = mybir.AxisListType.X
        V(lambda e: e.tensor_tensor(more[:, :, :], more[:, :, :], same[:, :, :], ALU.add), "both", [("same", 1)])
        V(lambda e: e.tensor_reduce(rank[:, :], more[:, :, :], X, ALU.add), "rank", ["both"])
        V(lambda e: e.tensor_reduce(top[:, :], row[:, :, :], X, ALU.max), "top", [])
        V(lambda e: e.tensor_scalar(chosen[:, :], rank[:, :], float(K), None, ALU.is_lt), "chosen", ["rank"])
        V(lambda e: e.tensor_tensor(expo[:, :], col[:, :], top[:, :], ALU.subtract), "less_top", ["top"])
        pre.do("scalar", lambda e: e.activation(expo[:, :], expo[:, :], ACT.Exp), done="exp", after=["less_top"])
        V(lambda e: e.tensor_tensor(expo[:, :], expo[:, :], chosen[:, :], ALU.mult), "kept", ["exp", "chosen"])
        for f in range(2):
            V(lambda e, f=f: e.tensor_scalar(weight[:, f, :], onesN[:, :], expo[:, f:f + 1], None, ALU.mult), ("weight", f), ["kept", "ones"])
            V(lambda e, f=f: e.tensor_scalar(place[:, f, :], index[:, 1:1 + K], rank[:, f:f + 1], None, ALU.is_equal), ("place", f), ["in"])
        for f in range(2):
            pre.do("tensor", mm(t_ps[0][:, f * K:(f + 1) * K], weight[:, f, :], place[:, f, :]), done=("w_row", f),
                   after=[("place", 1)])
            pre.do("tensor", mm(t_ps[1][0:1, f * K:(f + 1) * K], index[:, 0:1], place[:, f, :]), done=("pick", f),
                   after=[])
        V(lambda e: e.tensor_copy(w_row[:, :, :].rearrange("p a b -> p (a b)"), t_ps[0][:, 0:2 * K]), "w_row", [("pick", 1)])
        V(lambda e: e.tensor_copy(picks[:, :], t_ps[1][0:1, 0:2 * K]), "picks", [])
        V(lambda e: e.tensor_reduce(total[:, :], w_row[:, :, :], X, ALU.add), "total", ["w_row"])
        V(lambda e: e.reciprocal(inv_sum[:, :], total[:, :]), "inv", ["total"])
        for f in range(2):
            for half in range(2):
                rows = slice(R * half, R * half + R)
                V(lambda e, f=f, half=half, rows=rows: e.tensor_scalar(
                    w_col[rows, f, :], w_row[rows, f, :].rearrange("p (a two) -> p a two", two=2)[:, :, half],
                    inv_sum[rows, f:f + 1], None, ALU.mult), ("w_col", f, half), ["inv"])

        reg, number = {}, {}
        stages = []
        for f in range(2):
            A_d, B_d = comp[bases[f][0]], comp[bases[f][1]]
            d_in, d_out = A_d.shape[1], B_d.shape[2]
            MB = d_in // P
            NW = min(512, d_out)
            WA = min(512, d_in)
            A_BANKS = d_in // WA
            small_a = d_in < d_out
            slots = (Stage(nc, ctx, f"comp_ahead{f}"), Stage(nc, ctx, f"comp{f}"))
            a_rows = A_d.rearrange("k (o p) r -> k p o r", p=P)

            def chosen_number(e, f, q, half):
                if (e, q, half) not in number:
                    number[e, q, half] = e.value_load(picks[0:1, bass.ds(reg[e] * 4 + (f * K + 2 * q + half), 1)],
                                                      min_val=0, max_val=N - 1)
                return number[e, q, half]

            def load_pair(f, q, stage, a_rows, B_d, MB, d_out):
                for half in range(2):
                    def load_a(e, half=half):
                        k = chosen_number(e, f, q, half)
                        return e.dma_start(A[:, q, 0:MB, half, :], a_rows[bass.ds(k, 1)].rearrange("a p o r -> (a p) o r"))

                    def load_b(e, half=half):
                        k = chosen_number(e, f, q, half)
                        return e.dma_start(Bm[R * half:R * half + R, q, 0:d_out],
                                           B_d[bass.ds(k, 1)].rearrange("a r n -> (a r) n"))
                    for load in (load_a, load_b):
                        stage.do("sync", load, dma=("AB", q), after=[Prev(("AT_ps", q)), Prev(("B_lo", q))])

            def split_with(stage, weight, hi, lo, src, done_hi, done_lo, ready, free):
                if weight:
                    stage.do("scalar", lambda e: e.activation(hi, src, ACT.Copy, scale=weight(e)), done=done_hi,
                             after=[ready, free], apart=True)
                    stage.do("vector", lambda e: e.scalar_tensor_tensor(lo, src, weight(e), hi.bitcast(F32),
                                                                        ALU.mult, ALU.subtract), done=done_lo, after=[done_hi])
                else:
                    stage.do("scalar", lambda e: e.activation(hi, src, ACT.Copy), done=done_hi, after=[ready, free])
                    stage.do("vector", lambda e: e.tensor_tensor(lo, src, hi.bitcast(F32), ALU.subtract), done=done_lo,
                             after=[done_hi])

            def prepare(f, q, stage, MB, WA, A_BANKS, d_out, small_a, work):
                weight = lambda e: w_col[:, f, bass.ds(reg[e] * 2 + q, 1)]
                multiplied = Prev(("mm", 1)) if q else At(work, ("mm", 0), "before")
                for m in range(MB):
                    at = m * P
                    stage.do("tensor", lambda e, m=m, at=at: e.transpose(
                        t_ps[2 * q + at // 512][:, at % 512:at % 512 + P], A[:, q, m, :, :].rearrange("p h r -> p (h r)"),
                        identity[:, :]), done=("AT_ps", q) if m == MB - 1 else None,
                        after=[("AB", q), Prev(("AT_lo", q, A_BANKS - 1))])
                for i in range(A_BANKS):
                    hi, lo = (t[:, q, i * WA:(i + 1) * WA] for t in AT)
                    split_with(stage, weight if small_a else None, hi, lo, t_ps[2 * q + i][:, 0:WA],
                               ("AT_hi", q, i), ("AT_lo", q, i), ("AT_ps", q), multiplied)
                hi, lo = (t[:, q, 0:d_out] for t in Bs)
                split_with(stage, None if small_a else weight, hi, lo, Bm[:, q, 0:d_out],
                           ("B_hi", q), ("B_lo", q), ("AB", q), multiplied)

            def multiply(q, MB, NW, A_BANKS, d_out, slots):
                parts = []
                for m in range(MB):
                    for n in range(d_out // NW):
                        at = m * d_out + n * NW
                        parts.append((acc[at // 512][:, at % 512:at % 512 + NW],
                                      tuple(t[:, q, m * P:(m + 1) * P] for t in AT),
                                      tuple(t[:, q, n * NW:(n + 1) * NW] for t in Bs), False, False))
                event = lambda name: name if q else At(slots[0], name, "this")
                slots[1].do("tensor", mm3(parts), done=("mm", q),
                            after=[event(("AT_lo", q, A_BANKS - 1)), event(("B_lo", q))])

            for q in range(2):
                load_pair(f, q, slots[q], a_rows, B_d, MB, d_out)
            prepare(f, 0, slots[0], MB, WA, A_BANKS, d_out, small_a, slots[1])
            prepare(f, 1, slots[1], MB, WA, A_BANKS, d_out, small_a, slots[1])
            multiply(0, MB, NW, A_BANKS, d_out, slots)
            mark = {e: len(slots[1].queue[e]) for e in ENGINES}
            multiply(1, MB, NW, A_BANKS, d_out, slots)
            stages.append((slots, mark, A_BANKS))

        post = [Stage(nc, ctx, f"compout{f}") for f in range(2)]
        for f, (hi, lo) in enumerate((up, down)):
            for i in range(4):
                cols = slice(i * 512, (i + 1) * 512)
                fl = lambda t: t[:, :, :].rearrange("p a b -> p (a b)")[:, cols]
                last = At(stages[f][0][1], ("mm", 1), K // 4 - 1)
                post[f].do("tensor", lambda e, i=i: e.matmul(acc[i][:, :], zero[:, 0:P], zero[:, :], start=False, stop=True),
                           done=("closed", i), after=[last])
                post[f].do("scalar", lambda e, i=i, d=fl(hi): e.activation(d, acc[i][:, :], ACT.Copy), done=("hi", i),
                           after=[("closed", i)])
                post[f].do("vector", lambda e, i=i, d=fl(lo), g=fl(hi): e.tensor_tensor(d, acc[i][:, :], g.bitcast(F32), ALU.subtract),
                           done=("lo", i), after=[("hi", i)])

        def wait_for(eng, stage, name, iteration=0):
            sem, per, const = stage.value(name, iteration)
            eng.wait_ge(sem, iteration * per + const)

        with nc.Block() as block:
            def body(name):
                def group(eng, f, i, last=False):
                    (ahead, work), mark, _ = stages[f]
                    emit = lambda ops: (number.clear(), work.emit(name, eng, i, {"this": i}, ops))
                    reg[eng] = i
                    emit(work.queue[name][:mark[name]])
                    if not last:
                        reg[eng] = i + 1
                        number.clear()
                        ahead.emit(name, eng, i + 1, {"before": i})
                        reg[eng] = i
                    emit(work.queue[name][mark[name]:])

                def program(eng):
                    pre.credit(name, eng)
                    pre.emit(name, eng, 0)
                    for f in range(2):
                        (ahead, work), mark, _ = stages[f]
                        ahead.credit(name, eng)
                        work.credit(name, eng)
                        post[f].credit(name, eng)
                        if name == "tensor":
                            if f == 0:
                                wait_for(eng, pre, "zero")
                                wait_for(eng, pre, "picks")
                            else:
                                wait_for(eng, post[0], ("lo", 3))
                            for i in range(4):
                                eng.matmul(acc[i][:, :], zero[:, 0:P], zero[:, :], start=True, stop=False)
                        if name in ("scalar", "vector"):
                            wait_for(eng, pre, ("w_col", 1, 1))
                        if name == "scalar" and f == 1:
                            wait_for(eng, stages[0][0][1], ("mm", 1), K // 4 - 1)
                        if name == "sync":
                            wait_for(eng, pre, "picks")
                            if f == 1:
                                (ahead0, work0), _, banks0 = stages[0]
                                for q, stage in enumerate((ahead0, work0)):
                                    wait_for(eng, stage, ("AT_ps", q), K // 4 - 1)
                                    wait_for(eng, stage, ("B_lo", q), K // 4 - 1)
                        reg[eng] = 0
                        number.clear()
                        ahead.emit(name, eng, 0, {"before": -1})
                        with eng.Fori(0, K // 4 - 1) as i:
                            group(eng, f, i)
                        group(eng, f, K // 4 - 1, last=True)
                        post[f].emit(name, eng, 0)
                return program
            for name in ENGINES:
                getattr_block(block, name)(body(name))


def layernorm_pieces(stage, key, ins, outs, stats, moments, var_eps, rstd, minus_half, eps, gain, shift,
                     ready, free, done, first=(), step=None):
    n = len(ins)
    step = step or n

    def measure(a, b):
        for t in range(a, b):
            stage.do("vector", lambda e, t=t: e.bn_stats(stats[:, t, :], ins[t]), done=("stats", key, t),
                     after=list(ready) + list(first) if t == 0 else [])
        for t in range(a, b):
            stage.do("vector", lambda e, t=t: e.bn_aggr(moments[:, t, :], stats[:, t, :]), done=("moments", key, t),
                     after=[("stats", key, t)], apart=True)
        if b == n:
            stage.do("vector", lambda e: e.tensor_scalar(var_eps, moments[:, :, 1], eps, None, ALU.add),
                     done=("var", key), after=[("moments", key, n - 1)])
            if step == n:
                invert()

    def invert():
        stage.do("gpsimd", lambda e: e.tensor_tensor(rstd, var_eps, minus_half[:, 0:n], ALU.pow),
                 done=("rstd", key), after=[("var", key)])

    def centre(a, b):
        for t in range(a, b):
            stage.do("vector", lambda e, t=t: e.scalar_tensor_tensor(
                ins[t], ins[t], moments[:, t, 0:1], gain, ALU.subtract, ALU.mult), done=("centred", key, t))
        if b == n and step < n:
            invert()

    def apply(a, b):
        for t in range(a, b):
            event = done if t == n - 1 else (done, t)
            ready = [("rstd", key)] + (list(free) if t == 0 else [])
            if gain is not None:
                stage.do("vector", lambda e, t=t: e.scalar_tensor_tensor(
                    outs[t], ins[t], rstd[:, t:t + 1], shift, ALU.mult, ALU.add), done=event,
                    after=[("centred", key, t)] + ready)
            else:
                stage.do("vector", lambda e, t=t: e.tensor_scalar(
                    outs[t], ins[t], moments[:, t, 0:1], rstd[:, t:t + 1], ALU.subtract, ALU.mult), done=event,
                    after=ready)
    steps = (measure, centre, apply) if gain is not None else (measure, apply)
    return [lambda f=f, a=a: f(a, min(a + step, n)) for f in steps for a in range(0, n, step)]


def fixed(operand, e):
    return operand(e) if callable(operand) else operand


def getattr_block(block, name):
    return {"tensor": block.tensor, "vector": block.vector, "scalar": block.scalar,
            "gpsimd": block.gpsimd, "sync": block.sync}[name]


def build(nc, t):
    conv_phase(nc, t["x"], t["bands1"], t["bands2"], t["bias1"], t["bias2"], t["ln0"], t["eye"], t["h0"])
    attention_phase(nc, t["h0"], t["h4"], t["x"].shape[1], t["x"].shape[2], t["wqkv"], t["rows"], t["bq"], t["bk"],
                    {n: t[n] for n in ("cos_k", "sin_k", "cos_q", "sin_q")}, t)
    comp = {n: t[n] for n in ("logits", "logit_col", "index", "A1", "B1", "A2", "B2")}
    ffn_phase(nc, t["x"], t["h4"], t["out"], t["w1"], t["b1"], t["w2"], t["rows2"], comp, t["eye"], t["tri"])


def layout(inputs):
    import numpy as np
    f = lambda n: np.ascontiguousarray(inputs["L0_attn_" + n])
    x = f("x")
    H = x.shape[2]
    c1, c2 = f("conv1_w"), f("conv2_w")
    d = {"x": x}
    w1 = c1.reshape(H // 16, 2, 8, 4, 5)
    b1 = np.zeros((8, 2, 8, H // 16, 2, 4, 8, 4), c1.dtype)
    for k in range(2):
        for c in range(8):
            for s in range(4):
                for tap in range(5):
                    b1[s + tap, k, c, :, k, s, c, :] = w1[:, k, c, :, tap]
    d["bands1"] = b1.reshape(128, -1)
    w2 = c2.reshape(H // 8, 8, 4, 5)
    b2 = np.zeros((4, 8, 4, H // 8, 3, 4, 8), c2.dtype)
    for s in range(4):
        for c in range(8):
            for g in range(3):
                for so in range(4):
                    tap = 4 * (g - 1) + s - so + 2
                    if 0 <= tap < 5:
                        b2[s, c, :, :, g, so, c] = w2[:, c, :, tap].T
    d["bands2"] = b2.reshape(128, -1)
    bias1 = f("conv1_b").reshape(H // 8, 32).T
    d["bias1"] = np.ascontiguousarray(np.tile(bias1, (4, 1)))
    bias2 = f("conv2_b").reshape(H // 32, 4, 1, 8)
    d["bias2"] = np.ascontiguousarray(np.broadcast_to(bias2, (H // 32, 4, 4, 8)).reshape(H // 32, 128).T)
    d["ln0"] = np.stack([f("ln0_g"), f("ln0_b")])
    w = np.concatenate([f("Wq"), f("Wk"), f("Wv")], axis=2)
    L, T = w.shape[0], x.shape[1]
    w = w.reshape(L, 2, 128, 3 * H).transpose(0, 2, 1, 3).reshape(L, 128, 6 * H)
    d["wqkv"] = np.ascontiguousarray(np.concatenate([w, w[:1]]))
    d["rows"] = np.stack([f("bv"), f("lnA_g"), f("lnA_b")], axis=1).reshape(1, -1)
    d["bq"] = np.ascontiguousarray(f("bq").reshape(L * 2, 128).T)
    d["bk"] = np.ascontiguousarray(f("bk").reshape(L * 2, 128).T)
    inv = (np.float32(1) / np.float32(10000) ** (np.arange(0, H, 2, dtype=np.float32) / np.float32(H))).astype(np.float32)
    angle = np.repeat(np.arange(T, dtype=np.float32)[:, None] * inv[None, :], 2, axis=1).astype(np.float64)
    cos, sin = np.cos(angle).astype(np.float32), np.sin(angle).astype(np.float32)
    sign = np.tile(np.array([-1, 1], np.float32), H // 2)
    order = lambda a: a.reshape(T // 512, 128, 4, H).transpose(0, 2, 1, 3)
    rows = lambda a: np.ascontiguousarray(order(a).reshape(T // 128, 128, H).transpose(1, 0, 2).reshape(128, -1))
    cols = lambda a: np.ascontiguousarray(order(a).reshape(T, H).T.reshape(2, 128, T).transpose(1, 0, 2).reshape(128, -1))
    d["cos_k"], d["sin_k"] = rows(cos), rows(sin * sign)
    d["cos_q"], d["sin_q"] = cols(cos), cols(sin)
    i = np.arange(0, 128, 2)
    rot = np.zeros((128, 128), np.float32)
    rot[i + 1, i], rot[i, i + 1] = 1, -1
    d["rot"] = rot
    head = np.arange(128) // 16
    d["kv_mask"] = ((head[:, None] == head[None, :]) / T).astype(np.float32)
    d["head_mask"] = (head[:, None] == np.arange(8)[None, :]).astype(np.float32)
    d["w1"] = np.ascontiguousarray(f("W1").reshape(2, 128, 4 * H).transpose(1, 0, 2).reshape(128, 8 * H))
    d["w2"] = np.ascontiguousarray(f("W2").reshape(8, 128, H).transpose(1, 0, 2).reshape(128, 8 * H))
    d["b1"] = np.ascontiguousarray(f("b1").reshape(8, 128).T)
    d["rows2"] = np.concatenate([f("b2"), f("ln2_g"), f("ln2_b")])[None, :]
    g = lambda n: np.ascontiguousarray(inputs["L0_ffn_" + n])
    d["A1"], d["B1"], d["A2"], d["B2"] = g("fc1_A"), g("fc1_B"), g("fc2_A"), g("fc2_B")
    logits = np.stack([g("fc1_logits"), g("fc2_logits")])
    d["logits"], d["logit_col"] = logits.reshape(1, -1), np.ascontiguousarray(logits.T)
    n = np.arange(64, dtype=np.float32)
    d["index"] = np.concatenate([n[:, None], np.tile(n[None, :32], (64, 1))], axis=1)
    d["tri"] = (n[None, :] < n[:, None]).astype(np.float32)
    d["eye"] = np.eye(128, dtype=np.float32)
    return d


def kernel(**inputs):
    import numpy as _np
    import concourse.bacc as _bacc
    from concourse import mybir as _mybir
    from concourse.bass_utils import run_bass_kernel_spmd as _run

    nc = _bacc.Bacc("TRN2", target_bir_lowering=False, num_devices=1)
    arrays, t = {}, {}
    for name, a in layout(inputs).items():
        arrays[f"in_{name}"] = a
        t[name] = nc.dram_tensor(f"in_{name}", a.shape, _mybir.dt.from_np(a.dtype), kind="ExternalInput").ap()
    shape = inputs["L0_attn_x"].shape
    t["out"] = nc.dram_tensor("out_0", shape, _mybir.dt.float32, kind="ExternalOutput").ap()
    rows = (shape[0], 128, shape[1] * shape[2] // 128)
    t["h0"] = nc.dram_tensor("h0", rows, _mybir.dt.float32, kind="Internal").ap()
    t["h4"] = nc.dram_tensor("h4", rows, _mybir.dt.float32, kind="Internal").ap()
    build(nc, t)
    r = _run(nc, [arrays], core_ids=[0])
    return r.results[0]["out_0"]
```
